# Optimizing a Trainium2 kernel written in Bass

```python
import numpy as np
import jax
import jax.numpy as jnp

def _softmax(x, axis=-1):
    return jax.nn.softmax(x, axis=axis)

def _gelu(x):
    return jax.nn.gelu(x, approximate=True)

def _silu(x):
    return jax.nn.silu(x)

def _sigmoid(x):
    return jax.nn.sigmoid(x)

def _layernorm(x, axis=-1, eps=1e-05):
    m = jnp.mean(x, axis=axis, keepdims=True)
    v = jnp.var(x, axis=axis, keepdims=True)
    return (x - m) / jnp.sqrt(v + eps)

def _scatter_add(tgt, idx, src, axis=0):
    return tgt.at[idx].add(src)

def _segment_sum(src, seg, n):
    return jax.ops.segment_sum(src, seg, n)
kernel_name = 'mk_gnn_resnorm_d4_gnn_r16_a0db41'

def setup_inputs(seed: int=0):
    np.random.seed(seed)
    _w = jnp.asarray

    def _rec_inputs():
        import jax
        import jax.numpy as jnp
        _gk = jax.random.key(seed)
        x = -0.0003713 + 1 * jax.random.normal(jax.random.fold_in(_gk, 1), (3125, 256), jnp.float32)
        _s = jax.random.randint(jax.random.fold_in(_gk, 2), (25000,), 0, 3125, jnp.int32)
        _d = jax.random.randint(jax.random.fold_in(_gk, 3), (25000,), 0, 3125, jnp.int32)
        _loop = jnp.arange(3125, dtype=jnp.int32)
        src = jnp.concatenate([_s, _d, _loop])
        dst = jnp.concatenate([_d, _s, _loop])
        _o = jnp.argsort(dst, stable=True)
        src = src[_o]
        dst = dst[_o]
        return (x, src, dst)
    x, src, dst = _rec_inputs()

    def _L0_gnn_setup():
        import jax, jax.numpy as jnp
        import numpy as np
        N = 3125
        NUM_USERS = 1250
        E = 50000
        IN_DIM = 256
        OUT_DIM = 256
        H = 8
        DK = OUT_DIM // H
        key = jax.random.key(seed)
        ks = jax.random.split(key, 16)
        inp = {'x': jax.random.normal(ks[0], (N, IN_DIM), dtype=jnp.float32), 'row': jax.random.randint(ks[1], (E,), 0, N, dtype=jnp.int32), 'col': jax.random.randint(ks[2], (E,), 0, N, dtype=jnp.int32), 'relation_emb': jax.random.normal(ks[3], (OUT_DIM,), dtype=jnp.float32), 'user_text_embs': jax.random.normal(ks[4], (NUM_USERS, IN_DIM), dtype=jnp.float32), 'item_text_embs': jax.random.normal(ks[5], (N - NUM_USERS, IN_DIM), dtype=jnp.float32), 'Wq': jax.random.normal(ks[6], (OUT_DIM, IN_DIM), dtype=jnp.float32) * 0.02, 'bq': jnp.zeros((OUT_DIM,), dtype=jnp.float32), 'Wk': jax.random.normal(ks[7], (OUT_DIM, IN_DIM), dtype=jnp.float32) * 0.02, 'bk': jnp.zeros((OUT_DIM,), dtype=jnp.float32), 'Wv': jax.random.normal(ks[8], (OUT_DIM, IN_DIM), dtype=jnp.float32) * 0.02, 'bv': jnp.zeros((OUT_DIM,), dtype=jnp.float32), 'Wo': jax.random.normal(ks[9], (OUT_DIM, OUT_DIM), dtype=jnp.float32) * 0.02, 'bo': jnp.zeros((OUT_DIM,), dtype=jnp.float32)}
        return inp
    _L0_gnn_all = _L0_gnn_setup()
    _L0_gnn_in = {k: v for k, v in _L0_gnn_all.items() if k in ('relation_emb', 'user_text_embs', 'item_text_embs', 'Wq', 'bq', 'Wk', 'bk', 'Wv', 'bv', 'Wo', 'bo')}
    del _L0_gnn_all

    def _L1_gnn_setup():
        import jax, jax.numpy as jnp
        import numpy as np
        N = 3125
        E_RAND = 50000
        IN = 256
        OUT = 256
        H = 4
        D = OUT // H
        key = jax.random.key(seed)
        k1, k2, k3, k4, k5, k6 = jax.random.split(key, 6)
        feature = jax.random.normal(k1, (N, IN), jnp.float32)
        W_lin = jax.random.normal(k2, (OUT, IN), jnp.float32) / np.sqrt(IN)
        W_attn = jax.random.normal(k3, (OUT, IN), jnp.float32) / np.sqrt(IN)
        a = jax.random.normal(k4, (H, 2 * D), jnp.float32) * 0.1
        src = jnp.concatenate([jax.random.randint(k5, (E_RAND,), 0, N), jnp.arange(N)])
        dst = jnp.concatenate([jax.random.randint(k6, (E_RAND,), 0, N), jnp.arange(N)])
        return {'feature': feature, 'W_lin': W_lin, 'W_attn': W_attn, 'a': a, 'src': src, 'dst': dst}
    _L1_gnn_all = _L1_gnn_setup()
    _L1_gnn_in = {k: v for k, v in _L1_gnn_all.items() if k in ('W_lin', 'W_attn', 'a')}
    del _L1_gnn_all

    def _L2_gnn_setup():
        import jax, jax.numpy as jnp
        import numpy as np
        N = 3125
        E = 18750
        D = 256
        L = 5
        BN_EPS = 1e-05

        def _bn(h, gamma, beta):
            mean = jnp.mean(h, axis=0)
            var = jnp.var(h, axis=0)
            return (h - mean) * jax.lax.rsqrt(var + BN_EPS) * gamma + beta
        key = jax.random.key(seed)
        ks = jax.random.split(key, 6)
        scale = 0.05
        return {'x': jax.random.normal(ks[0], (N, D), jnp.float32), 'src': jax.random.randint(ks[1], (E,), 0, N, dtype=jnp.int32), 'dst': jax.random.randint(ks[2], (E,), 0, N, dtype=jnp.int32), 'W1': jax.random.normal(ks[3], (L, D, D), jnp.float32) * scale, 'b1': jnp.zeros((L, D), jnp.float32), 'g1': jnp.ones((L, D), jnp.float32), 'bt1': jnp.zeros((L, D), jnp.float32), 'W2': jax.random.normal(ks[4], (L, D, D), jnp.float32) * scale, 'b2': jnp.zeros((L, D), jnp.float32), 'eps': jnp.zeros((L,), jnp.float32), 'bn_g': jnp.ones((L, D), jnp.float32), 'bn_b': jnp.zeros((L, D), jnp.float32)}
    _L2_gnn_all = _L2_gnn_setup()
    _L2_gnn_in = {k: v for k, v in _L2_gnn_all.items() if k in ('W1', 'b1', 'g1', 'bt1', 'W2', 'b2', 'eps', 'bn_g', 'bn_b')}
    del _L2_gnn_all

    def _L3_gnn_setup():
        import jax, jax.numpy as jnp
        import numpy as np
        N_NODES = 3125
        N_EDGES = 50000
        D_IN = 256
        D_HID = 256
        D_OUT = 256

        def _sage_conv(x, src, dst, Wl, bl, Wr, num_nodes):
            msg = x[src]
            agg = jax.ops.segment_sum(msg, dst, num_segments=num_nodes)
            deg = jax.ops.segment_sum(jnp.ones((src.shape[0],), x.dtype), dst, num_segments=num_nodes)
            mean = agg / jnp.maximum(deg, 1.0)[:, None]
            return jnp.einsum('nd,od->no', mean, Wl) + bl + jnp.einsum('nd,od->no', x, Wr)
        key = jax.random.key(seed)
        ks = jax.random.split(key, 12)
        x = jax.random.normal(ks[0], (N_NODES, D_IN), dtype=jnp.float32)
        edge_index = jax.random.randint(ks[1], (2, N_EDGES), 0, N_NODES, dtype=jnp.int32)

        def lin(k, dout, din):
            return jax.random.normal(k, (dout, din), dtype=jnp.float32) * (1.0 / np.sqrt(din))
        return {'x': x, 'edge_index': edge_index, 'W1l': lin(ks[2], D_HID, D_IN), 'b1l': jnp.zeros((D_HID,), jnp.float32), 'W1r': lin(ks[3], D_HID, D_IN), 'W2l': lin(ks[4], D_HID, D_HID), 'b2l': jnp.zeros((D_HID,), jnp.float32), 'W2r': lin(ks[5], D_HID, D_HID), 'W3l': lin(ks[6], D_OUT, D_HID), 'b3l': jnp.zeros((D_OUT,), jnp.float32), 'W3r': lin(ks[7], D_OUT, D_HID)}
    _L3_gnn_all = _L3_gnn_setup()
    _L3_gnn_in = {k: v for k, v in _L3_gnn_all.items() if k in ('W1l', 'b1l', 'W1r', 'W2l', 'b2l', 'W2r', 'W3l', 'b3l', 'W3r')}
    del _L3_gnn_all
    return {'x': x, 'src': src, 'dst': dst, 'L0_gnn_relation_emb': _L0_gnn_in['relation_emb'], 'L0_gnn_user_text_embs': _L0_gnn_in['user_text_embs'], 'L0_gnn_item_text_embs': _L0_gnn_in['item_text_embs'], 'L0_gnn_Wq': _L0_gnn_in['Wq'], 'L0_gnn_bq': _L0_gnn_in['bq'], 'L0_gnn_Wk': _L0_gnn_in['Wk'], 'L0_gnn_bk': _L0_gnn_in['bk'], 'L0_gnn_Wv': _L0_gnn_in['Wv'], 'L0_gnn_bv': _L0_gnn_in['bv'], 'L0_gnn_Wo': _L0_gnn_in['Wo'], 'L0_gnn_bo': _L0_gnn_in['bo'], 'L1_gnn_W_lin': _L1_gnn_in['W_lin'], 'L1_gnn_W_attn': _L1_gnn_in['W_attn'], 'L1_gnn_a': _L1_gnn_in['a'], 'L2_gnn_W1': _L2_gnn_in['W1'], 'L2_gnn_b1': _L2_gnn_in['b1'], 'L2_gnn_g1': _L2_gnn_in['g1'], 'L2_gnn_bt1': _L2_gnn_in['bt1'], 'L2_gnn_W2': _L2_gnn_in['W2'], 'L2_gnn_b2': _L2_gnn_in['b2'], 'L2_gnn_eps': _L2_gnn_in['eps'], 'L2_gnn_bn_g': _L2_gnn_in['bn_g'], 'L2_gnn_bn_b': _L2_gnn_in['bn_b'], 'L3_gnn_W1l': _L3_gnn_in['W1l'], 'L3_gnn_b1l': _L3_gnn_in['b1l'], 'L3_gnn_W1r': _L3_gnn_in['W1r'], 'L3_gnn_W2l': _L3_gnn_in['W2l'], 'L3_gnn_b2l': _L3_gnn_in['b2l'], 'L3_gnn_W2r': _L3_gnn_in['W2r'], 'L3_gnn_W3l': _L3_gnn_in['W3l'], 'L3_gnn_b3l': _L3_gnn_in['b3l'], 'L3_gnn_W3r': _L3_gnn_in['W3r']}

def reference(x, src, dst, L0_gnn_relation_emb, L0_gnn_user_text_embs, L0_gnn_item_text_embs, L0_gnn_Wq, L0_gnn_bq, L0_gnn_Wk, L0_gnn_bk, L0_gnn_Wv, L0_gnn_bv, L0_gnn_Wo, L0_gnn_bo, L1_gnn_W_lin, L1_gnn_W_attn, L1_gnn_a, L2_gnn_W1, L2_gnn_b1, L2_gnn_g1, L2_gnn_bt1, L2_gnn_W2, L2_gnn_b2, L2_gnn_eps, L2_gnn_bn_g, L2_gnn_bn_b, L3_gnn_W1l, L3_gnn_b1l, L3_gnn_W1r, L3_gnn_W2l, L3_gnn_b2l, L3_gnn_W2r, L3_gnn_W3l, L3_gnn_b3l, L3_gnn_W3r):
    import jax
    import jax.numpy as jnp

    def _L0_gnn_ref(x, row, col, relation_emb, user_text_embs, item_text_embs, Wq, bq, Wk, bk, Wv, bv, Wo, bo):
        import jax, jax.numpy as jnp
        import numpy as np
        N = 3125
        NUM_USERS = 1250
        E = 50000
        IN_DIM = 256
        OUT_DIM = 256
        H = 8
        DK = OUT_DIM // H
        text_emb = jnp.concatenate([user_text_embs, item_text_embs], axis=0)
        Q = (text_emb @ Wq.T + bq).reshape(N, H, DK)
        K = (text_emb @ Wk.T + bk).reshape(N, H, DK)
        V = (x @ Wv.T + bv).reshape(N, H, DK)
        Q_ = Q[col]
        K_ = K[row]
        V_ = V[row]
        rel = relation_emb.reshape(1, H, DK)
        scores = jnp.sum(Q_ * (K_ + rel), axis=-1) / np.sqrt(DK).astype(np.float32)
        m = jax.ops.segment_max(scores, col, num_segments=N)
        e = jnp.exp(scores - m[col])
        denom = jax.ops.segment_sum(e, col, num_segments=N)
        attn = e / denom[col]
        out = jax.ops.segment_sum(attn[:, :, None] * V_, col, num_segments=N)
        out = out.reshape(N, OUT_DIM)
        return out @ Wo.T + bo

    def _L1_gnn_ref(feature, W_lin, W_attn, a, src, dst):
        import jax, jax.numpy as jnp
        import numpy as np
        N = 3125
        E_RAND = 50000
        IN = 256
        OUT = 256
        H = 4
        D = OUT // H
        key = (feature @ W_attn.T).reshape(N, H, D)
        alpha_src = jnp.einsum('nhd,hd->nh', key, a[:, :D])
        alpha_dst = jnp.einsum('nhd,hd->nh', key, a[:, D:])
        score = alpha_src[src] + alpha_dst[dst]
        score = jnp.where(score > 0, score, 0.2 * score)
        smax = jax.ops.segment_max(score, dst, num_segments=N)
        ex = jnp.exp(score - smax[dst])
        denom = jax.ops.segment_sum(ex, dst, num_segments=N)
        attn = ex / denom[dst]
        val = (feature @ W_lin.T).reshape(N, H, D)
        msg = attn[:, :, None] * val[src]
        h = jax.ops.segment_sum(msg, dst, num_segments=N).reshape(N, OUT)
        return h

    def _L2_gnn_ref(x, src, dst, W1, b1, g1, bt1, W2, b2, eps, bn_g, bn_b):
        import jax, jax.numpy as jnp
        import numpy as np
        N = 3125
        E = 18750
        D = 256
        L = 5
        BN_EPS = 1e-05

        def _bn(h, gamma, beta):
            mean = jnp.mean(h, axis=0)
            var = jnp.var(h, axis=0)
            return (h - mean) * jax.lax.rsqrt(var + BN_EPS) * gamma + beta
        h = x
        for l in range(L):
            msg = jax.nn.relu(h[src])
            agg = jax.ops.segment_sum(msg, dst, num_segments=N)
            z = (1.0 + eps[l]) * h + agg
            z = z @ W1[l] + b1[l]
            z = jax.nn.relu(_bn(z, g1[l], bt1[l]))
            z = z @ W2[l] + b2[l]
            z = _bn(z, bn_g[l], bn_b[l])
            if l < L - 1:
                z = jax.nn.relu(z)
            h = z
        return h

    def _L3_gnn_ref(x, edge_index, W1l, b1l, W1r, W2l, b2l, W2r, W3l, b3l, W3r):
        import jax, jax.numpy as jnp
        import numpy as np
        N_NODES = 3125
        N_EDGES = 50000
        D_IN = 256
        D_HID = 256
        D_OUT = 256

        def _sage_conv(x, src, dst, Wl, bl, Wr, num_nodes):
            msg = x[src]
            agg = jax.ops.segment_sum(msg, dst, num_segments=num_nodes)
            deg = jax.ops.segment_sum(jnp.ones((src.shape[0],), x.dtype), dst, num_segments=num_nodes)
            mean = agg / jnp.maximum(deg, 1.0)[:, None]
            return jnp.einsum('nd,od->no', mean, Wl) + bl + jnp.einsum('nd,od->no', x, Wr)
        src, dst = (edge_index[0], edge_index[1])
        n = x.shape[0]
        h = _sage_conv(x, src, dst, W1l, b1l, W1r, n)
        h = jax.nn.relu(h)
        h = _sage_conv(h, src, dst, W2l, b2l, W2r, n)
        h = jax.nn.relu(h)
        h = _sage_conv(h, src, dst, W3l, b3l, W3r, n)
        return h
    edge_index = jnp.stack([src, dst])
    x = _layernorm(x + _L0_gnn_ref(x, src, dst, L0_gnn_relation_emb, L0_gnn_user_text_embs, L0_gnn_item_text_embs, L0_gnn_Wq, L0_gnn_bq, L0_gnn_Wk, L0_gnn_bk, L0_gnn_Wv, L0_gnn_bv, L0_gnn_Wo, L0_gnn_bo), axis=-1)
    x = _layernorm(x + _L1_gnn_ref(x, L1_gnn_W_lin, L1_gnn_W_attn, L1_gnn_a, src, dst), axis=-1)
    x = _layernorm(x + _L2_gnn_ref(x, src, dst, L2_gnn_W1, L2_gnn_b1, L2_gnn_g1, L2_gnn_bt1, L2_gnn_W2, L2_gnn_b2, L2_gnn_eps, L2_gnn_bn_g, L2_gnn_bn_b), axis=-1)
    x = _layernorm(x + _L3_gnn_ref(x, edge_index, L3_gnn_W1l, L3_gnn_b1l, L3_gnn_W1r, L3_gnn_W2l, L3_gnn_b2l, L3_gnn_W2r, L3_gnn_W3l, L3_gnn_b3l, L3_gnn_W3r), axis=-1)
    return x

_drawn_inputs = setup_inputs


def setup_inputs(seed=0):
    import zlib

    import numpy as np

    out = dict(_drawn_inputs(seed))
    spreads = {'L0_gnn_bq': (0.0, 0.8),
     'L0_gnn_bk': (0.0, 0.8),
     'L0_gnn_bv': (0.0, 0.1),
     'L0_gnn_bo': (0.0, 0.1),
     'L2_gnn_b1': (0.0, 0.8),
     'L2_gnn_g1': (1.0, 0.2),
     'L2_gnn_bt1': (0.0, 0.1),
     'L2_gnn_b2': (0.0, 0.8),
     'L2_gnn_eps': (0.0, 0.378),
     'L2_gnn_bn_g': (1.0, 0.2),
     'L2_gnn_bn_b': (0.0, 0.1),
     'L3_gnn_b1l': (0.0, 0.1),
     'L3_gnn_b2l': (0.0, 0.1),
     'L3_gnn_b3l': (0.0, 0.1)}
    factors = {'L0_gnn_relation_emb': 8.0,
     'L0_gnn_user_text_embs': 8.0,
     'L0_gnn_item_text_embs': 8.0,
     'L0_gnn_Wq': 8.0,
     'L0_gnn_Wk': 8.0}
    for name, (base, spread) in spreads.items():
        noise = np.random.default_rng([zlib.crc32(name.encode()), seed]).standard_normal(out[name].shape)
        drawn = base * np.exp(spread * noise) if base else spread * noise
        out[name] = jnp.asarray(drawn.astype(out[name].dtype))
    for name, factor in factors.items():
        out[name] = (out[name] * factor).astype(out[name].dtype)
    return out
```

```python
from contextlib import ExitStack

import concourse.bass as bass
from concourse import mybir

F32 = mybir.dt.float32
F16 = mybir.dt.float16
BF16 = mybir.dt.bfloat16
I32 = mybir.dt.int32
ALU = mybir.AluOpType
ACT = mybir.ActivationFunctionType
AX_X = mybir.AxisListType.X

P = 128
N = 3125
D = 256
E = 53125
KH = D // P
NT = -(-N // P)
NP = NT * P
H = 8
DK = D // H
C = 416
G = 8
NG = C // G
LINK = P + 1
PT = 28
PARTS = PT * P
PBUF = PARTS + P
BLK = 512
NB = PARTS // BLK
FAR = 1.0e30
SMALL = 96
COL_MAX = 32
COL_NODE = 64
EPS = 1e-5

APASS = 4
ACOLS = 782
AW = APASS * ACOLS
AN = ACOLS // 2
SLAB = 5
NSLAB = NT // SLAB
FS = 16.0


class Phase(ExitStack):

    def __init__(self, nc):
        super().__init__()
        self.nc, self.used = nc, []
        self.callback(self.clear)

    def clear(self):
        self.nc.clear_and_free_semaphores(self.used)
        self.nc.all_engine_barrier()


def sems(nc, ctx, *names):
    made = [nc.alloc_semaphore(name=n) for n in names]
    ctx.used += made
    return made


def prepare_edges(nc, ins, keep, scratch):
    with Phase(nc) as ctx:
        def sb(name, shape, dt):
            return ctx.enter_context(nc.sbuf_tensor("pe_" + name, shape, dt))
        link_in = sb("link_in", [G * H, NG, P], I32)
        same = sb("same", [G * H, NG, P], BF16)
        dst_f = sb("dst_f", [P, C], F32)
        prev_f = sb("prev_f", [P, C], I32)
        src_rank = sb("src_rank", [P, C], I32)
        dst_rank = sb("dst_rank", [P, C], I32)
        cell = sb("cell", [P, C], F32)
        tri = sb("tri", [P, P], F32)
        zero16 = sb("zero16", [P, NP * AW // P // 8], F16)
        counts = sb("counts", [1, C + 1], F32)
        zrow = sb("zrow", [1, C], F32)
        rank_ps = ctx.enter_context(nc.psum_tensor("pe_rank_ps", [P, BLK], F32))
        num_ps = ctx.enter_context(nc.psum_tensor("pe_num_ps", [P, BLK], F32))
        loaded, links, zeroed, const, ramp, first, rank, offs, done, cells, lk = sems(
            nc, ctx, "pe_loaded", "pe_links", "pe_zeroed", "pe_const", "pe_ramp", "pe_first", "pe_rank",
            "pe_offs", "pe_done", "pe_cells", "pe_lk")
        block = ctx.enter_context(nc.Block("prep"))

        @block.sync
        def _(sp):
            for to, of in ((keep["src"], ins["src_col"]), (keep["dst"], ins["dst_col"]), (prev_f, ins["dst_prev"]),
                           (src_rank, ins["src_row"]), (dst_rank, ins["dst_row"])):
                sp.dma_start(to[:, :], of).then_inc(loaded, 16)
            rows = ins["dst_chunk"].rearrange("(g j) e -> j g e", j=G)
            for j in range(G):
                wide = bass.AP(tensor=rows.tensor, offset=rows[j].offset, ap=[[0, H]] + [list(a) for a in rows[j].ap])
                sp.dma_start(link_in[j * H:(j + 1) * H, :, :], wide).then_inc(links, 16)
            sp.wait_ge(const, 5)
            adj = scratch["adj"].rearrange("(e p c) o -> e p (c o)", e=8, p=P)
            for k in range(8):
                sp.dma_start(adj[k], zero16[:, :]).then_inc(zeroed, 16)
            for name in ("out0", "out1"):
                sp.dma_start(scratch[name].rearrange("(t p) d -> p t d", p=P), keep["x"][:, :, :]).then_inc(zeroed, 16)
            sp.wait_ge(zeroed, 160)
            sp.dma_start(keep["x"][:, :, :], ins["x"].rearrange("(t p) d -> p t d", p=P)).then_inc(loaded, 16)
            sp.wait_ge(loaded, 96)

        @block.gpsimd
        def _(pool):
            nc.gpsimd.memset(keep["ident"][:, :], 0.0).then_inc(const, 1)
            nc.gpsimd.memset(tri[:, :], 1.0).then_inc(const, 1)
            nc.gpsimd.memset(keep["hsel"][:, :], 1.0).then_inc(const, 1)
            pool.wait_ge(const, 5)
            nc.gpsimd.affine_select(out=keep["ident"][:, :], in_=keep["ident"][:, :], compare_op=ALU.not_equal,
                                    fill=1.0, base=0, pattern=[[-1, P]], channel_multiplier=1).then_inc(const, 1)
            nc.gpsimd.affine_select(out=tri[:, :], in_=tri[:, :], compare_op=ALU.is_ge,
                                    fill=0.0, base=0, pattern=[[1, P]], channel_multiplier=-1).then_inc(const, 1)
            nc.gpsimd.affine_select(out=keep["hsel"][:, :], in_=keep["hsel"][:, :], compare_op=ALU.is_ge,
                                    fill=0.0, base=0, pattern=[[1, D]], channel_multiplier=-DK).then_inc(const, 1)
            pool.wait_ge(const, 8)
            nc.gpsimd.affine_select(out=keep["hsel"][:, :], in_=keep["hsel"][:, :], compare_op=ALU.is_ge,
                                    fill=0.0, base=DK - 1, pattern=[[-1, D]], channel_multiplier=DK).then_inc(const, 1)
            nc.gpsimd.iota(keep["iota"][:, :], [[1, P]], base=0, channel_multiplier=0,
                           allow_small_or_imprecise_dtypes=True).then_inc(ramp, 1)

        @block.vector
        def _(v):
            nc.vector.memset(zero16[:, :], 0.0).then_inc(const, 1)
            nc.vector.memset(keep["x"][:, :, :], 0.0).then_inc(const, 1)
            nc.vector.memset(keep["ones"][:, :], 1.0).then_inc(rank, 1)
            nc.vector.memset(zrow[:, :], 0.0).then_inc(rank, 1)
            nc.vector.memset(counts[:, :], 0.0).then_inc(rank, 1)
            nc.vector.memset(keep["link"][:, :, :], 0.0).then_inc(lk, 1)
            v.wait_ge(loaded, 80)
            nc.vector.tensor_tensor(keep["first"][:, :], keep["dst"][:, :], prev_f[:, :], ALU.not_equal).then_inc(first, 1)
            nc.vector.tensor_scalar(dst_f[:, :], keep["dst"][:, :], 1.0, None, ALU.add).then_inc(first, 1)
            nc.vector.tensor_scalar(cell[:, :], src_rank[:, :], float(AW), None, ALU.mult).then_inc(cells, 1)
            v.wait_ge(cells, 1)
            nc.vector.tensor_tensor(keep["cell"][:, :], cell[:, :], dst_rank[:, :], ALU.add).then_inc(cells, 1)
            v.wait_ge(first, 2)
            nc.vector.tensor_tensor(keep["node"][:, :], dst_f[:, :], keep["first"][:, :], ALU.mult).then_inc(done, 1)
            v.wait_ge(rank, 5)
            nc.vector.tensor_scalar(keep["slot"][:, :], rank_ps[:, 0:C], -1.0, None, ALU.add).then_inc(done, 1)
            nc.vector.tensor_tensor_scan(counts[:, 1:C + 1], zrow[:, :], num_ps[0:1, 0:C], 0.0, ALU.add, ALU.add).then_inc(offs, 1)
            v.wait_ge(offs, 1)
            nc.vector.tensor_copy(keep["offset"][:, :], counts[:, 0:C]).then_inc(done, 1)
            v.wait_ge(links, 16 * G)
            v.wait_ge(lk, 1)
            nc.vector.tensor_tensor(same[:, :, 1:P], link_in[:, :, 1:P], link_in[:, :, 0:P - 1], ALU.is_equal).then_inc(lk, 1)
            v.wait_ge(lk, 2)
            nc.vector.tensor_scalar(keep["link"][:, :, 1:P], same[:, :, 1:P], -1.0, FAR, ALU.add, ALU.mult).then_inc(lk, 1)
            v.wait_ge(lk, 3)
            nc.vector.tensor_copy(keep["link_back"][:, :, :], keep["link"][:, :, P:0:-1]).then_inc(lk, 1)

        @block.tensor
        def _(pe):
            pe.wait_ge(const, 7)
            pe.wait_ge(rank, 3)
            pe.wait_ge(first, 1)
            nc.tensor.matmul(rank_ps[:, 0:C], tri[:, :], keep["first"][:, :], start=True, stop=True).then_inc(rank, 1)
            nc.tensor.matmul(num_ps[0:1, 0:C], keep["ones"][:, 0:1], keep["first"][:, :], start=True, stop=True).then_inc(rank, 1)


def tables_layer0(nc, ins, keep, scratch):
    with Phase(nc) as ctx:
        def sb(name, shape, dt):
            return ctx.enter_context(nc.sbuf_tensor("t0_" + name, shape, dt))
        x_t = sb("x_t", [P, KH, NP], F32)
        text_t = sb("text_t", [P, KH, NP], F32)
        w = sb("w", [P, 3, KH, D], F32)
        bias = sb("bias", [P, 3, D], F32)
        rel = sb("rel", [P, D], F32)
        out = sb("out", [P, 4, 3 * D], F32)
        ps = [ctx.enter_context(nc.psum_tensor(f"t0_ps{i}", [P, 2, BLK], F32)) for i in range(4)]
        loaded, bias_in, biased, summed, made = sems(
            nc, ctx, "t0_loaded", "t0_bias_in", "t0_biased", "t0_summed", "t0_made")
        stored = sems(nc, ctx, *(f"t0_stored{i}" for i in range(4)))
        block = ctx.enter_context(nc.Block("tables0"))

        def all_rows(ap):
            return bass.AP(tensor=ap.tensor, offset=ap.offset, ap=[[0, P]] + [list(a) for a in ap.ap])

        @block.sync
        def _(sp):
            for i, name in enumerate(("wv_t", "wk_t", "wq_t")):
                sp.dma_start(w[:, i, :, :], ins[name].rearrange("(k p) o -> p k o", p=P)).then_inc(loaded, 16)
            sp.dma_start(x_t[:, :, :], ins["x_t"].rearrange("(k p) n -> p k n", p=P)).then_inc(loaded, 16)
            sp.dma_start(text_t[:, :, :], ins["text_t"].rearrange("(k p) n -> p k n", p=P)).then_inc(loaded, 16)
            for i, name in enumerate(("L0_gnn_bv", "L0_gnn_bk", "L0_gnn_bq")):
                sp.dma_start(bias[:, i, :], all_rows(ins[name])).then_inc(bias_in, 16)
            sp.dma_start(rel[:, :], all_rows(ins["L0_gnn_relation_emb"])).then_inc(bias_in, 16)
            for t in range(NT):
                sp.wait_ge(made, 2 * (t + 1))
                sp.dma_start(scratch["vk"][t * P:(t + 1) * P, :], out[:, t % 4, 0:2 * D]).then_inc(stored[t % 4], 16)
                sp.dma_start(scratch["q"][t * P:(t + 1) * P, :], out[:, t % 4, 2 * D:3 * D]).then_inc(stored[t % 4], 16)
            for i in range(4):
                sp.wait_ge(stored[i], 32 * len(range(i, NT, 4)))

        @block.tensor
        def _(pe):
            pe.wait_ge(loaded, 80)
            for t in range(NT):
                if t >= 4:
                    pe.wait_ge(made, 2 * (t - 3))
                for i, of in enumerate((x_t, text_t, text_t)):
                    for k in range(KH):
                        mm = nc.tensor.matmul(ps[t % 4][:, i // 2, (i % 2) * D:(i % 2) * D + D],
                                              of[:, k, t * P:(t + 1) * P], w[:, i, k, :], start=(k == 0), stop=(k == KH - 1))
                mm.then_inc(summed, 1)

        @block.vector
        def _(v):
            v.wait_ge(bias_in, 64)
            nc.vector.tensor_tensor(bias[:, 1, :], bias[:, 1, :], rel[:, :], ALU.add).then_inc(biased, 1)
            v.wait_ge(biased, 1)
            for t in range(NT):
                v.wait_ge(summed, t + 1)
                if t >= 4:
                    v.wait_ge(stored[t % 4], 32 * (t // 4))
                nc.vector.tensor_tensor(out[:, t % 4, 0:2 * D], ps[t % 4][:, 0, :],
                                        bias[:, 0:2, :].rearrange("p a d -> p (a d)"), ALU.add).then_inc(made, 1)
                nc.vector.tensor_tensor(out[:, t % 4, 2 * D:3 * D], ps[t % 4][:, 1, 0:D], bias[:, 2, :], ALU.add).then_inc(made, 1)


def attend_edges(nc, keep, scratch, layer, by_src, by_dst, ws, wd, scale, build_adjacency):
    with Phase(nc) as ctx:
        def sb(name, shape, dt):
            return ctx.enter_context(nc.sbuf_tensor(f"e{layer}_" + name, shape, dt))
        from_src = sb("from_src", [P, 2, G, ws], F32)
        from_dst = sb("from_dst", [P, 2, G, wd], F32)
        src_ix = sb("src_ix", [P, 2, G], I32)
        dst_ix = sb("dst_ix", [P, 2, G], I32)
        cell_ix = sb("cell_ix", [P, 2, G], I32)
        one16 = sb("one16", [P, 1], F16)
        score = sb("score", [P, 2, G * H], F32)
        shifted = sb("shifted", [P, 2, G * H], F32)
        running = sb("running", [G * H, P], F32)
        peak = sb("peak", [G * H, 2, P], F32)
        small = sb("small", [P, 2, G, SMALL], F32)
        onehot = sb("onehot", [P, 2, G, P], F32)

        def pst(name):
            return ctx.enter_context(nc.psum_tensor(f"e{layer}_" + name, [P, BLK], F32))
        turned = pst("turned")
        back = pst("back")
        part_ps = [pst(f"part_ps{i}") for i in range(2)]
        (ix_ready, cell_added, raw, scored, t_turned, fwd, peaked, t_back, shift_done, prob, mask_done, weighted,
         zeroed, one_set, passed, pe_passed) = sems(
            nc, ctx, *(f"e{layer}_" + n for n in (
                "ix_ready", "cell_added", "raw", "scored", "t_turned", "fwd", "peaked", "t_back", "shift_done",
                "prob", "mask_done", "weighted", "zeroed", "one_set", "passed", "pe_passed")))
        chunk_summed = sems(nc, ctx, *(f"e{layer}_chunk_summed{b}" for b in range(2)))
        evacuated = sems(nc, ctx, *(f"e{layer}_evacuated{s}" for s in range(2)))
        src_in = sems(nc, ctx, *(f"e{layer}_src_in{b}" for b in range(2)))
        dst_in = sems(nc, ctx, *(f"e{layer}_dst_in{b}" for b in range(2)))
        block = ctx.enter_context(nc.Block(f"edges{layer}"))

        @block.gpsimd
        def _(pool):
            pool.wait_ge(one_set, 1)
            with pool.Fori(0, NG // 2) as it:
                for b in range(2):
                    g = 2 * it + b
                    pool.wait_ge(chunk_summed[b], G * it + 1)
                    cols = bass.ds(g * G, G)
                    nc.gpsimd.tensor_copy(src_ix[:, b, :], keep["src"][:, cols]).then_inc(ix_ready, 1)
                    nc.gpsimd.tensor_copy(dst_ix[:, b, :], keep["dst"][:, cols]).then_inc(ix_ready, 1)
                    nc.gpsimd.tensor_copy(cell_ix[:, b, :], keep["cell"][:, cols]).then_inc(ix_ready, 1)
                    pool.wait_ge(ix_ready, 3 * g + 3)
                    pool.sem_inc(passed, 1)
                    for j in range(G):
                        if build_adjacency:
                            if j:
                                pool.wait_ge(cell_added, 16 * G * g + 16 * j)
                                pool.sem_inc(passed, 1)
                            nc.gpsimd.indirect_dma_start(
                                scratch["adj"], bass.IndirectOffsetOnAxis(ap=cell_ix[:, b, j:j + 1], axis=0),
                                one16[:, 0:1], None, compute_op=ALU.add).then_inc(cell_added, 16)
                        nc.gpsimd.indirect_dma_start(
                            from_src[:, b, j, :], None, by_src,
                            bass.IndirectOffsetOnAxis(ap=src_ix[:, b, j:j + 1], axis=0)).then_inc(src_in[b], 16)
                        nc.gpsimd.indirect_dma_start(
                            from_dst[:, b, j, :], None, by_dst,
                            bass.IndirectOffsetOnAxis(ap=dst_ix[:, b, j:j + 1], axis=0)).then_inc(dst_in[b], 16)
                    if build_adjacency:
                        pool.wait_ge(cell_added, 16 * G * g + 16 * G)

        @block.vector
        def _(v):
            nc.vector.memset(one16[:, :], 1.0).then_inc(one_set, 1)
            nc.vector.memset(small[:, :, :, :], 0.0).then_inc(zeroed, 1)
            nc.vector.memset(keep["sums"][:, :, :], 0.0).then_inc(zeroed, 1)
            nc.vector.memset(keep["side"][:, :], 0.0).then_inc(zeroed, 1)
            v.wait_ge(zeroed, 3)
            with v.Fori(0, NG // 2) as it:
                for b in range(2):
                    g = 2 * it + b
                    v.wait_ge(src_in[b], 16 * G * it + 16 * G)
                    v.wait_ge(dst_in[b], 16 * G * it + 16 * G)
                    if layer == 0:
                        nc.vector.tensor_tensor(from_dst[:, b, :, :], from_dst[:, b, :, :], from_src[:, b, :, D:2 * D],
                                                ALU.mult).then_inc(raw, 1)
                        v.wait_ge(raw, g + 1)
                        nc.vector.tensor_reduce(score[:, b, :], from_dst[:, b, :, :].rearrange("p j (h d) -> p (j h) d", h=H),
                                                AX_X, ALU.add).then_inc(scored, 1)
                    else:
                        nc.vector.tensor_tensor(from_dst[:, b, :, :], from_dst[:, b, :, :], from_src[:, b, :, D:D + H],
                                                ALU.add).then_inc(raw, 1)
                        v.wait_ge(raw, g + 1)
                        nc.vector.scalar_tensor_tensor(
                            out=score[:, b, :].rearrange("p (j h) -> p j h", h=H), in0=from_dst[:, b, :, :], scalar=0.2,
                            in1=from_dst[:, b, :, :], op0=ALU.mult, op1=ALU.max).then_inc(scored, 1)
                    v.wait_ge(t_turned, g + 1)
                    nc.vector.tensor_tensor_scan(running[:, :], keep["link"][:, g, 0:P], turned[0:G * H, 0:P],
                                                 -FAR, ALU.add, ALU.max).then_inc(fwd, 1)
                    v.wait_ge(fwd, g + 1)
                    nc.vector.tensor_tensor_scan(peak[:, b, ::-1], keep["link_back"][:, g, :], running[:, ::-1],
                                                 -FAR, ALU.add, ALU.max).then_inc(peaked, 1)
                    v.wait_ge(t_back, g + 1)
                    nc.vector.tensor_tensor(shifted[:, b, :], score[:, b, :], back[:, 0:G * H], ALU.subtract).then_inc(shift_done, 1)
                    cols = bass.ds(g * G, G)
                    nc.vector.tensor_tensor(small[:, b, :, COL_MAX:COL_MAX + H],
                                            back[:, 0:G * H].rearrange("p (j h) -> p j h", h=H),
                                            keep["first"][:, cols].unsqueeze(2).to_broadcast([P, G, H]), ALU.mult).then_inc(mask_done, 1)
                    nc.vector.tensor_copy(small[:, b, :, COL_NODE], keep["node"][:, cols]).then_inc(mask_done, 1)
                    nc.vector.tensor_tensor(onehot[:, b, :, :], keep["iota"][:, :].unsqueeze(1).to_broadcast([P, G, P]),
                                            keep["slot"][:, cols].unsqueeze(2).to_broadcast([P, G, P]), ALU.is_equal).then_inc(mask_done, 1)
                    v.wait_ge(prob, g + 1)
                    nc.vector.tensor_tensor(
                        from_src[:, b, :, 0:D].rearrange("p j (h d) -> p j h d", h=H),
                        from_src[:, b, :, 0:D].rearrange("p j (h d) -> p j h d", h=H),
                        small[:, b, :, 0:H].unsqueeze(3).to_broadcast([P, G, H, DK]), ALU.mult).then_inc(weighted, 1)

        @block.tensor
        def _(pe):
            for b in range(2):
                pe.sem_inc(chunk_summed[b], 1)
            with pe.Fori(0, NG // 2) as it:
                for b in range(2):
                    g = 2 * it + b
                    pe.wait_ge(scored, g + 1)
                    pe.sem_inc(pe_passed, 1)
                    nc.tensor.transpose(turned[0:G * H, 0:P], score[:, b, :], keep["ident"][:, :]).then_inc(t_turned, 1)
                    pe.wait_ge(peaked, g + 1)
                    pe.sem_inc(pe_passed, 1)
                    nc.tensor.transpose(back[:, 0:G * H], peak[:, b, :], keep["ident"][0:G * H, 0:G * H]).then_inc(t_back, 1)
                    pe.wait_ge(weighted, g + 1)
                    pe.wait_ge(mask_done, 3 * g + 3)
                    for j in range(G):
                        s = j % 2
                        pe.wait_ge(evacuated[s], G * g + 2 * (j // 2) + 1)
                        for k in range(KH):
                            nc.tensor.matmul(part_ps[s][:, k * P:(k + 1) * P], from_src[:, b, j, k * P:(k + 1) * P],
                                             onehot[:, b, j, :], start=True, stop=True)
                        mm = nc.tensor.matmul(part_ps[s][0:SMALL, KH * P:KH * P + P], small[:, b, j, :], onehot[:, b, j, :],
                                              start=True, stop=True)
                        mm.then_inc(chunk_summed[b], 1)

        @block.scalar
        def _(act):
            act.wait_ge(zeroed, 3)
            for s in range(2):
                act.sem_inc(evacuated[s], 1)
            with act.Fori(0, NG // 2) as it:
                for b in range(2):
                    g = 2 * it + b
                    act.wait_ge(shift_done, g + 1)
                    nc.scalar.activation(small[:, b, :, 0:H], shifted[:, b, :].rearrange("p (j h) -> p j h", h=H),
                                         ACT.Exp, scale=scale).then_inc(prob, 1)
                    for j in range(G):
                        s = j % 2
                        at = act.value_load(keep["offset"][0:1, bass.ds(g * G + j, 1)], min_val=0, max_val=PARTS)
                        act.wait_ge(chunk_summed[b], G * it + j + 2)
                        act.wait_ge(evacuated[1 - s], G * g + 2 * ((j + 1) // 2) + 1)
                        nc.scalar.activation(keep["sums"][:, :, bass.ds(at, P)],
                                             part_ps[s][:, 0:KH * P].rearrange("p (k e) -> p k e", k=KH), ACT.Copy).then_inc(evacuated[s], 1)
                        nc.scalar.activation(keep["side"][:, bass.ds(at, P)], part_ps[s][0:SMALL, KH * P:KH * P + P],
                                             ACT.Copy).then_inc(evacuated[s], 1)


def merge_parts(nc, ins, keep, scratch, layer, weight, out_rows, scale):
    with Phase(nc) as ctx:
        def sb(name, shape, dt):
            return ctx.enter_context(nc.sbuf_tensor(f"m{layer}_" + name, shape, dt))
        w_out = sb("w_out", [P, KH, D], F32)
        node_row = sb("node_row", [1, PARTS], F32)
        node_all = sb("node_all", [P, PARTS + 2], F32)
        joined = sb("joined", [P, PARTS + 1], BF16)
        peak = sb("peak", [H, PARTS], F32)
        link = sb("link", [H, PARTS + 1], F32)
        work = sb("work", [H, PARTS], F32)
        top = sb("top", [H, PARTS], F32)
        rows = sb("rows", [P, 4, D], F32)
        index = sb("index", [P, PT], I32)

        def pst(name):
            return ctx.enter_context(nc.psum_tensor(f"m{layer}_" + name, [P, BLK], F32))
        wide_ps = [pst(f"wide_ps{i}") for i in range(4)]
        row_ps = [pst(f"row_ps{i}") for i in range(2)]
        index_ps = pst("index_ps")
        carried = sb("carried", [P, KH, NB], F32)
        sums, side = keep["sums"], keep["side"]
        (w_in, moved, spread, copied, step, expd, wide, summed, idx, idx_t, projected, out_copied, carry_kept,
         indexed, ends_set) = sems(
            nc, ctx, *(f"m{layer}_" + n for n in (
                "w_in", "moved", "spread", "copied", "step", "expd", "wide", "summed", "idx", "idx_t", "projected",
                "out_copied", "carry_kept", "indexed", "ends_set")))
        stored = sems(nc, ctx, *(f"m{layer}_stored{i}" for i in range(4)))
        block = ctx.enter_context(nc.Block(f"merge{layer}"))

        @block.sync
        def _(sp):
            if weight is not None:
                sp.dma_start(w_out[:, :, :], ins[weight].rearrange("(k p) o -> p k o", p=P)).then_inc(w_in, 16)

        @block.scalar
        def _(act):
            nc.scalar.activation(node_row[:, :], side[COL_NODE:COL_NODE + 1, 0:PARTS], ACT.Copy).then_inc(moved, 1)
            nc.scalar.activation(peak[:, :], side[COL_MAX:COL_MAX + H, 0:PARTS], ACT.Copy).then_inc(moved, 1)
            for b in range(NB):
                act.wait_ge(spread, b + 1)
                nc.scalar.activation(node_all[:, 1 + b * BLK:1 + (b + 1) * BLK], wide_ps[b % 4][:, :], ACT.Copy).then_inc(copied, 1)
            act.wait_ge(step, 5)
            nc.scalar.activation(peak[:, :], work[:, :], ACT.Exp, scale=scale).then_inc(expd, 1)
            for t in range(PT):
                act.wait_ge(projected, t + 1)
                if t >= 4:
                    act.wait_ge(stored[t % 4], 16 * (t // 4))
                nc.scalar.activation(rows[:, t % 4, :], row_ps[t % 2][:, 0:D], ACT.Copy).then_inc(out_copied, 1)

        @block.tensor
        def _(pe):
            pe.wait_ge(moved, 1)
            for b in range(NB):
                if b >= 4:
                    pe.wait_ge(copied, b - 3)
                nc.tensor.matmul(wide_ps[b % 4][:, :], keep["ones"][0:1, :], node_row[:, b * BLK:(b + 1) * BLK],
                                 start=True, stop=True).then_inc(spread, 1)
            pe.wait_ge(copied, NB)
            pe.wait_ge(step, 9)
            for b in range(NB):
                for k in range(KH):
                    n = b * KH + k
                    for i, of in enumerate((peak, work)):
                        if n >= 2:
                            pe.wait_ge(summed, 3 * (n - 2) + (1 if i == 0 else 3))
                        nc.tensor.matmul(wide_ps[2 * (n % 2) + i][:, :], keep["hsel"][:, k * P:(k + 1) * P],
                                         of[:, b * BLK:(b + 1) * BLK], start=True, stop=True).then_inc(wide, 1)
            pe.wait_ge(idx, 4)
            for t in range(PT):
                mm = nc.tensor.matmul(index_ps[:, t:t + 1], node_row[:, t * P:(t + 1) * P], keep["ones"][0:1, 0:1],
                                      start=True, stop=True)
            mm.then_inc(idx_t, 1)
            if weight is not None:
                pe.wait_ge(w_in, 16)
            pe.wait_ge(summed, 3 * KH * NB)
            for t in range(PT):
                if t >= 2:
                    pe.wait_ge(out_copied, t - 1)
                for k in range(KH):
                    if weight is None:
                        mm = nc.tensor.transpose(row_ps[t % 2][:, k * P:(k + 1) * P], sums[:, k, t * P:(t + 1) * P],
                                                 keep["ident"][:, :])
                    else:
                        mm = nc.tensor.matmul(row_ps[t % 2][:, 0:D], sums[:, k, t * P:(t + 1) * P], w_out[:, k, :],
                                              start=(k == 0), stop=(k == KH - 1))
                mm.then_inc(projected, 1)

        @block.vector
        def _(v):
            nc.vector.memset(node_all[:, 0:1], -1.0).then_inc(ends_set, 1)
            nc.vector.memset(node_all[:, PARTS + 1:PARTS + 2], -1.0).then_inc(ends_set, 1)
            v.wait_ge(moved, 2)
            v.wait_ge(ends_set, 2)
            v.wait_ge(copied, NB)
            nc.vector.tensor_tensor(joined[:, :], node_all[:, 1:PARTS + 2], node_all[:, 0:PARTS + 1], ALU.is_equal).then_inc(step, 1)
            v.wait_ge(step, 1)
            nc.vector.tensor_scalar(link[:, :], joined[0:H, :], -1.0, FAR, ALU.add, ALU.mult).then_inc(step, 1)
            v.wait_ge(step, 2)
            nc.vector.tensor_tensor_scan(work[:, :], link[:, 0:PARTS], peak[:, :], -FAR, ALU.add, ALU.max).then_inc(step, 1)
            v.wait_ge(step, 3)
            nc.vector.tensor_tensor_scan(top[:, ::-1], link[:, PARTS:0:-1], work[:, ::-1], -FAR, ALU.add, ALU.max).then_inc(step, 1)
            v.wait_ge(step, 4)
            nc.vector.tensor_tensor(work[:, :], peak[:, :], top[:, :], ALU.subtract).then_inc(step, 1)
            nc.vector.tensor_scalar(link[0:1, 0:PARTS], joined[0:1, 1:PARTS + 1], -1.0, 1.0, ALU.mult, ALU.add).then_inc(idx, 1)
            v.wait_ge(idx, 1)
            nc.vector.tensor_tensor(node_row[:, :], node_row[:, :], link[0:1, 0:PARTS], ALU.mult).then_inc(idx, 1)
            v.wait_ge(idx, 2)
            nc.vector.tensor_scalar(link[0:1, 0:PARTS], node_row[:, :], 0.0, 8192.0, ALU.is_equal, ALU.mult).then_inc(idx, 1)
            v.wait_ge(idx, 3)
            nc.vector.scalar_tensor_tensor(out=node_row[:, :], in0=node_row[:, :], scalar=-1.0, in1=link[0:1, 0:PARTS],
                                           op0=ALU.add, op1=ALU.add).then_inc(idx, 1)
            v.wait_ge(expd, 1)
            nc.vector.tensor_tensor(work[:, :], side[0:H, 0:PARTS], peak[:, :], ALU.mult).then_inc(step, 1)
            v.wait_ge(step, 6)
            nc.vector.tensor_tensor_scan(top[:, :], joined[0:H, 0:PARTS], work[:, :], 0.0, ALU.mult, ALU.add).then_inc(step, 1)
            v.wait_ge(step, 7)
            nc.vector.tensor_scalar(top[:, :], top[:, :], 1e-30, None, ALU.max).then_inc(step, 1)
            v.wait_ge(step, 8)
            nc.vector.reciprocal(work[:, :], top[:, :]).then_inc(step, 1)
            for b in range(NB):
                cols = slice(b * BLK, (b + 1) * BLK)
                for k in range(KH):
                    n = b * KH + k
                    part, carry = sums[:, k, cols], 0.0 if b == 0 else carried[:, k, b - 1:b]
                    v.wait_ge(wide, 2 * n + 1)
                    nc.vector.tensor_tensor(part, part, wide_ps[2 * (n % 2)][:, :], ALU.mult).then_inc(summed, 1)
                    v.wait_ge(summed, 3 * n + 1)
                    nc.vector.tensor_tensor_scan(part, joined[:, cols], part, carry, ALU.mult, ALU.add).then_inc(summed, 1)
                    v.wait_ge(wide, 2 * n + 2)
                    v.wait_ge(summed, 3 * n + 2)
                    nc.vector.tensor_copy(carried[:, k, b:b + 1], part[:, BLK - 1:BLK]).then_inc(carry_kept, 1)
                    v.wait_ge(carry_kept, n + 1)
                    nc.vector.tensor_tensor(part, part, wide_ps[2 * (n % 2) + 1][:, :], ALU.mult).then_inc(summed, 1)
            v.wait_ge(idx_t, 1)
            nc.vector.tensor_copy(index[:, :], index_ps[:, 0:PT]).then_inc(indexed, 1)

        @block.gpsimd
        def _(pool):
            pool.wait_ge(indexed, 1)
            for t in range(PT):
                pool.wait_ge(out_copied, t + 1)
                nc.gpsimd.indirect_dma_start(
                    out_rows, bass.IndirectOffsetOnAxis(ap=index[:, t:t + 1], axis=0), rows[:, t % 4, :], None,
                    bounds_check=N - 1, oob_is_err=False).then_inc(stored[t % 4], 16)
            for i in range(4):
                pool.wait_ge(stored[i], 16 * (PT // 4))


def residual_norm(nc, ins, keep, scratch, layer, add, bias):
    with Phase(nc) as ctx:
        def sb(name, shape, dt):
            return ctx.enter_context(nc.sbuf_tensor(f"n{layer}_" + name, shape, dt))
        more = sb("more", [P, NT, D], F32) if add is not None else None
        bias_all = sb("bias_all", [P, D], F32)
        stats = sb("stats", [P, NT, 6], F32)
        mean_var = sb("mean_var", [P, NT, 2], F32)
        std = sb("std", [P, NT], F32)
        x = keep["x"]
        loaded, summed, stat, aggr, rooted, inv, normed = sems(
            nc, ctx, *(f"n{layer}_" + n for n in ("loaded", "summed", "stat", "aggr", "rooted", "inv", "normed")))
        block = ctx.enter_context(nc.Block(f"norm{layer}"))

        @block.sync
        def _(sp):
            if add is not None:
                sp.dma_start(more[:, :, :], add.rearrange("(t p) d -> p t d", p=P)).then_inc(loaded, 16)
            if bias is not None:
                of = ins[bias]
                sp.dma_start(bias_all[:, :], bass.AP(tensor=of.tensor, offset=of.offset,
                                                     ap=[[0, P]] + [list(a) for a in of.ap])).then_inc(loaded, 16)

        @block.vector
        def _(v):
            if add is not None:
                v.wait_ge(loaded, 16 if bias is None else 32)
                nc.vector.tensor_tensor(x[:, :, :], x[:, :, :], more[:, :, :], ALU.add).then_inc(summed, 1)
                v.wait_ge(summed, 1)
            if bias is not None:
                nc.vector.tensor_tensor(x[:, :, :], x[:, :, :], bias_all[:, :].unsqueeze(1).to_broadcast([P, NT, D]),
                                        ALU.add).then_inc(summed, 1)
                v.wait_ge(summed, 2)
            for t in range(NT):
                nc.vector.bn_stats(stats[:, t, :], x[:, t, :]).then_inc(stat, 1)
            v.wait_ge(stat, NT)
            for t in range(NT):
                nc.vector.bn_aggr(mean_var[:, t, :], stats[:, t, :]).then_inc(aggr, 1)
            v.wait_ge(aggr, NT)
            nc.vector.tensor_scalar(std[:, :], mean_var[:, :, 1], EPS, None, ALU.add).then_inc(inv, 1)
            v.wait_ge(rooted, 1)
            nc.vector.reciprocal(std[:, :], std[:, :]).then_inc(inv, 1)
            v.wait_ge(inv, 2)
            for t in range(NT):
                nc.vector.tensor_scalar(x[:, t, :], x[:, t, :], mean_var[:, t, 0:1], std[:, t:t + 1],
                                        ALU.subtract, ALU.mult).then_inc(normed, 1)

        @block.scalar
        def _(act):
            act.wait_ge(inv, 1)
            nc.scalar.activation(std[:, :], std[:, :], ACT.Sqrt).then_inc(rooted, 1)


def store_x(nc, keep, out):
    with Phase(nc) as ctx:
        stored, = sems(nc, ctx, "out_stored")
        block = ctx.enter_context(nc.Block("store"))

        @block.sync
        def _(sp):
            full = N // P
            sp.dma_start(out[0:full * P, :].rearrange("(t p) d -> p t d", p=P), keep["x"][:, 0:full, :]).then_inc(stored, 16)
            sp.dma_start(out[full * P:N, :], keep["x"][0:N - full * P, full, :]).then_inc(stored, 16)
            sp.wait_ge(stored, 32)


def tables_layer1(nc, ins, keep, scratch):
    HEADS4, DH = 4, D // 4
    WIDE = D + 2 * H
    with Phase(nc) as ctx:
        def sb(name, shape, dt):
            return ctx.enter_context(nc.sbuf_tensor("t1_" + name, shape, dt))
        x_t = sb("x_t", [P, KH, NP], F32)
        w_attn = sb("w_attn", [P, KH, D], F32)
        a_cols = sb("a_cols", [P, KH, 2 * H], F32)
        w_all = sb("w_all", [P, KH, WIDE], F32)
        out = sb("out", [P, 4, WIDE], F32)
        ps = [ctx.enter_context(nc.psum_tensor(f"t1_ps{i}", [P, BLK], F32)) for i in range(4)]
        fold_ps = ctx.enter_context(nc.psum_tensor("t1_fold_ps", [P, KH, 2 * H], F32))
        cleared, w_in, a_in, turned, copied, folded, fold_copied, summed, made = sems(
            nc, ctx, *("t1_" + n for n in ("cleared", "w_in", "a_in", "turned", "copied", "folded", "fold_copied",
                                           "summed", "made")))
        stored = sems(nc, ctx, *(f"t1_stored{i}" for i in range(4)))
        block = ctx.enter_context(nc.Block("tables1"))

        @block.sync
        def _(sp):
            sp.dma_start(w_attn[:, :, :], ins["L1_gnn_W_attn"].rearrange("(k p) i -> p k i", p=P)).then_inc(w_in, 16)
            sp.dma_start(w_all[:, :, 0:D], ins["L1_gnn_W_lin_t"].rearrange("(k p) o -> p k o", p=P)).then_inc(w_in, 16)
            sp.wait_ge(cleared, 1)
            a = ins["L1_gnn_a"]
            for h in range(HEADS4):
                rows = slice(h * DH % P, h * DH % P + DH)
                for side in range(2):
                    for twin in range(2):
                        col = side * H + 2 * h + twin
                        sp.dma_start(a_cols[rows, h * DH // P, col:col + 1],
                                     a[h, side * DH:(side + 1) * DH].rearrange("(d o) -> d o", o=1)).then_inc(a_in, 16)
            for t in range(NT):
                sp.wait_ge(made, t + 1)
                sp.dma_start(scratch["val"][t * P:(t + 1) * P, :], out[:, t % 4, 0:D + H]).then_inc(stored[t % 4], 16)
                sp.dma_start(scratch["alpha"][t * P:(t + 1) * P, :], out[:, t % 4, D + H:WIDE]).then_inc(stored[t % 4], 16)
            for i in range(4):
                sp.wait_ge(stored[i], 32 * len(range(i, NT, 4)))

        @block.tensor
        def _(pe):
            for t in range(NT):
                if t >= 4:
                    pe.wait_ge(copied, t - 3)
                for k in range(KH):
                    mm = nc.tensor.transpose(ps[t % 4][:, k * P:(k + 1) * P], keep["x"][:, t, k * P:(k + 1) * P], keep["ident"][:, :])
                mm.then_inc(turned, 1)
            pe.wait_ge(w_in, 32)
            pe.wait_ge(a_in, 256)
            for k_in in range(KH):
                for k in range(KH):
                    mm = nc.tensor.matmul(fold_ps[:, k_in, :], w_attn[:, k, k_in * P:(k_in + 1) * P], a_cols[:, k, :],
                                          start=(k == 0), stop=(k == KH - 1))
            mm.then_inc(folded, 1)
            pe.wait_ge(fold_copied, 1)
            pe.wait_ge(copied, NT)
            for t in range(NT):
                if t >= 4:
                    pe.wait_ge(made, t - 3)
                for k in range(KH):
                    mm = nc.tensor.matmul(ps[t % 4][:, 0:WIDE], x_t[:, k, t * P:(t + 1) * P], w_all[:, k, :],
                                          start=(k == 0), stop=(k == KH - 1))
                mm.then_inc(summed, 1)

        @block.vector
        def _(v):
            nc.vector.memset(a_cols[:, :, :], 0.0).then_inc(cleared, 1)
            for t in range(NT):
                v.wait_ge(turned, t + 1)
                nc.vector.tensor_copy(x_t[:, :, t * P:(t + 1) * P], ps[t % 4][:, 0:D].rearrange("p (k n) -> p k n", k=KH)).then_inc(copied, 1)
            v.wait_ge(folded, 1)
            nc.vector.tensor_copy(w_all[:, :, D:WIDE], fold_ps[:, :, :]).then_inc(fold_copied, 1)

        @block.scalar
        def _(act):
            for t in range(NT):
                act.wait_ge(summed, t + 1)
                if t >= 4:
                    act.wait_ge(stored[t % 4], 32 * (t // 4))
                nc.scalar.activation(out[:, t % 4, :], ps[t % 4][:, 0:WIDE], ACT.Copy).then_inc(made, 1)


def turn_x(nc, keep, state, name):
    with Phase(nc) as ctx:
        ps = [ctx.enter_context(nc.psum_tensor(f"{name}_ps{i}", [P, BLK], F32)) for i in range(4)]
        turned, copied = sems(nc, ctx, name + "_turned", name + "_copied")
        block = ctx.enter_context(nc.Block(name))

        @block.tensor
        def _(pe):
            for t in range(NT):
                if t >= 4:
                    pe.wait_ge(copied, t - 3)
                for k in range(KH):
                    mm = nc.tensor.transpose(ps[t % 4][:, k * P:(k + 1) * P], keep["x"][:, t, k * P:(k + 1) * P], keep["ident"][:, :])
                mm.then_inc(turned, 1)

        @block.vector
        def _(v):
            for t in range(NT):
                v.wait_ge(turned, t + 1)
                nc.vector.tensor_copy(state["h_t"][:, :, t * P:(t + 1) * P],
                                      ps[t % 4][:, 0:D].rearrange("p (k n) -> p k n", k=KH)).then_inc(copied, 1)


def add_turned(nc, keep, state, name):
    with Phase(nc) as ctx:
        ps = [ctx.enter_context(nc.psum_tensor(f"{name}_ps{i}", [P, BLK], F32)) for i in range(4)]
        turned, added = sems(nc, ctx, name + "_turned", name + "_added")
        block = ctx.enter_context(nc.Block(name))

        @block.tensor
        def _(pe):
            for t in range(NT):
                if t >= 4:
                    pe.wait_ge(added, t - 3)
                for k in range(KH):
                    mm = nc.tensor.transpose(ps[t % 4][:, k * P:(k + 1) * P], state["h_t"][:, k, t * P:(t + 1) * P], keep["ident"][:, :])
                mm.then_inc(turned, 1)

        @block.vector
        def _(v):
            for t in range(NT):
                v.wait_ge(turned, t + 1)
                nc.vector.tensor_tensor(keep["x"][:, t, :], keep["x"][:, t, :], ps[t % 4][:, 0:D], ALU.add).then_inc(added, 1)


def split_x(nc, keep, state, name, relu):
    with Phase(nc) as ctx:
        scaled = ctx.enter_context(nc.sbuf_tensor(name + "_scaled", [P, 2, D], F32))
        made, high_done, low_done = sems(nc, ctx, *(name + n for n in ("_made", "_high_done", "_low_done")))
        block = ctx.enter_context(nc.Block(name))

        @block.vector
        def _(v):
            for t in range(NT):
                nc.vector.tensor_scalar(scaled[:, t % 2, :], keep["x"][:, t, :], 0.0 if relu else 1.0, FS,
                                        ALU.max if relu else ALU.mult, ALU.mult).then_inc(made, 1)
                v.wait_ge(high_done, t + 1)
                nc.vector.tensor_tensor(state["low"][:, t, :], scaled[:, t % 2, :], state["high"][:, t, :], ALU.subtract).then_inc(low_done, 1)

        @block.scalar
        def _(act):
            for t in range(NT):
                act.wait_ge(made, t + 1)
                nc.scalar.activation(state["high"][:, t, :], scaled[:, t % 2, :], ACT.Copy).then_inc(high_done, 1)


def split_h(nc, keep, state, name):
    with Phase(nc) as ctx:
        ps = [ctx.enter_context(nc.psum_tensor(f"{name}_ps{i}", [P, BLK], F32)) for i in range(4)]
        turned, high_done, low_done = sems(nc, ctx, *(name + n for n in ("_turned", "_high_done", "_low_done")))
        block = ctx.enter_context(nc.Block(name))

        @block.tensor
        def _(pe):
            for t in range(NT):
                if t >= 4:
                    pe.wait_ge(low_done, t - 3)
                for k in range(KH):
                    mm = nc.tensor.transpose(ps[t % 4][:, k * P:(k + 1) * P], state["h_t"][:, k, t * P:(t + 1) * P], keep["ident"][:, :])
                mm.then_inc(turned, 1)

        @block.scalar
        def _(act):
            for t in range(NT):
                act.wait_ge(turned, t + 1)
                nc.scalar.activation(state["high"][:, t, :], ps[t % 4][:, 0:D], ACT.Copy, scale=FS).then_inc(high_done, 1)

        @block.vector
        def _(v):
            for t in range(NT):
                v.wait_ge(high_done, t + 1)
                nc.vector.scalar_tensor_tensor(out=state["low"][:, t, :], in0=ps[t % 4][:, 0:D], scalar=FS,
                                               in1=state["high"][:, t, :], op0=ALU.mult, op1=ALU.subtract).then_inc(low_done, 1)


def aggregate(nc, keep, scratch, state, name, kind, own_scale=None):
    halves = 1 if kind == "degree" else KH
    with Phase(nc) as ctx:
        ps = [[ctx.enter_context(nc.psum_tensor(f"{name}_ps{i}_{j}", [P, BLK], F32)) for j in range(4)] for i in range(2)]
        counts = ctx.enter_context(nc.sbuf_tensor(name + "_counts", [P, 2, AN], F32)) if kind == "degree" else None
        slab = state["slab"]
        slab_used, scaled, clipped = sems(nc, ctx, *(name + n for n in ("_slab_used", "_scaled", "_clipped")))
        slab_in = sems(nc, ctx, *(f"{name}_slab_in{i}" for i in range(NSLAB)))
        pass_read = sems(nc, ctx, *(f"{name}_pass_read{i}" for i in range(2)))
        block = ctx.enter_context(nc.Block(name))
        adj = scratch["adj"].rearrange("(s k p a c) o -> s a p k (c o)", s=NSLAB, k=SLAB, p=P, a=APASS)

        @block.sync
        def _(sp):
            for a in range(APASS):
                for s in range(NSLAB):
                    if a:
                        sp.wait_ge(slab_used, NSLAB * (a - 1) + s + 1)
                    sp.dma_start(slab[:, s, :, :], adj[s, a]).then_inc(slab_in[s], 16)

        @block.tensor
        def _(pe):
            parts = ("ones16",) if kind == "degree" else ("high", "low")
            for b in range(2):
                pe.sem_inc(pass_read[b], 1)
            with pe.Fori(0, APASS // 2) as it:
                for b in range(2):
                    pe.wait_ge(pass_read[b], 2 * halves * it + 1)
                    for s in range(NSLAB):
                        pe.wait_ge(slab_in[s], 32 * it + 16 * b + 16)
                        for k in range(SLAB):
                            t = s * SLAB + k
                            for m in range(halves):
                                for i, part in enumerate(parts):
                                    left = state[part][:, :] if kind == "degree" else state[part][:, t, m * P:(m + 1) * P]
                                    for n in range(2):
                                        mm = nc.tensor.matmul(ps[b][2 * m + n][:, 0:AN], left, slab[:, s, k, n * AN:(n + 1) * AN],
                                                              start=(t == 0 and i == 0), stop=(t == NT - 1 and i == len(parts) - 1))
                        mm.then_inc(slab_used, 1)

        @block.scalar
        def _(act):
            if kind == "gin":
                nc.scalar.activation(state["z_t"][:, :, :], state["h_t"][:, :, 0:AW], ACT.Copy, scale=own_scale).then_inc(scaled, 1)

        @block.vector
        def _(v):
            if kind == "gin":
                v.wait_ge(scaled, 1)
            for a in range(APASS):
                v.wait_ge(slab_used, NSLAB * (a + 1))
                for m in range(halves):
                    for n in range(2):
                        cols = slice(a * ACOLS + n * AN, a * ACOLS + (n + 1) * AN)
                        bank = ps[a % 2][2 * m + n][:, 0:AN]
                        if kind == "gin":
                            z = state["z_t"][:, m, cols]
                            nc.vector.scalar_tensor_tensor(out=z, in0=bank, scalar=1.0 / FS, in1=z,
                                                           op0=ALU.mult, op1=ALU.add).then_inc(pass_read[a % 2], 1)
                        elif kind == "mean":
                            nc.vector.tensor_tensor(state["z_t"][:, m, cols], bank, state["inv_degree"][:, cols],
                                                    ALU.mult).then_inc(pass_read[a % 2], 1)
                        else:
                            nc.vector.tensor_scalar(counts[:, n, :], bank, 1.0, FS, ALU.max, ALU.mult).then_inc(pass_read[a % 2], 1)
                            v.wait_ge(pass_read[a % 2], 2 * (a // 2) + n + 2)
                            nc.vector.reciprocal(state["inv_degree"][:, cols], counts[:, n, :]).then_inc(clipped, 1)


def project(nc, keep, state, name, terms, bias, func, target, norm=None):
    NBLK = 2 * APASS
    with Phase(nc) as ctx:
        def sb(n, shape, dt):
            return ctx.enter_context(nc.sbuf_tensor(name + n, shape, dt))
        ps = [[ctx.enter_context(nc.psum_tensor(f"{name}_ps{i}_{j}", [P, BLK], F32)) for j in range(KH)] for i in range(2)]
        stats = sb("_stats", [P, KH, NBLK, 6], F32)
        mean_var = sb("_mean_var", [P, KH, 2], F32)
        std = sb("_std", [P, KH], F32)
        gain = sb("_gain", [P, KH], F32)
        shift = sb("_shift", [P, KH], F32)
        summed, moved, stat, aggr, step, rooted, normed = sems(
            nc, ctx, *(name + n for n in ("_summed", "_moved", "_stat", "_aggr", "_step", "_rooted", "_normed")))
        block = ctx.enter_context(nc.Block(name))

        def cols(b):
            return slice(b * AN, (b + 1) * AN)

        @block.tensor
        def _(pe):
            for b in range(NBLK):
                if b >= 2:
                    pe.wait_ge(moved, KH * (b - 1))
                for m in range(KH):
                    for i, (src, w) in enumerate(terms):
                        for k in range(KH):
                            mm = nc.tensor.matmul(ps[b % 2][m][:, 0:AN], w[:, k, m * P:(m + 1) * P], src[:, k, cols(b)],
                                                  start=(i == 0 and k == 0), stop=(i == len(terms) - 1 and k == KH - 1))
                mm.then_inc(summed, 1)

        @block.scalar
        def _(act):
            for b in range(NBLK):
                act.wait_ge(summed, b + 1)
                for m in range(KH):
                    nc.scalar.activation(target[:, m, cols(b)], ps[b % 2][m][:, 0:AN], func, bias=bias[:, m:m + 1]).then_inc(moved, 1)
            if norm:
                act.wait_ge(step, 1)
                nc.scalar.activation(std[:, :], std[:, :], ACT.Sqrt).then_inc(rooted, 1)
                act.wait_ge(step, 5)
                for m in range(KH):
                    nc.scalar.activation(norm[3][:, m, 0:AW], target[:, m, 0:AW], ACT.Relu if norm[2] else ACT.Identity,
                                         bias=shift[:, m:m + 1], scale=gain[:, m:m + 1]).then_inc(normed, 1)

        @block.vector
        def _(v):
            if norm:
                for b in range(NBLK):
                    v.wait_ge(moved, KH * (b + 1))
                    for m in range(KH):
                        nc.vector.bn_stats(stats[:, m, b, :], target[:, m, b * AN:min((b + 1) * AN, N)]).then_inc(stat, 1)
                v.wait_ge(stat, KH * NBLK)
                for m in range(KH):
                    nc.vector.bn_aggr(mean_var[:, m, :], stats[:, m, :, :].rearrange("p b s -> p (b s)")).then_inc(aggr, 1)
                v.wait_ge(aggr, KH)
                nc.vector.tensor_scalar(std[:, :], mean_var[:, :, 1], EPS, None, ALU.add).then_inc(step, 1)
                v.wait_ge(step, 1)
                v.wait_ge(rooted, 1)
                nc.vector.reciprocal(std[:, :], std[:, :]).then_inc(step, 1)
                v.wait_ge(step, 2)
                nc.vector.tensor_tensor(gain[:, :], std[:, :], norm[0], ALU.mult).then_inc(step, 1)
                v.wait_ge(step, 3)
                nc.vector.tensor_tensor(shift[:, :], mean_var[:, :, 0], gain[:, :], ALU.mult).then_inc(step, 1)
                v.wait_ge(step, 4)
                nc.vector.tensor_tensor(shift[:, :], norm[1], shift[:, :], ALU.subtract).then_inc(step, 1)


GIN_LAYERS = 5
SAGE_LAYERS = 3
GIN_COLUMNS = ("L2_gnn_b1", "L2_gnn_g1", "L2_gnn_bt1", "L2_gnn_b2", "L2_gnn_bn_g", "L2_gnn_bn_b")


def load_gin(nc, ins, state, w, columns, own):
    with Phase(nc) as ctx:
        w_in, eps_in, ready, cleared = sems(nc, ctx, "lg_w_in", "lg_eps_in", "lg_ready", "lg_cleared")
        block = ctx.enter_context(nc.Block("load_gin"))

        @block.sync
        def _(sp):
            eps = ins["L2_gnn_eps"]
            sp.dma_start(own[:, :], bass.AP(tensor=eps.tensor, offset=eps.offset,
                                            ap=[[0, P]] + [list(a) for a in eps.ap])).then_inc(eps_in, 16)
            for i, name in enumerate(("L2_gnn_W1", "L2_gnn_W2")):
                for l in range(GIN_LAYERS):
                    sp.dma_start(w[:, 2 * l + i, :, :], ins[name][l].rearrange("(k p) o -> p k o", p=P)).then_inc(w_in, 16)
            sp.dma_start(columns[:, :, :, :], ins["gin_columns"]).then_inc(w_in, 16)
            sp.wait_ge(w_in, 16 * (2 * GIN_LAYERS + 1))

        @block.vector
        def _(v):
            v.wait_ge(eps_in, 16)
            nc.vector.tensor_scalar(own[:, :], own[:, :], 1.0, None, ALU.add).then_inc(ready, 1)
            nc.vector.memset(state["ones16"][:, :], 1.0).then_inc(cleared, 1)
            nc.vector.memset(state["h_t"][:, :, :], 0.0).then_inc(cleared, 1)


def load_sage(nc, ins, w, bias):
    with Phase(nc) as ctx:
        w_in, = sems(nc, ctx, "ls_w_in")
        block = ctx.enter_context(nc.Block("load_sage"))

        @block.sync
        def _(sp):
            for l in range(SAGE_LAYERS):
                for i, side in enumerate("lr"):
                    sp.dma_start(w[:, 2 * l + i, :, :],
                                 ins[f"L3_gnn_W{l + 1}{side}_t"].rearrange("(k p) o -> p k o", p=P)).then_inc(w_in, 16)
            sp.dma_start(bias[:, :, :], ins["sage_columns"]).then_inc(w_in, 16)
            sp.wait_ge(w_in, 16 * (2 * SAGE_LAYERS + 1))


PLAIN = ("L0_gnn_relation_emb", "L0_gnn_bq", "L0_gnn_bk", "L0_gnn_bv", "L0_gnn_bo", "L1_gnn_W_attn", "L1_gnn_a",
         "L2_gnn_W1", "L2_gnn_W2", "L2_gnn_eps")
SAGE_COLUMNS = ("L3_gnn_b1l", "L3_gnn_b2l", "L3_gnn_b3l")
TURNED = ("L1_gnn_W_lin", "L3_gnn_W1l", "L3_gnn_W1r", "L3_gnn_W2l", "L3_gnn_W2r", "L3_gnn_W3l", "L3_gnn_W3r")


def gnn_kernel(nc, ins, out):
    with ExitStack() as ctx:
        def sb(name, shape, dt):
            return ctx.enter_context(nc.sbuf_tensor(name, shape, dt))
        scratch = {
            "adj": nc.dram_tensor("adj", [NP * AW, 1], F16, kind="Internal").ap(),
            "vk": nc.dram_tensor("vk", [NP, 2 * D], F32, kind="Internal").ap(),
            "q": nc.dram_tensor("q", [NP, D], F32, kind="Internal").ap(),
            "val": nc.dram_tensor("val", [NP, D + H], F32, kind="Internal").ap(),
            "alpha": nc.dram_tensor("alpha", [NP, H], F32, kind="Internal").ap(),
            "out0": nc.dram_tensor("out0", [NP, D], F32, kind="Internal").ap(),
            "out1": nc.dram_tensor("out1", [NP, D], F32, kind="Internal").ap(),
        }
        keep = {
            "x": sb("x", [P, NT, D], F32),
            "ident": sb("ident", [P, P], F32),
            "ones": sb("ones", [P, P], F32),
        }
        with ExitStack() as edge_ctx:
            def esb(name, shape, dt):
                return edge_ctx.enter_context(nc.sbuf_tensor(name, shape, dt))
            keep.update({
                "hsel": esb("hsel", [H, D], F32), "iota": esb("iota", [P, P], F32),
                "src": esb("src", [P, C], I32), "dst": esb("dst", [P, C], I32), "cell": esb("cell", [P, C], I32),
                "first": esb("first", [P, C], F32), "slot": esb("slot", [P, C], F32), "node": esb("node", [P, C], F32),
                "offset": esb("offset", [1, C], I32), "link": esb("link", [G * H, NG, LINK], BF16),
                "link_back": esb("link_back", [G * H, NG, P], BF16),
            })
            prepare_edges(nc, ins, keep, scratch)
            tables_layer0(nc, ins, keep, scratch)
            with ExitStack() as part_ctx:
                keep["sums"] = part_ctx.enter_context(nc.sbuf_tensor("sums0", [P, KH, PBUF], F32))
                keep["side"] = part_ctx.enter_context(nc.sbuf_tensor("side0", [SMALL, PBUF], F32))
                attend_edges(nc, keep, scratch, 0, scratch["vk"], scratch["q"], 2 * D, D, float(DK) ** -0.5, True)
                merge_parts(nc, ins, keep, scratch, 0, "wo_t", scratch["out0"], float(DK) ** -0.5)
            residual_norm(nc, ins, keep, scratch, 0, scratch["out0"], "L0_gnn_bo")
            tables_layer1(nc, ins, keep, scratch)
            with ExitStack() as part_ctx:
                keep["sums"] = part_ctx.enter_context(nc.sbuf_tensor("sums1", [P, KH, PBUF], F32))
                keep["side"] = part_ctx.enter_context(nc.sbuf_tensor("side1", [SMALL, PBUF], F32))
                attend_edges(nc, keep, scratch, 1, scratch["val"], scratch["alpha"], D + H, H, 1.0, False)
                merge_parts(nc, ins, keep, scratch, 1, None, scratch["out1"], 1.0)
            residual_norm(nc, ins, keep, scratch, 1, scratch["out1"], None)
        state = {
            "h_t": sb("h_t", [P, KH, NP], F32), "z_t": sb("z_t", [P, KH, AW], F32),
            "high": sb("high", [P, NT, D], F16), "low": sb("low", [P, NT, D], F16),
            "slab": sb("slab", [P, NSLAB, SLAB, ACOLS], F16), "ones16": sb("ones16", [P, P], F16),
        }
        with ExitStack() as gin_ctx:
            w = gin_ctx.enter_context(nc.sbuf_tensor("gin_w", [P, 2 * GIN_LAYERS, KH, D], F32))
            columns = gin_ctx.enter_context(nc.sbuf_tensor("gin_columns", [P, len(GIN_COLUMNS), GIN_LAYERS, KH], F32))
            own = gin_ctx.enter_context(nc.sbuf_tensor("gin_own", [P, GIN_LAYERS], F32))
            load_gin(nc, ins, state, w, columns, own)
            turn_x(nc, keep, state, "turn2")
            split_x(nc, keep, state, "split2", True)
            h_t, z_t = state["h_t"], state["z_t"]
            for l in range(GIN_LAYERS):
                if l:
                    split_h(nc, keep, state, f"gsplit{l}")
                b1, g1, bt1, b2, bn_g, bn_b = (columns[:, i, l, :] for i in range(len(GIN_COLUMNS)))
                aggregate(nc, keep, scratch, state, f"gagg{l}", "gin", own[:, l:l + 1])
                project(nc, keep, state, f"gone{l}", [(z_t, w[:, 2 * l])], b1, ACT.Identity, z_t, (g1, bt1, True, z_t))
                project(nc, keep, state, f"gtwo{l}", [(z_t, w[:, 2 * l + 1])], b2, ACT.Identity, z_t,
                        (bn_g, bn_b, l < GIN_LAYERS - 1, h_t))
            add_turned(nc, keep, state, "add2")
            residual_norm(nc, ins, keep, scratch, 2, None, None)
        with ExitStack() as sage_ctx:
            w = sage_ctx.enter_context(nc.sbuf_tensor("sage_w", [P, 2 * SAGE_LAYERS, KH, D], F32))
            bias = sage_ctx.enter_context(nc.sbuf_tensor("sage_bias", [P, SAGE_LAYERS, KH], F32))
            state["inv_degree"] = sage_ctx.enter_context(nc.sbuf_tensor("inv_degree", [P, AW], F32))
            load_sage(nc, ins, w, bias)
            turn_x(nc, keep, state, "turn3")
            split_x(nc, keep, state, "split3", False)
            aggregate(nc, keep, scratch, state, "degree", "degree")
            for l in range(SAGE_LAYERS):
                if l:
                    split_h(nc, keep, state, f"ssplit{l}")
                aggregate(nc, keep, scratch, state, f"sagg{l}", "mean")
                project(nc, keep, state, f"sone{l}", [(z_t, w[:, 2 * l]), (h_t, w[:, 2 * l + 1])], bias[:, l, :],
                        ACT.Relu if l < SAGE_LAYERS - 1 else ACT.Identity, h_t)
            add_turned(nc, keep, state, "add3")
            residual_norm(nc, ins, keep, scratch, 3, None, None)
        store_x(nc, keep, out)


def kernel(**inputs):
    import numpy as _np
    import concourse.bacc as _bacc
    from concourse import mybir as _mybir
    from concourse.bass_utils import run_bass_kernel_spmd as _run

    def padded_t(a):
        return _np.pad(_np.asarray(a).T, ((0, 0), (0, NP - N)))

    x = _np.asarray(inputs["x"])
    text = _np.concatenate([_np.asarray(inputs["L0_gnn_user_text_embs"]), _np.asarray(inputs["L0_gnn_item_text_embs"])])
    src = _np.pad(_np.asarray(inputs["src"]), (0, C * P - E))
    dst = _np.pad(_np.asarray(inputs["dst"]), (0, C * P - E), constant_values=N)
    chunks = dst.reshape(C, P)
    arrays = {
        "x": _np.pad(x, ((0, NP - N), (0, 0))), "x_t": padded_t(x), "text_t": padded_t(text),
        "src_col": src.reshape(C, P).T, "dst_col": chunks.T,
        "dst_prev": _np.pad(chunks[:, :-1], ((0, 0), (1, 0)), constant_values=-1).T,
        "src_row": src.reshape(P, C), "dst_row": dst.reshape(P, C), "dst_chunk": chunks,
        "wq_t": _np.asarray(inputs["L0_gnn_Wq"]).T, "wk_t": _np.asarray(inputs["L0_gnn_Wk"]).T,
        "wv_t": _np.asarray(inputs["L0_gnn_Wv"]).T, "wo_t": _np.asarray(inputs["L0_gnn_Wo"]).T,
    }
    for name, rows in (("gin_columns", GIN_COLUMNS), ("sage_columns", SAGE_COLUMNS)):
        a = _np.stack([_np.asarray(inputs[r]) for r in rows])
        arrays[name] = _np.moveaxis(a.reshape(*a.shape[:-1], KH, P), -1, 0)
    for name in PLAIN:
        arrays[name] = _np.asarray(inputs[name])
    for name in TURNED:
        arrays[name + "_t"] = _np.asarray(inputs[name]).T
    arrays = {"in_" + k: _np.ascontiguousarray(a) for k, a in arrays.items()}
    nc = _bacc.Bacc("TRN2", target_bir_lowering=False, num_devices=1)
    ins = {k[3:]: nc.dram_tensor(k, a.shape, _mybir.dt.from_np(a.dtype), kind="ExternalInput").ap() for k, a in arrays.items()}
    out = nc.dram_tensor("out_x", (N, D), _mybir.dt.float32, kind="ExternalOutput").ap()
    gnn_kernel(nc, ins, out)
    r = _run(nc, [arrays], core_ids=[0])
    return r.results[0]["out_x"]
```

```python
from contextlib import ExitStack

import concourse.bass as bass
from concourse import mybir

F32 = mybir.dt.float32
F16 = mybir.dt.float16
BF16 = mybir.dt.bfloat16
I32 = mybir.dt.int32
ALU = mybir.AluOpType
ACT = mybir.ActivationFunctionType
AX_X = mybir.AxisListType.X

P = 128
N = 3125
D = 256
E = 53125
KH = D // P
NT = -(-N // P)
NP = NT * P
H = 8
DK = D // H
RING = 4
C = 416
G = 8
NG = C // G
LINK = P + 1
PT = 28
PARTS = PT * P
PBUF = PARTS + P
BLK = 512
NB = PARTS // BLK
FAR = 1.0e30
SMALL = 96
COL_MAX = 32
COL_NODE = 64
EPS = 1e-5

APASS = 4
ACOLS = 782
AW = APASS * ACOLS
AN = ACOLS // 2
SLAB = 5
NSLAB = NT // SLAB
FS = 16.0


class Phase(ExitStack):

    def __init__(self, nc):
        super().__init__()
        self.nc, self.used = nc, []
        self.callback(self.clear)

    def clear(self):
        self.nc.clear_and_free_semaphores(self.used)
        self.nc.all_engine_barrier()


def sems(nc, ctx, *names):
    made = [nc.alloc_semaphore(name=n) for n in names]
    ctx.used += made
    return made


def prepare_edges(nc, ins, keep, scratch):
    with Phase(nc) as ctx:
        def sb(name, shape, dt):
            return ctx.enter_context(nc.sbuf_tensor("pe_" + name, shape, dt))
        link_in = sb("link_in", [G * H, NG, P], I32)
        same = sb("same", [G * H, NG, P], BF16)
        dst_f = sb("dst_f", [P, C], F32)
        prev_f = sb("prev_f", [P, C], I32)
        src_rank = sb("src_rank", [P, C], I32)
        dst_rank = sb("dst_rank", [P, C], I32)
        cell = sb("cell", [P, C], F32)
        tri = sb("tri", [P, P], F32)
        zero16 = sb("zero16", [P, NP * AW // P // 8], F16)
        zeros = sb("zeros", [P, NT * D], F32)
        counts = sb("counts", [P, C + 1], F32)
        zrow = sb("zrow", [P, C], F32)
        part = sb("part", [P, C], F32)
        part_i = sb("part_i", [P, 3, C], I32)
        tile_of = sb("tile_of", [P, C], F32)
        row_of = sb("row_of", [P, C], F32)
        tile_ramp = sb("tile_ramp", [P, PT + 1], F32)
        is_row = sb("is_row", [P, 2, 2 * G, P], F32)
        is_tile = sb("is_tile", [P, 2, 2 * G, PT + 1], F32)
        node_ps = ctx.enter_context(nc.psum_tensor("pe_node_ps", [P, BLK], F32))
        rank_ps = ctx.enter_context(nc.psum_tensor("pe_rank_ps", [P, BLK], F32))
        num_ps = ctx.enter_context(nc.psum_tensor("pe_num_ps", [P, BLK], F32))
        loaded, links, zeroed, const, ramp, first, rank, offs, done, cells, lk, part_sem, spotted, placed = sems(
            nc, ctx, "pe_loaded", "pe_links", "pe_zeroed", "pe_const", "pe_ramp", "pe_first", "pe_rank",
            "pe_offs", "pe_done", "pe_cells", "pe_lk",
            "pe_part", "pe_spotted", "pe_placed")
        block = ctx.enter_context(nc.Block("prep"))

        @block.sync
        def _(sp):
            for to, of in ((keep["src"], ins["src_col"]), (keep["dst"], ins["dst_col"]), (prev_f, ins["dst_prev"]),
                           (src_rank, ins["src_row"]), (dst_rank, ins["dst_row"])):
                sp.dma_start(to[:, :], of).then_inc(loaded, 16)
            rows = ins["dst_chunk"].rearrange("(g j) e -> j g e", j=G)
            for j in range(G):
                wide = bass.AP(tensor=rows.tensor, offset=rows[j].offset, ap=[[0, H]] + [list(a) for a in rows[j].ap])
                sp.dma_start(link_in[j * H:(j + 1) * H, :, :], wide).then_inc(links, 16)
            sp.wait_ge(const, 5)
            adj = scratch["adj"].rearrange("(e p c) o -> e p (c o)", e=8, p=P)
            for k in range(8):
                sp.dma_start(adj[k], zero16[:, :]).then_inc(zeroed, 16)
            for name in ("out0", "out1"):
                sp.dma_start(scratch[name].rearrange("(p t) d -> p (t d)", p=P), zeros[:, :]).then_inc(zeroed, 16)
            sp.wait_ge(zeroed, 160)

        @block.gpsimd
        def _(pool):
            nc.gpsimd.memset(keep["ident"][:, :], 0.0).then_inc(const, 1)
            nc.gpsimd.memset(tri[:, :], 1.0).then_inc(const, 1)
            nc.gpsimd.memset(keep["hsel"][:, :], 1.0).then_inc(const, 1)
            pool.wait_ge(const, 5)
            nc.gpsimd.affine_select(out=keep["ident"][:, :], in_=keep["ident"][:, :], compare_op=ALU.not_equal,
                                    fill=1.0, base=0, pattern=[[-1, P]], channel_multiplier=1).then_inc(const, 1)
            nc.gpsimd.affine_select(out=tri[:, :], in_=tri[:, :], compare_op=ALU.is_ge,
                                    fill=0.0, base=0, pattern=[[1, P]], channel_multiplier=-1).then_inc(const, 1)
            nc.gpsimd.affine_select(out=keep["hsel"][:, :], in_=keep["hsel"][:, :], compare_op=ALU.is_ge,
                                    fill=0.0, base=0, pattern=[[1, D]], channel_multiplier=-DK).then_inc(const, 1)
            pool.wait_ge(const, 8)
            nc.gpsimd.affine_select(out=keep["hsel"][:, :], in_=keep["hsel"][:, :], compare_op=ALU.is_ge,
                                    fill=0.0, base=DK - 1, pattern=[[-1, D]], channel_multiplier=DK).then_inc(const, 1)
            nc.gpsimd.iota(keep["iota"][:, :], [[1, P]], base=0, channel_multiplier=0,
                           allow_small_or_imprecise_dtypes=True).then_inc(ramp, 1)
            nc.gpsimd.iota(tile_ramp[:, :], [[1, PT + 1]], base=0, channel_multiplier=0,
                           allow_small_or_imprecise_dtypes=True).then_inc(ramp, 1)

        @block.vector
        def _(v):
            nc.vector.memset(zero16[:, :], 0.0).then_inc(const, 1)
            nc.vector.memset(zeros[:, :], 0.0).then_inc(const, 1)
            nc.vector.memset(keep["ones"][:, :], 1.0).then_inc(rank, 1)
            nc.vector.memset(zrow[:, :], 0.0).then_inc(rank, 1)
            nc.vector.memset(counts[:, :], 0.0).then_inc(rank, 1)
            nc.vector.memset(keep["link"][:, :, :], 0.0).then_inc(lk, 1)
            v.wait_ge(loaded, 80)
            nc.vector.tensor_tensor(keep["first"][:, :], keep["dst"][:, :], prev_f[:, :], ALU.not_equal).then_inc(first, 1)
            nc.vector.tensor_scalar(dst_f[:, :], keep["dst"][:, :], 1.0, None, ALU.add).then_inc(first, 1)
            nc.vector.tensor_scalar(cell[:, :], src_rank[:, :], float(AW), None, ALU.mult).then_inc(cells, 1)
            v.wait_ge(cells, 1)
            nc.vector.tensor_tensor(keep["cell"][:, :], cell[:, :], dst_rank[:, :], ALU.add).then_inc(cells, 1)
            v.wait_ge(first, 2)
            nc.vector.tensor_tensor(keep["node"][:, :], dst_f[:, :], keep["first"][:, :], ALU.mult).then_inc(done, 1)
            v.wait_ge(rank, 5)
            nc.vector.tensor_scalar(keep["slot"][:, :], rank_ps[:, 0:C], -1.0, None, ALU.add).then_inc(done, 1)
            nc.vector.tensor_tensor_scan(counts[:, 1:C + 1], zrow[:, :], num_ps[:, 0:C], 0.0, ALU.add, ALU.add).then_inc(offs, 1)
            v.wait_ge(offs, 1)
            v.wait_ge(done, 2)
            nc.vector.tensor_copy(keep["offset"][:, :], counts[0:1, 0:C]).then_inc(done, 1)
            nc.vector.tensor_tensor(part_i[:, 0, :], keep["slot"][:, :], counts[:, 0:C], ALU.add).then_inc(part_sem, 1)
            v.wait_ge(part_sem, 1)
            nc.vector.tensor_scalar(part_i[:, 1, :], part_i[:, 0, :], 7, None, ALU.arith_shift_right).then_inc(part_sem, 1)
            nc.vector.tensor_scalar(part_i[:, 2, :], part_i[:, 0, :], P - 1, None, ALU.bitwise_and).then_inc(part_sem, 1)
            v.wait_ge(part_sem, 3)
            nc.vector.tensor_copy(tile_of[:, :], part_i[:, 1, :]).then_inc(part_sem, 1)
            nc.vector.tensor_copy(row_of[:, :], part_i[:, 2, :]).then_inc(part_sem, 1)
            v.wait_ge(part_sem, 5)
            v.wait_ge(ramp, 2)
            B = 2 * G
            for u in range(C // B):
                cols = slice(u * B, (u + 1) * B)
                if u >= 2:
                    v.wait_ge(placed, u - 1)
                nc.vector.tensor_tensor(is_row[:, u % 2, :, :], keep["iota"][:, :].unsqueeze(1).to_broadcast([P, B, P]),
                                        row_of[:, cols].unsqueeze(2).to_broadcast([P, B, P]), ALU.is_equal).then_inc(spotted, 1)
                nc.vector.tensor_tensor(is_tile[:, u % 2, :, :], tile_ramp[:, :].unsqueeze(1).to_broadcast([P, B, PT + 1]),
                                        tile_of[:, cols].unsqueeze(2).to_broadcast([P, B, PT + 1]), ALU.is_equal).then_inc(part_sem, 1)
                v.wait_ge(part_sem, 6 + u)
                nc.vector.tensor_tensor(is_tile[:, u % 2, :, :], is_tile[:, u % 2, :, :],
                                        keep["node"][:, cols].unsqueeze(2).to_broadcast([P, B, PT + 1]), ALU.mult).then_inc(spotted, 1)
            v.wait_ge(placed, C // B)
            nc.vector.tensor_scalar(keep["part_node"][:, :], node_ps[:, 0:PT + 1], -1.0, 0.0, ALU.add, ALU.max).then_inc(done, 1)
            v.wait_ge(links, 16 * G)
            v.wait_ge(lk, 1)
            nc.vector.tensor_tensor(same[:, :, 1:P], link_in[:, :, 1:P], link_in[:, :, 0:P - 1], ALU.is_equal).then_inc(lk, 1)
            v.wait_ge(lk, 2)
            nc.vector.tensor_scalar(keep["link"][:, :, 1:P], same[:, :, 1:P], -1.0, FAR, ALU.add, ALU.mult).then_inc(lk, 1)
            v.wait_ge(lk, 3)
            nc.vector.tensor_copy(keep["link_back"][:, :, :], keep["link"][:, :, P:0:-1]).then_inc(lk, 1)

        @block.tensor
        def _(pe):
            pe.wait_ge(const, 7)
            pe.wait_ge(rank, 3)
            pe.wait_ge(first, 1)
            nc.tensor.matmul(rank_ps[:, 0:C], tri[:, :], keep["first"][:, :], start=True, stop=True).then_inc(rank, 1)
            nc.tensor.matmul(num_ps[:, 0:C], keep["ones"][:, :], keep["first"][:, :], start=True, stop=True).then_inc(rank, 1)
            B = 2 * G
            for u in range(C // B):
                pe.wait_ge(spotted, 2 * u + 2)
                for j in range(B):
                    mm = nc.tensor.matmul(node_ps[:, 0:PT + 1], is_row[:, u % 2, j, :], is_tile[:, u % 2, j, :],
                                          start=(u == 0 and j == 0), stop=(u == C // B - 1 and j == B - 1))
                mm.then_inc(placed, 1)


def tables_layer0(nc, ins, keep, scratch):
    with Phase(nc) as ctx:
        def sb(name, shape, dt):
            return ctx.enter_context(nc.sbuf_tensor("t0_" + name, shape, dt))
        x_t = sb("x_t", [P, KH, NP], F32)
        text_t = sb("text_t", [P, KH, NP], F32)
        w = sb("w", [P, 3, KH, D], F32)
        bias = sb("bias", [P, 3, D], F32)
        rel = sb("rel", [P, D], F32)
        out = sb("out", [P, 4, 3 * D], F32)
        ps = [ctx.enter_context(nc.psum_tensor(f"t0_ps{i}", [P, 2, BLK], F32)) for i in range(4)]
        loaded, bias_in, biased, summed, made = sems(
            nc, ctx, "t0_loaded", "t0_bias_in", "t0_biased", "t0_summed", "t0_made")
        stored = sems(nc, ctx, *(f"t0_stored{i}" for i in range(4)))
        block = ctx.enter_context(nc.Block("tables0"))

        def all_rows(ap):
            return bass.AP(tensor=ap.tensor, offset=ap.offset, ap=[[0, P]] + [list(a) for a in ap.ap])

        @block.sync
        def _(sp):
            for i, name in enumerate(("wv_t", "wk_t", "wq_t")):
                sp.dma_start(w[:, i, :, :], ins[name].rearrange("(k p) o -> p k o", p=P)).then_inc(loaded, 16)
            sp.dma_start(x_t[:, :, :], ins["x_t"].rearrange("(k p) n -> p k n", p=P)).then_inc(loaded, 16)
            sp.dma_start(text_t[:, :, :], ins["text_t"].rearrange("(k p) n -> p k n", p=P)).then_inc(loaded, 16)
            for i, name in enumerate(("L0_gnn_bv", "L0_gnn_bk", "L0_gnn_bq")):
                sp.dma_start(bias[:, i, :], all_rows(ins[name])).then_inc(bias_in, 16)
            sp.dma_start(rel[:, :], all_rows(ins["L0_gnn_relation_emb"])).then_inc(bias_in, 16)
            for t in range(NT):
                sp.wait_ge(made, 2 * (t + 1))
                sp.dma_start(scratch["vk"][t * P:(t + 1) * P, :], out[:, t % 4, 0:2 * D]).then_inc(stored[t % 4], 16)
                sp.dma_start(scratch["q"][t * P:(t + 1) * P, :], out[:, t % 4, 2 * D:3 * D]).then_inc(stored[t % 4], 16)
            for i in range(4):
                sp.wait_ge(stored[i], 32 * len(range(i, NT, 4)))

        @block.tensor
        def _(pe):
            pe.wait_ge(loaded, 80)
            for t in range(NT):
                if t >= 4:
                    pe.wait_ge(made, 2 * (t - 3))
                for i, of in enumerate((x_t, text_t, text_t)):
                    for k in range(KH):
                        mm = nc.tensor.matmul(ps[t % 4][:, i // 2, (i % 2) * D:(i % 2) * D + D],
                                              of[:, k, t * P:(t + 1) * P], w[:, i, k, :], start=(k == 0), stop=(k == KH - 1))
                mm.then_inc(summed, 1)

        @block.vector
        def _(v):
            v.wait_ge(bias_in, 64)
            nc.vector.tensor_tensor(bias[:, 1, :], bias[:, 1, :], rel[:, :], ALU.add).then_inc(biased, 1)
            v.wait_ge(biased, 1)
            for t in range(NT):
                v.wait_ge(summed, t + 1)
                if t >= 4:
                    v.wait_ge(stored[t % 4], 32 * (t // 4))
                nc.vector.tensor_tensor(out[:, t % 4, 0:2 * D], ps[t % 4][:, 0, :],
                                        bias[:, 0:2, :].rearrange("p a d -> p (a d)"), ALU.add).then_inc(made, 1)
                nc.vector.tensor_tensor(out[:, t % 4, 2 * D:3 * D], ps[t % 4][:, 1, 0:D], bias[:, 2, :], ALU.add).then_inc(made, 1)


def spread_to_parts(nc, keep, name, by_node, by_part, width):
    with Phase(nc) as ctx:
        rows = ctx.enter_context(nc.sbuf_tensor(name + "_rows", [P, PT + 1, width], F32))
        got, stored = sems(nc, ctx, name + "_got", name + "_stored")
        block = ctx.enter_context(nc.Block(name))

        @block.gpsimd
        def _(pool):
            for t in range(PT + 1):
                nc.gpsimd.indirect_dma_start(
                    rows[:, t, :], None, by_node,
                    bass.IndirectOffsetOnAxis(ap=keep["part_node"][:, t:t + 1], axis=0)).then_inc(got, 16)

        @block.sync
        def _(sp):
            sp.wait_ge(got, 16 * (PT + 1))
            sp.dma_start(by_part.rearrange("(t p) d -> p t d", p=P), rows[:, :, :]).then_inc(stored, 16)
            sp.wait_ge(stored, 16)


def attend_edges(nc, keep, scratch, layer, by_src, by_part, ws, wd, scale, scatters):
    with Phase(nc) as ctx:
        def sb(name, shape, dt):
            return ctx.enter_context(nc.sbuf_tensor(f"e{layer}_" + name, shape, dt))
        from_src = sb("from_src", [P, RING, G, ws], F32)
        window = sb("window", [P, 2, G, wd], F32)
        src_ix = sb("src_ix", [P, RING, G], I32)
        cell_ix = sb("cell_ix", [P, RING, G], I32)
        one16 = sb("one16", [P, 1], F16)
        raw_score = sb("raw_score", [P, 2, G * H], F32)
        score = sb("score", [P, 2, G * H], F32)
        shifted = sb("shifted", [P, 2, G * H], F32)
        running = sb("running", [G * H, P], F32)
        peak = sb("peak", [G * H, 2, P], F32)
        small = sb("small", [P, 2, G, SMALL], F32)
        onehot = sb("onehot", [P, RING, G, P], F32)
        onehot_t = sb("onehot_t", [P, 2, G, P], F32)
        PAIRS = G // 2

        def pst(name):
            return ctx.enter_context(nc.psum_tensor(f"e{layer}_" + name, [P, BLK], F32))
        turned = pst("turned")
        back = pst("back")
        part_ps = [pst(f"part_ps{i}") for i in range(2)]
        hot_ps = [pst(f"hot_ps{i}") for i in range(2)]
        spread_ps = [pst(f"spread_ps{i}") for i in range(2)]
        (ix_ready, cell_added, raw, scored, t_turned, fwd, peaked, t_back, shift_done, prob, mask_done, weighted,
         zeroed, one_set, passed, pe_passed, hot, hot_turned, hot_copied, part_written) = sems(
            nc, ctx, *(f"e{layer}_" + n for n in (
                "ix_ready", "cell_added", "raw", "scored", "t_turned", "fwd", "peaked", "t_back", "shift_done",
                "prob", "mask_done", "weighted", "zeroed", "one_set", "passed", "pe_passed", "hot", "hot_turned",
                "hot_copied", "part_written")))
        chunk_summed = sems(nc, ctx, *(f"e{layer}_chunk_summed{b}" for b in range(RING)))
        evacuated = sems(nc, ctx, *(f"e{layer}_evacuated{s}" for s in range(2)))
        src_in = sems(nc, ctx, *(f"e{layer}_src_in{b}" for b in range(RING)))
        win_in = sems(nc, ctx, *(f"e{layer}_win_in{b}" for b in range(2)))
        spread = sems(nc, ctx, *(f"e{layer}_spread{s}" for s in range(2)))
        used = sems(nc, ctx, *(f"e{layer}_used{s}" for s in range(2)))
        block = ctx.enter_context(nc.Block(f"edges{layer}"))

        LAST = NG // RING - 1

        def ticks(eng, tick):
            def at(it, b, first, last):
                before = (it, b - 1) if b else None if first else (it - 1, RING - 1)
                after = (it, b + 1) if b + 1 < RING else None if last else (it + 1, 0)
                tick(before, (it, b), after)

            for b in range(RING):
                at(0, b, True, False)
            with eng.Fori(1, LAST) as it:
                for b in range(RING):
                    at(it, b, False, False)
            for b in range(RING):
                at(LAST, b, False, True)

        @block.sync
        def _(sp):
            with sp.Fori(0, NG // RING) as it:
                for b in range(RING):
                    g = RING * it + b
                    sp.wait_ge(scored, g + 1)
                    for j in range(G):
                        at = sp.value_load(keep["offset"][0:1, bass.ds(g * G + j, 1)], min_val=0, max_val=PARTS)
                        sp.dma_start(window[:, b % 2, j, :], by_part[bass.ds(at, P), :]).then_inc(win_in[b % 2], 16)

        @block.gpsimd
        def _(pool):
            first_col, per_group = scatters
            pool.wait_ge(one_set, 1)
            with pool.Fori(0, NG // RING) as it:
                for b in range(RING):
                    g = RING * it + b
                    pool.wait_ge(chunk_summed[b], G * it + 1)
                    nc.gpsimd.tensor_copy(src_ix[:, b, :], keep["src"][:, bass.ds(g * G, G)]).then_inc(ix_ready, 1)
                    nc.gpsimd.tensor_copy(cell_ix[:, b, 0:per_group],
                                          keep["cell"][:, bass.ds(g * per_group + first_col, per_group)]).then_inc(ix_ready, 1)
                    pool.wait_ge(ix_ready, 2 * (g + 1))
                    pool.sem_inc(passed, 1)
                    done = 0
                    for j in range(G):
                        if j * per_group // G == done:
                            if done:
                                pool.wait_ge(cell_added, 16 * per_group * g + 16 * done)
                                pool.sem_inc(passed, 1)
                            nc.gpsimd.indirect_dma_start(
                                scratch["adj"], bass.IndirectOffsetOnAxis(ap=cell_ix[:, b, done:done + 1], axis=0),
                                one16[:, 0:1], None, compute_op=ALU.add).then_inc(cell_added, 16)
                            done += 1
                        nc.gpsimd.indirect_dma_start(
                            from_src[:, b, j, :], None, by_src,
                            bass.IndirectOffsetOnAxis(ap=src_ix[:, b, j:j + 1], axis=0)).then_inc(src_in[b], 16)
                    pool.wait_ge(cell_added, 16 * per_group * g + 16 * per_group)

        @block.vector
        def _(v):
            nc.vector.memset(one16[:, :], 1.0).then_inc(one_set, 1)
            nc.vector.memset(small[:, :, :, :], 0.0).then_inc(zeroed, 1)
            nc.vector.memset(keep["sums"][:, :, :], 0.0).then_inc(zeroed, 1)
            nc.vector.memset(keep["side"][:, :], 0.0).then_inc(zeroed, 1)
            v.wait_ge(zeroed, 3)

            def spot_slots(it, b):
                v.wait_ge(chunk_summed[b], G * it + 1)
                nc.vector.tensor_tensor(onehot[:, b, :, :], keep["iota"][:, :].unsqueeze(1).to_broadcast([P, G, P]),
                                        keep["slot"][:, bass.ds((RING * it + b) * G, G)].unsqueeze(2).to_broadcast([P, G, P]),
                                        ALU.is_equal).then_inc(hot, 1)

            def tick(before, group, after):
                it, b = group
                g, r = RING * it + b, b % 2
                pair = RING // 2 * it + b // 2
                cols = bass.ds(g * G, G)
                v.wait_ge(chunk_summed[(b - 2) % RING], G * it + (G if b >= 2 else 0) + 1)
                v.wait_ge(src_in[b], 16 * G * it + 16 * G)
                if layer == 0:
                    for i in range(PAIRS):
                        v.wait_ge(spread[i % 2], PAIRS // 2 * g + i // 2 + 1)
                        k_rows = from_src[:, b, 2 * i:2 * i + 2, D:2 * D]
                        nc.vector.tensor_tensor(k_rows, k_rows, spread_ps[i % 2][:, :].rearrange("p (j d) -> p j d", j=2),
                                                ALU.mult).then_inc(used[i % 2], 1)
                    for i in range(2):
                        v.wait_ge(used[i], PAIRS // 2 * (g + 1) + 1)
                    nc.vector.tensor_reduce(score[:, r, :].rearrange("p (j h) -> p j h", h=H),
                                            from_src[:, b, :, D:2 * D].rearrange("p j (h d) -> p j h d", h=H),
                                            AX_X, ALU.add).then_inc(scored, 1)
                else:
                    v.wait_ge(spread[r], pair + 1)
                    nc.vector.tensor_tensor(raw_score[:, r, :].rearrange("p (j h) -> p j h", h=H), from_src[:, b, :, D:D + H],
                                            spread_ps[r][:, 0:G * H].rearrange("p (j h) -> p j h", h=H), ALU.add).then_inc(used[r], 1)
                    v.wait_ge(used[r], pair + 2)
                    nc.vector.scalar_tensor_tensor(out=score[:, r, :], in0=raw_score[:, r, :], scalar=0.2,
                                                   in1=raw_score[:, r, :], op0=ALU.mult, op1=ALU.max).then_inc(scored, 1)
                if after:
                    spot_slots(*after)
                v.wait_ge(t_turned, g + 1)
                nc.vector.tensor_tensor_scan(running[:, :], keep["link"][:, g, 0:P], turned[0:G * H, 0:P],
                                             -FAR, ALU.add, ALU.max).then_inc(fwd, 1)
                v.wait_ge(fwd, g + 1)
                nc.vector.tensor_tensor_scan(peak[:, r, ::-1], keep["link_back"][:, g, :], running[:, ::-1],
                                             -FAR, ALU.add, ALU.max).then_inc(peaked, 1)
                v.wait_ge(t_back, g + 1)
                nc.vector.tensor_tensor(shifted[:, r, :], score[:, r, :], back[:, 0:G * H], ALU.subtract).then_inc(shift_done, 1)
                nc.vector.tensor_tensor(small[:, r, :, COL_MAX:COL_MAX + H],
                                        back[:, 0:G * H].rearrange("p (j h) -> p j h", h=H),
                                        keep["first"][:, cols].unsqueeze(2).to_broadcast([P, G, H]), ALU.mult).then_inc(mask_done, 1)
                nc.vector.tensor_copy(small[:, r, :, COL_NODE], keep["node"][:, cols]).then_inc(mask_done, 1)
                v.wait_ge(prob, g + 1)
                nc.vector.tensor_tensor(
                    from_src[:, b, :, 0:D].rearrange("p j (h d) -> p j h d", h=H),
                    from_src[:, b, :, 0:D].rearrange("p j (h d) -> p j h d", h=H),
                    small[:, r, :, 0:H].unsqueeze(3).to_broadcast([P, G, H, DK]), ALU.mult).then_inc(weighted, 1)

            spot_slots(0, 0)
            ticks(v, tick)

        @block.tensor
        def _(pe):
            for b in range(RING):
                pe.sem_inc(chunk_summed[b], 1)
            for s in range(2):
                pe.sem_inc(used[s], 1)
                pe.sem_inc(scored, 1)

            def turn_slots(it, b):
                g = RING * it + b
                pe.wait_ge(hot, g + 1)
                for q in range(2):
                    pe.wait_ge(hot_copied, 2 * g + q + 1)
                    pe.sem_inc(pe_passed, 1)
                    for j in range(4 * q, 4 * q + 4):
                        mm = nc.tensor.transpose(hot_ps[q][:, j % 4 * P:(j % 4 + 1) * P], onehot[:, b, j, :], keep["ident"][:, :])
                    mm.then_inc(hot_turned, 1)

            def spread_windows(it, b):
                g, r = RING * it + b, b % 2
                pair = RING // 2 * it + b // 2
                pe.wait_ge(win_in[r], 16 * G * pair + 16 * G)
                for j in range(G):
                    if j % 4 == 0:
                        pe.wait_ge(hot_copied, 2 * g + j // 4 + 3)
                    if layer == 0:
                        s = j // 2 % 2
                        if j % 2 == 0:
                            pe.wait_ge(used[s], PAIRS // 2 * g + j // 4 + 1)
                        to = spread_ps[s][:, j % 2 * D:(j % 2 + 1) * D]
                    else:
                        s = r
                        if j == 0:
                            pe.wait_ge(used[s], pair + 1)
                        to = spread_ps[s][:, j * H:(j + 1) * H]
                    mm = nc.tensor.matmul(to, onehot_t[:, r, j, :], window[:, r, j, :], start=True, stop=True)
                    if (layer == 0 and j % 2) or j == G - 1:
                        mm.then_inc(spread[s], 1)

            def turn_scores(it, b):
                g, r = RING * it + b, b % 2
                pe.wait_ge(scored, g + 3)
                pe.sem_inc(pe_passed, 1)
                nc.tensor.transpose(turned[0:G * H, 0:P], score[:, r, :], keep["ident"][:, :]).then_inc(t_turned, 1)
                pe.wait_ge(peaked, g + 1)
                pe.sem_inc(pe_passed, 1)
                nc.tensor.transpose(back[:, 0:G * H], peak[:, r, :], keep["ident"][0:G * H, 0:G * H]).then_inc(t_back, 1)

            def sum_parts(it, b):
                g, r = RING * it + b, b % 2
                pe.wait_ge(weighted, g + 1)
                pe.wait_ge(mask_done, 2 * g + 2)
                for j in range(G):
                    s = j % 2
                    pe.wait_ge(evacuated[s], G * g + 2 * (j // 2) + 1)
                    for k in range(KH):
                        nc.tensor.matmul(part_ps[s][:, k * P:(k + 1) * P], from_src[:, b, j, k * P:(k + 1) * P],
                                         onehot[:, b, j, :], start=True, stop=True)
                    nc.tensor.matmul(part_ps[s][0:SMALL, KH * P:KH * P + P], small[:, r, j, :], onehot[:, b, j, :],
                                     start=True, stop=True).then_inc(chunk_summed[b], 1)

            def tick(before, group, after):
                spread_windows(*group)
                if before:
                    sum_parts(*before)
                turn_scores(*group)
                if after:
                    turn_slots(*after)

            turn_slots(0, 0)
            ticks(pe, tick)
            sum_parts(LAST, RING - 1)

        @block.scalar
        def _(act):
            act.wait_ge(zeroed, 3)
            for s in range(2):
                act.sem_inc(evacuated[s], 1)
                act.sem_inc(hot_copied, 1)

            def copy_turned(it, b):
                g, r = RING * it + b, b % 2
                for q in range(2):
                    act.wait_ge(hot_turned, 2 * g + q + 1)
                    nc.scalar.activation(onehot_t[:, r, 4 * q:4 * q + 4, :], hot_ps[q][:, :].rearrange("p (j e) -> p j e", j=4),
                                         ACT.Copy).then_inc(hot_copied, 1)

            def weigh(it, b):
                g, r = RING * it + b, b % 2
                act.wait_ge(shift_done, g + 1)
                nc.scalar.activation(small[:, r, :, 0:H], shifted[:, r, :].rearrange("p (j h) -> p j h", h=H),
                                     ACT.Exp, scale=scale).then_inc(prob, 1)

            def copy_sums(it, b):
                g = RING * it + b
                for j in range(G):
                    s = j % 2
                    at = act.value_load(keep["offset"][0:1, bass.ds(g * G + j, 1)], min_val=0, max_val=PARTS)
                    act.wait_ge(chunk_summed[b], G * it + j + 2)
                    act.wait_ge(evacuated[1 - s], G * g + 2 * ((j + 1) // 2) + 1)
                    nc.scalar.activation(keep["sums"][:, :, bass.ds(at, P)],
                                         part_ps[s][:, 0:KH * P].rearrange("p (k e) -> p k e", k=KH), ACT.Copy).then_inc(evacuated[s], 1)
                    nc.scalar.activation(keep["side"][:, bass.ds(at, P)], part_ps[s][0:SMALL, KH * P:KH * P + P],
                                         ACT.Copy).then_inc(evacuated[s], 1)

            def tick(before, group, after):
                if before:
                    copy_sums(*before)
                weigh(*group)
                if after:
                    copy_turned(*after)

            copy_turned(0, 0)
            ticks(act, tick)
            copy_sums(LAST, RING - 1)


def merge_parts(nc, ins, keep, scratch, layer, weight, out_rows, scale):
    with Phase(nc) as ctx:
        def sb(name, shape, dt):
            return ctx.enter_context(nc.sbuf_tensor(f"m{layer}_" + name, shape, dt))
        w_out = sb("w_out", [P, KH, D], F32)
        node_row = sb("node_row", [1, PARTS], F32)
        node_all = sb("node_all", [P, PARTS + 2], F32)
        joined = sb("joined", [P, PARTS + 1], BF16)
        peak = sb("peak", [H, PARTS], F32)
        link = sb("link", [H, PARTS + 1], F32)
        work = sb("work", [H, PARTS], F32)
        top = sb("top", [H, PARTS], F32)
        rows = sb("rows", [P, 4, D], F32)
        index = sb("index", [P, PT], I32)

        def pst(name):
            return ctx.enter_context(nc.psum_tensor(f"m{layer}_" + name, [P, BLK], F32))
        wide_ps = [pst(f"wide_ps{i}") for i in range(4)]
        row_ps = [pst(f"row_ps{i}") for i in range(2)]
        index_ps = pst("index_ps")
        carried = sb("carried", [P, KH, NB], F32)
        sums, side = keep["sums"], keep["side"]
        (w_in, moved, spread, copied, step, expd, wide, summed, idx, idx_t, projected, out_copied, carry_kept,
         indexed, ends_set) = sems(
            nc, ctx, *(f"m{layer}_" + n for n in (
                "w_in", "moved", "spread", "copied", "step", "expd", "wide", "summed", "idx", "idx_t", "projected",
                "out_copied", "carry_kept", "indexed", "ends_set")))
        stored = sems(nc, ctx, *(f"m{layer}_stored{i}" for i in range(4)))
        block = ctx.enter_context(nc.Block(f"merge{layer}"))

        @block.sync
        def _(sp):
            if weight is not None:
                sp.dma_start(w_out[:, :, :], ins[weight].rearrange("(k p) o -> p k o", p=P)).then_inc(w_in, 16)

        @block.scalar
        def _(act):
            nc.scalar.activation(node_row[:, :], side[COL_NODE:COL_NODE + 1, 0:PARTS], ACT.Copy).then_inc(moved, 1)
            nc.scalar.activation(peak[:, :], side[COL_MAX:COL_MAX + H, 0:PARTS], ACT.Copy).then_inc(moved, 1)
            for b in range(NB):
                act.wait_ge(spread, b + 1)
                nc.scalar.activation(node_all[:, 1 + b * BLK:1 + (b + 1) * BLK], wide_ps[b % 4][:, :], ACT.Copy).then_inc(copied, 1)
            act.wait_ge(step, 5)
            nc.scalar.activation(peak[:, :], work[:, :], ACT.Exp, scale=scale).then_inc(expd, 1)
            for t in range(PT):
                act.wait_ge(projected, t + 1)
                if t >= 4:
                    act.wait_ge(stored[t % 4], 16 * (t // 4))
                nc.scalar.activation(rows[:, t % 4, :], row_ps[t % 2][:, 0:D], ACT.Copy).then_inc(out_copied, 1)

        @block.tensor
        def _(pe):
            pe.wait_ge(moved, 1)
            for b in range(NB):
                if b >= 4:
                    pe.wait_ge(copied, b - 3)
                nc.tensor.matmul(wide_ps[b % 4][:, :], keep["ones"][0:1, :], node_row[:, b * BLK:(b + 1) * BLK],
                                 start=True, stop=True).then_inc(spread, 1)
            pe.wait_ge(copied, NB)
            pe.wait_ge(step, 9)
            for b in range(NB):
                for k in range(KH):
                    n = b * KH + k
                    for i, of in enumerate((peak, work)):
                        if n >= 2:
                            pe.wait_ge(summed, 3 * (n - 2) + (1 if i == 0 else 3))
                        nc.tensor.matmul(wide_ps[2 * (n % 2) + i][:, :], keep["hsel"][:, k * P:(k + 1) * P],
                                         of[:, b * BLK:(b + 1) * BLK], start=True, stop=True).then_inc(wide, 1)
            pe.wait_ge(idx, 4)
            for t in range(PT):
                mm = nc.tensor.matmul(index_ps[:, t:t + 1], node_row[:, t * P:(t + 1) * P], keep["ones"][0:1, 0:1],
                                      start=True, stop=True)
            mm.then_inc(idx_t, 1)
            if weight is not None:
                pe.wait_ge(w_in, 16)
            pe.wait_ge(summed, 3 * KH * NB)
            for t in range(PT):
                if t >= 2:
                    pe.wait_ge(out_copied, t - 1)
                for k in range(KH):
                    if weight is None:
                        mm = nc.tensor.transpose(row_ps[t % 2][:, k * P:(k + 1) * P], sums[:, k, t * P:(t + 1) * P],
                                                 keep["ident"][:, :])
                    else:
                        mm = nc.tensor.matmul(row_ps[t % 2][:, 0:D], sums[:, k, t * P:(t + 1) * P], w_out[:, k, :],
                                              start=(k == 0), stop=(k == KH - 1))
                mm.then_inc(projected, 1)

        @block.vector
        def _(v):
            nc.vector.memset(node_all[:, 0:1], -1.0).then_inc(ends_set, 1)
            nc.vector.memset(node_all[:, PARTS + 1:PARTS + 2], -1.0).then_inc(ends_set, 1)
            v.wait_ge(moved, 2)
            v.wait_ge(ends_set, 2)
            v.wait_ge(copied, NB)
            nc.vector.tensor_tensor(joined[:, :], node_all[:, 1:PARTS + 2], node_all[:, 0:PARTS + 1], ALU.is_equal).then_inc(step, 1)
            v.wait_ge(step, 1)
            nc.vector.tensor_scalar(link[:, :], joined[0:H, :], -1.0, FAR, ALU.add, ALU.mult).then_inc(step, 1)
            v.wait_ge(step, 2)
            nc.vector.tensor_tensor_scan(work[:, :], link[:, 0:PARTS], peak[:, :], -FAR, ALU.add, ALU.max).then_inc(step, 1)
            v.wait_ge(step, 3)
            nc.vector.tensor_tensor_scan(top[:, ::-1], link[:, PARTS:0:-1], work[:, ::-1], -FAR, ALU.add, ALU.max).then_inc(step, 1)
            v.wait_ge(step, 4)
            nc.vector.tensor_tensor(work[:, :], peak[:, :], top[:, :], ALU.subtract).then_inc(step, 1)
            nc.vector.tensor_scalar(link[0:1, 0:PARTS], joined[0:1, 1:PARTS + 1], -1.0, 1.0, ALU.mult, ALU.add).then_inc(idx, 1)
            v.wait_ge(idx, 1)
            nc.vector.tensor_tensor(node_row[:, :], node_row[:, :], link[0:1, 0:PARTS], ALU.mult).then_inc(idx, 1)
            v.wait_ge(idx, 2)
            nc.vector.tensor_scalar(link[0:1, 0:PARTS], node_row[:, :], 0.0, 8192.0, ALU.is_equal, ALU.mult).then_inc(idx, 1)
            v.wait_ge(idx, 3)
            nc.vector.scalar_tensor_tensor(out=node_row[:, :], in0=node_row[:, :], scalar=-1.0, in1=link[0:1, 0:PARTS],
                                           op0=ALU.add, op1=ALU.add).then_inc(idx, 1)
            v.wait_ge(expd, 1)
            nc.vector.tensor_tensor(work[:, :], side[0:H, 0:PARTS], peak[:, :], ALU.mult).then_inc(step, 1)
            v.wait_ge(step, 6)
            nc.vector.tensor_tensor_scan(top[:, :], joined[0:H, 0:PARTS], work[:, :], 0.0, ALU.mult, ALU.add).then_inc(step, 1)
            v.wait_ge(step, 7)
            nc.vector.tensor_scalar(top[:, :], top[:, :], 1e-30, None, ALU.max).then_inc(step, 1)
            v.wait_ge(step, 8)
            nc.vector.reciprocal(work[:, :], top[:, :]).then_inc(step, 1)
            for b in range(NB):
                cols = slice(b * BLK, (b + 1) * BLK)
                for k in range(KH):
                    n = b * KH + k
                    part, carry = sums[:, k, cols], 0.0 if b == 0 else carried[:, k, b - 1:b]
                    v.wait_ge(wide, 2 * n + 1)
                    nc.vector.tensor_tensor(part, part, wide_ps[2 * (n % 2)][:, :], ALU.mult).then_inc(summed, 1)
                    v.wait_ge(summed, 3 * n + 1)
                    nc.vector.tensor_tensor_scan(part, joined[:, cols], part, carry, ALU.mult, ALU.add).then_inc(summed, 1)
                    v.wait_ge(wide, 2 * n + 2)
                    v.wait_ge(summed, 3 * n + 2)
                    nc.vector.tensor_copy(carried[:, k, b:b + 1], part[:, BLK - 1:BLK]).then_inc(carry_kept, 1)
                    v.wait_ge(carry_kept, n + 1)
                    nc.vector.tensor_tensor(part, part, wide_ps[2 * (n % 2) + 1][:, :], ALU.mult).then_inc(summed, 1)
            v.wait_ge(idx_t, 1)
            nc.vector.tensor_copy(index[:, :], index_ps[:, 0:PT]).then_inc(indexed, 1)

        @block.gpsimd
        def _(pool):
            pool.wait_ge(indexed, 1)
            for t in range(PT):
                pool.wait_ge(out_copied, t + 1)
                nc.gpsimd.indirect_dma_start(
                    out_rows, bass.IndirectOffsetOnAxis(ap=index[:, t:t + 1], axis=0), rows[:, t % 4, :], None,
                    bounds_check=N - 1, oob_is_err=False).then_inc(stored[t % 4], 16)
            for i in range(4):
                pool.wait_ge(stored[i], 16 * (PT // 4))


def residual_norm(nc, ins, keep, scratch, layer, add, bias, x_from=None):
    with Phase(nc) as ctx:
        def sb(name, shape, dt):
            return ctx.enter_context(nc.sbuf_tensor(f"n{layer}_" + name, shape, dt))
        more = sb("more", [P, NT, D], F32) if add is not None else None
        bias_all = sb("bias_all", [P, D], F32)
        stats = sb("stats", [P, NT, 6], F32)
        mean_var = sb("mean_var", [P, NT, 2], F32)
        std = sb("std", [P, NT], F32)
        x = keep["x"]
        loaded, summed, stat, aggr, rooted, inv, normed, x_in = sems(
            nc, ctx, *(f"n{layer}_" + n for n in ("loaded", "summed", "stat", "aggr", "rooted", "inv", "normed", "x_in")))
        block = ctx.enter_context(nc.Block(f"norm{layer}"))

        @block.sync
        def _(sp):
            if x_from is not None:
                sp.dma_start(x[:, :, :], x_from.rearrange("(t p) d -> p t d", p=P)).then_inc(x_in, 16)
            if add is not None:
                sp.dma_start(more[:, :, :], add.rearrange("(t p) d -> p t d", p=P)).then_inc(loaded, 16)
            if bias is not None:
                of = ins[bias]
                sp.dma_start(bias_all[:, :], bass.AP(tensor=of.tensor, offset=of.offset,
                                                     ap=[[0, P]] + [list(a) for a in of.ap])).then_inc(loaded, 16)

        @block.vector
        def _(v):
            if x_from is not None:
                v.wait_ge(x_in, 16)
            if add is not None:
                v.wait_ge(loaded, 16 if bias is None else 32)
                nc.vector.tensor_tensor(x[:, :, :], x[:, :, :], more[:, :, :], ALU.add).then_inc(summed, 1)
                v.wait_ge(summed, 1)
            if bias is not None:
                nc.vector.tensor_tensor(x[:, :, :], x[:, :, :], bias_all[:, :].unsqueeze(1).to_broadcast([P, NT, D]),
                                        ALU.add).then_inc(summed, 1)
                v.wait_ge(summed, 2)
            for t in range(NT):
                nc.vector.bn_stats(stats[:, t, :], x[:, t, :]).then_inc(stat, 1)
            v.wait_ge(stat, NT)
            for t in range(NT):
                nc.vector.bn_aggr(mean_var[:, t, :], stats[:, t, :]).then_inc(aggr, 1)
            v.wait_ge(aggr, NT)
            nc.vector.tensor_scalar(std[:, :], mean_var[:, :, 1], EPS, None, ALU.add).then_inc(inv, 1)
            v.wait_ge(rooted, 1)
            nc.vector.reciprocal(std[:, :], std[:, :]).then_inc(inv, 1)
            v.wait_ge(inv, 2)
            for t in range(NT):
                nc.vector.tensor_scalar(x[:, t, :], x[:, t, :], mean_var[:, t, 0:1], std[:, t:t + 1],
                                        ALU.subtract, ALU.mult).then_inc(normed, 1)

        @block.scalar
        def _(act):
            act.wait_ge(inv, 1)
            nc.scalar.activation(std[:, :], std[:, :], ACT.Sqrt).then_inc(rooted, 1)


def store_x(nc, keep, out):
    with Phase(nc) as ctx:
        stored, = sems(nc, ctx, "out_stored")
        block = ctx.enter_context(nc.Block("store"))

        @block.sync
        def _(sp):
            full = N // P
            sp.dma_start(out[0:full * P, :].rearrange("(t p) d -> p t d", p=P), keep["x"][:, 0:full, :]).then_inc(stored, 16)
            sp.dma_start(out[full * P:N, :], keep["x"][0:N - full * P, full, :]).then_inc(stored, 16)
            sp.wait_ge(stored, 32)


def tables_layer1(nc, ins, keep, scratch):
    HEADS4, DH = 4, D // 4
    WIDE = D + 2 * H
    with Phase(nc) as ctx:
        def sb(name, shape, dt):
            return ctx.enter_context(nc.sbuf_tensor("t1_" + name, shape, dt))
        x_t = sb("x_t", [P, KH, NP], F32)
        w_attn = sb("w_attn", [P, KH, D], F32)
        a_cols = sb("a_cols", [P, KH, 2 * H], F32)
        w_all = sb("w_all", [P, KH, WIDE], F32)
        out = sb("out", [P, 4, WIDE], F32)
        ps = [ctx.enter_context(nc.psum_tensor(f"t1_ps{i}", [P, BLK], F32)) for i in range(4)]
        fold_ps = ctx.enter_context(nc.psum_tensor("t1_fold_ps", [P, KH, 2 * H], F32))
        cleared, w_in, a_in, turned, copied, folded, fold_copied, summed, made, x_out = sems(
            nc, ctx, *("t1_" + n for n in ("cleared", "w_in", "a_in", "turned", "copied", "folded", "fold_copied",
                                           "summed", "made", "x_out")))
        stored = sems(nc, ctx, *(f"t1_stored{i}" for i in range(4)))
        block = ctx.enter_context(nc.Block("tables1"))

        @block.sync
        def _(sp):
            sp.dma_start(scratch["x1"].rearrange("(t p) d -> p t d", p=P), keep["x"][:, :, :]).then_inc(x_out, 16)
            sp.dma_start(w_attn[:, :, :], ins["L1_gnn_W_attn"].rearrange("(k p) i -> p k i", p=P)).then_inc(w_in, 16)
            sp.dma_start(w_all[:, :, 0:D], ins["L1_gnn_W_lin_t"].rearrange("(k p) o -> p k o", p=P)).then_inc(w_in, 16)
            sp.wait_ge(cleared, 1)
            a = ins["L1_gnn_a"]
            for h in range(HEADS4):
                rows = slice(h * DH % P, h * DH % P + DH)
                for side in range(2):
                    for twin in range(2):
                        col = side * H + 2 * h + twin
                        sp.dma_start(a_cols[rows, h * DH // P, col:col + 1],
                                     a[h, side * DH:(side + 1) * DH].rearrange("(d o) -> d o", o=1)).then_inc(a_in, 16)
            for t in range(NT):
                sp.wait_ge(made, t + 1)
                sp.dma_start(scratch["val"][t * P:(t + 1) * P, :], out[:, t % 4, 0:D + H]).then_inc(stored[t % 4], 16)
                sp.dma_start(scratch["alpha"][t * P:(t + 1) * P, :], out[:, t % 4, D + H:WIDE]).then_inc(stored[t % 4], 16)
            for i in range(4):
                sp.wait_ge(stored[i], 32 * len(range(i, NT, 4)))
            sp.wait_ge(x_out, 16)

        @block.tensor
        def _(pe):
            for t in range(NT):
                if t >= 4:
                    pe.wait_ge(copied, t - 3)
                for k in range(KH):
                    mm = nc.tensor.transpose(ps[t % 4][:, k * P:(k + 1) * P], keep["x"][:, t, k * P:(k + 1) * P], keep["ident"][:, :])
                mm.then_inc(turned, 1)
            pe.wait_ge(w_in, 32)
            pe.wait_ge(a_in, 256)
            for k_in in range(KH):
                for k in range(KH):
                    mm = nc.tensor.matmul(fold_ps[:, k_in, :], w_attn[:, k, k_in * P:(k_in + 1) * P], a_cols[:, k, :],
                                          start=(k == 0), stop=(k == KH - 1))
            mm.then_inc(folded, 1)
            pe.wait_ge(fold_copied, 1)
            pe.wait_ge(copied, NT)
            for t in range(NT):
                if t >= 4:
                    pe.wait_ge(made, t - 3)
                for k in range(KH):
                    mm = nc.tensor.matmul(ps[t % 4][:, 0:WIDE], x_t[:, k, t * P:(t + 1) * P], w_all[:, k, :],
                                          start=(k == 0), stop=(k == KH - 1))
                mm.then_inc(summed, 1)

        @block.vector
        def _(v):
            nc.vector.memset(a_cols[:, :, :], 0.0).then_inc(cleared, 1)
            for t in range(NT):
                v.wait_ge(turned, t + 1)
                nc.vector.tensor_copy(x_t[:, :, t * P:(t + 1) * P], ps[t % 4][:, 0:D].rearrange("p (k n) -> p k n", k=KH)).then_inc(copied, 1)
            v.wait_ge(folded, 1)
            nc.vector.tensor_copy(w_all[:, :, D:WIDE], fold_ps[:, :, :]).then_inc(fold_copied, 1)

        @block.scalar
        def _(act):
            for t in range(NT):
                act.wait_ge(summed, t + 1)
                if t >= 4:
                    act.wait_ge(stored[t % 4], 32 * (t // 4))
                nc.scalar.activation(out[:, t % 4, :], ps[t % 4][:, 0:WIDE], ACT.Copy).then_inc(made, 1)


def turn_x(nc, keep, state, name):
    with Phase(nc) as ctx:
        ps = [ctx.enter_context(nc.psum_tensor(f"{name}_ps{i}", [P, BLK], F32)) for i in range(4)]
        turned, copied = sems(nc, ctx, name + "_turned", name + "_copied")
        block = ctx.enter_context(nc.Block(name))

        @block.tensor
        def _(pe):
            for t in range(NT):
                if t >= 4:
                    pe.wait_ge(copied, t - 3)
                for k in range(KH):
                    mm = nc.tensor.transpose(ps[t % 4][:, k * P:(k + 1) * P], keep["x"][:, t, k * P:(k + 1) * P], keep["ident"][:, :])
                mm.then_inc(turned, 1)

        @block.vector
        def _(v):
            for t in range(NT):
                v.wait_ge(turned, t + 1)
                nc.vector.tensor_copy(state["h_t"][:, :, t * P:(t + 1) * P],
                                      ps[t % 4][:, 0:D].rearrange("p (k n) -> p k n", k=KH)).then_inc(copied, 1)


def add_turned(nc, keep, state, name):
    with Phase(nc) as ctx:
        ps = [ctx.enter_context(nc.psum_tensor(f"{name}_ps{i}", [P, BLK], F32)) for i in range(4)]
        turned, added = sems(nc, ctx, name + "_turned", name + "_added")
        block = ctx.enter_context(nc.Block(name))

        @block.tensor
        def _(pe):
            for t in range(NT):
                if t >= 4:
                    pe.wait_ge(added, t - 3)
                for k in range(KH):
                    mm = nc.tensor.transpose(ps[t % 4][:, k * P:(k + 1) * P], state["h_t"][:, k, t * P:(t + 1) * P], keep["ident"][:, :])
                mm.then_inc(turned, 1)

        @block.vector
        def _(v):
            for t in range(NT):
                v.wait_ge(turned, t + 1)
                nc.vector.tensor_tensor(keep["x"][:, t, :], keep["x"][:, t, :], ps[t % 4][:, 0:D], ALU.add).then_inc(added, 1)


GIN_LAYERS = 5
SAGE_LAYERS = 3
GIN_COLUMNS = ("L2_gnn_b1", "L2_gnn_g1", "L2_gnn_bt1", "L2_gnn_b2", "L2_gnn_bn_g", "L2_gnn_bn_b")
SAGE_COLUMNS = ("L3_gnn_b1l", "L3_gnn_b2l", "L3_gnn_b3l")


def count_degrees(nc, state, scratch):
    with Phase(nc) as ctx:
        ps = [[ctx.enter_context(nc.psum_tensor(f"cd_ps{i}_{n}", [P, BLK], F32)) for n in range(2)] for i in range(2)]
        counts = ctx.enter_context(nc.sbuf_tensor("cd_counts", [P, 2, AN], F32))
        ones16 = ctx.enter_context(nc.sbuf_tensor("cd_ones16", [P, P], F16))
        slab = state["slab"]
        ones_set, slab_used, pass_read, inverted = sems(nc, ctx, "cd_ones_set", "cd_slab_used", "cd_pass_read", "cd_inverted")
        slab_in = sems(nc, ctx, *(f"cd_slab_in{s}" for s in range(NSLAB)))
        block = ctx.enter_context(nc.Block("degrees"))
        adj = slabs_of(scratch)

        @block.sync
        def _(sp):
            for a in range(APASS):
                for s in range(NSLAB):
                    if a:
                        sp.wait_ge(slab_used, NSLAB * (a - 1) + s + 1)
                    sp.dma_start(slab[:, s, :, :], adj[s, a]).then_inc(slab_in[s], 16)

        @block.tensor
        def _(pe):
            pe.wait_ge(ones_set, 1)
            for a in range(APASS):
                if a >= 2:
                    pe.wait_ge(pass_read, 2 * (a - 1))
                for s in range(NSLAB):
                    pe.wait_ge(slab_in[s], 16 * (a + 1))
                    for k in range(SLAB):
                        for n in range(2):
                            mm = nc.tensor.matmul(ps[a % 2][n][:, 0:AN], ones16[:, :], slab[:, s, k, n * AN:(n + 1) * AN],
                                                  start=(s == 0 and k == 0), stop=(s == NSLAB - 1 and k == SLAB - 1))
                    mm.then_inc(slab_used, 1)

        @block.vector
        def _(v):
            nc.vector.memset(ones16[:, :], 1.0).then_inc(ones_set, 1)
            for a in range(APASS):
                v.wait_ge(slab_used, NSLAB * (a + 1))
                for n in range(2):
                    cols = slice((2 * a + n) * AN, (2 * a + n + 1) * AN)
                    nc.vector.tensor_scalar(counts[:, n, :], ps[a % 2][n][:, 0:AN], 1.0, FS, ALU.max, ALU.mult).then_inc(pass_read, 1)
                    v.wait_ge(pass_read, 2 * a + n + 1)
                    nc.vector.reciprocal(state["inv_degree"][:, cols], counts[:, n, :]).then_inc(inverted, 1)


def slabs_of(scratch):
    return scratch["adj"].rearrange("(s k p a c) o -> s a p k (c o)", s=NSLAB, k=SLAB, p=P, a=APASS)


def graph_layers(nc, ins, keep, scratch, state, kind):
    gin = kind == "gin"
    LAYERS = GIN_LAYERS if gin else SAGE_LAYERS
    COLS = len(GIN_COLUMNS if gin else SAGE_COLUMNS[:1])
    NBLK = 2 * APASS
    PROJ = 2 if gin else 1
    LAG = 3
    RT = 3
    with Phase(nc) as ctx:
        def sb(n, shape, dt):
            return ctx.enter_context(nc.sbuf_tensor(f"{kind}_{n}", shape, dt))

        def pst(n):
            return ctx.enter_context(nc.psum_tensor(f"{kind}_{n}", [P, BLK], F32))
        w = sb("w", [P, 2, KH, D], F32)
        columns = sb("columns", [P, COLS, KH], F32)
        floors = sb("floors", [P, LAYERS], F32)
        floor = sb("floor", [P, 2], F32)
        message = sb("message", [P, RT, D], F32)
        stats = sb("stats", [P, KH, NBLK, 6], F32)
        mean_var = sb("mean_var", [P, KH, 2], F32)
        std = sb("std", [P, KH], F32)
        gain = sb("gain", [P, KH], F32)
        shift = sb("shift", [P, KH], F32)
        own_all = sb("own_all", [P, LAYERS], F32)
        own = sb("own", [P, 1], F32)
        sum_ps = [pst(f"sum_ps{i}") for i in range(2 * KH)]
        proj_ps = [pst(f"proj_ps{i}") for i in range(2 * KH)]
        h_t, z_t, high, low, slab = (state[n] for n in ("h_t", "z_t", "high", "low", "slab"))
        (ready, own_in, own_set, floor_set, pool_floor_set, params_in, turned, message_made, high_done, low_done, floored,
         slab_used, evacuated, summed, moved, normed, stat, aggr, step, rooted, passed,
         v_passed, pool_passed) = sems(
            nc, ctx, *(f"{kind}_" + n for n in (
                "ready", "own_in", "own_set", "floor_set", "pool_floor_set", "params_in", "turned", "message_made",
                "high_done", "low_done", "floored", "slab_used", "evacuated", "summed", "moved", "normed", "stat", "aggr",
                "step", "rooted", "passed", "v_passed", "pool_passed")))
        slab_in = sems(nc, ctx, *(f"{kind}_slab_in{s}" for s in range(NSLAB)))
        h_done = sems(nc, ctx, *(f"{kind}_h_done{m}" for m in range(KH)))
        block = ctx.enter_context(nc.Block(f"{kind}_layers"))
        adj = slabs_of(scratch)

        USED0, EVAC0, H0 = NSLAB, 1, NBLK
        MOVED0 = 2 * KH + KH * NBLK

        def cols(b):
            return slice(b * AN, (b + 1) * AN)

        def wait_h(eng, l, b):
            if gin:
                for m in range(KH):
                    eng.wait_ge(h_done[m], NBLK * l + b + 1)
            else:
                eng.wait_ge(moved, KH * NBLK * l + 2 * KH + KH * (b + 1))

        @block.sync
        def _(sp):
            if gin:
                eps = ins["L2_gnn_eps"]
                sp.dma_start(own_all[:, :], bass.AP(tensor=eps.tensor, offset=eps.offset,
                                                    ap=[[0, P]] + [list(a) for a in eps.ap])).then_inc(own_in, 16)
            with sp.Fori(0, LAYERS) as l:
                for a in range(APASS):
                    for s in range(NSLAB):
                        sp.wait_ge(slab_used, NSLAB * APASS * l + NSLAB * a + s + 1)
                        sp.dma_start(slab[:, s, :, :], adj[s, a]).then_inc(slab_in[s], 16)
                    if a == 0:
                        wait_h(sp, l, NBLK - 1)
                        sp.dma_start(w[:, :, :, :], ins[kind + "_w"][bass.ds(l, 1)].rearrange("l i (k p) o -> p (l i) k o", p=P)).then_inc(params_in, 16)
                        sp.dma_start(columns[:, :, :], ins[kind + "_columns"][bass.ds(l, 1)].rearrange("l p c k -> p (l c) k")).then_inc(params_in, 16)

        @block.tensor
        def _(pe):
            pe.sem_inc(slab_used, USED0)
            pe.sem_inc(evacuated, EVAC0)
            pe.sem_inc(moved, MOVED0)
            for m in range(KH):
                pe.sem_inc(h_done[m], H0)

            def turn(l, t):
                wait_h(pe, l, min(NBLK - 1, ((t + 1) * P - 1) // AN) if gin else NBLK - 1)
                if t >= 2 * KH:
                    pe.wait_ge(message_made, NT * l + t - 2 * KH + 1)
                pe.sem_inc(passed, 1)
                for k in range(KH):
                    mm = nc.tensor.transpose(proj_ps[t % (2 * KH)][:, k * P:(k + 1) * P], h_t[:, k, t * P:(t + 1) * P],
                                             keep["ident"][:, :])
                mm.then_inc(turned, 1)

            def sum_tile(l, a, t):
                s, k = t // SLAB, t % SLAB
                if t == 0:
                    pe.wait_ge(evacuated, 2 * KH * APASS * l + 2 * KH * a + EVAC0)
                if k == 0:
                    pe.wait_ge(slab_in[s], 16 * APASS * l + 16 * (a + 1))
                for m in range(KH):
                    for i, part in enumerate((high, low)):
                        for n in range(2):
                            mm = nc.tensor.matmul(sum_ps[KH * n + m][:, 0:AN], part[:, t, m * P:(m + 1) * P],
                                                  slab[:, s, k, n * AN:(n + 1) * AN],
                                                  start=(t == 0 and i == 0), stop=(t == NT - 1 and i == 1))
                if k == SLAB - 1:
                    mm.then_inc(slab_used, 1)

            def project(l, p, b, terms):
                pe.wait_ge(moved, KH * NBLK * PROJ * l + KH * (NBLK * p + b - 1) + MOVED0)
                for m in range(KH):
                    for i, (src, weight) in enumerate(terms):
                        for k in range(KH):
                            mm = nc.tensor.matmul(proj_ps[KH * (b % 2) + m][:, 0:AN], weight[:, k, m * P:(m + 1) * P],
                                                  src[:, k, cols(b)], start=(i == 0 and k == 0),
                                                  stop=(i == len(terms) - 1 and k == KH - 1))
                mm.then_inc(summed, 1)

            with pe.Fori(0, LAYERS) as l:
                for t in range(NT + LAG):
                    if t < NT:
                        turn(l, t)
                    if t >= LAG:
                        pe.wait_ge(low_done, NT * l + t - LAG + 1)
                        sum_tile(l, 0, t - LAG)
                for a in range(1, APASS + 1):
                    if a < APASS:
                        for t in range(NT):
                            sum_tile(l, a, t)
                    if a == 1:
                        pe.wait_ge(params_in, 32 * l + 32)
                        if not gin:
                            pe.wait_ge(floored, l + 2)
                    for b in range(2 * (a - 1), 2 * a):
                        pe.wait_ge(evacuated, 2 * KH * APASS * l + KH * (b + 1) + EVAC0)
                        project(l, 0, b, [(z_t, w[:, 0])] if gin else [(z_t, w[:, 0]), (h_t, w[:, 1])])
                if gin:
                    for b in range(NBLK):
                        pe.wait_ge(normed, KH * NBLK * l + KH * (b + 1))
                        project(l, 1, b, [(z_t, w[:, 1])])

        @block.gpsimd
        def _(pool):
            nc.gpsimd.memset(floors[:, 0:1], -FAR).then_inc(ready, 1)
            nc.gpsimd.memset(floors[:, 1:LAYERS], 0.0).then_inc(ready, 1)
            pool.wait_ge(ready, 2)
            pool.sem_inc(floored, 1)
            with pool.Fori(0, LAYERS) as l:
                pool.wait_ge(floored, l + 1)
                nc.gpsimd.tensor_copy(floor[:, 1:2], floors[:, bass.ds(l, 1)]).then_inc(pool_floor_set, 1)
                pool.wait_ge(pool_floor_set, l + 1)
                pool.wait_ge(turned, NT * l + NT)
                pool.sem_inc(pool_passed, 1)
                nc.gpsimd.tensor_scalar(h_t[:, :, 0:AW], h_t[:, :, 0:AW], floor[:, 1:2], None, ALU.max).then_inc(floored, 1)

        @block.scalar
        def _(act):
            def move(l, p, b):
                act.wait_ge(summed, NBLK * PROJ * l + NBLK * p + b + 1)
                to = z_t if gin else h_t
                for m in range(KH):
                    nc.scalar.activation(to[:, m, cols(b)], proj_ps[KH * (b % 2) + m][:, 0:AN], ACT.Identity,
                                         bias=columns[:, 3 * p, m:m + 1], scale=1.0 / FS if gin and p == 0 else 1.0).then_inc(moved, 1)

            def root(l, p):
                act.wait_ge(step, 10 * l + 5 * p + 1)
                nc.scalar.activation(std[:, :], std[:, :], ACT.Sqrt).then_inc(rooted, 1)
                act.wait_ge(step, 10 * l + 5 * p + 5)

            def norm_relu(b):
                for m in range(KH):
                    nc.scalar.activation(z_t[:, m, cols(b)], z_t[:, m, cols(b)], ACT.Relu,
                                         bias=shift[:, m:m + 1], scale=gain[:, m:m + 1]).then_inc(normed, 1)

            with act.Fori(0, LAYERS) as l:
                for t in range(NT):
                    act.wait_ge(message_made, NT * l + t + 1)
                    nc.scalar.activation(high[:, t, :], message[:, t % RT, :], ACT.Copy).then_inc(high_done, 1)
                act.wait_ge(params_in, 32 * l + 32)
                for b in range(NBLK):
                    move(l, 0, b)
                if gin:
                    root(l, 0)
                    norm_relu(0)
                    norm_relu(1)
                    for b in range(NBLK):
                        move(l, 1, b)
                        if b + 2 < NBLK:
                            norm_relu(b + 2)
                    root(l, 1)
                    for b in range(NBLK):
                        nc.scalar.activation(h_t[:, 0, cols(b)], z_t[:, 0, cols(b)], ACT.Identity,
                                             bias=shift[:, 0:1], scale=gain[:, 0:1]).then_inc(h_done[0], 1)

        @block.vector
        def _(v):
            v.wait_ge(ready, 2)
            if gin:
                v.wait_ge(own_in, 16)
                nc.vector.tensor_scalar(own_all[:, :], own_all[:, :], 1.0, FS, ALU.add, ALU.mult).then_inc(own_set, 1)
                v.wait_ge(own_set, 1)

            def make_message(l, t):
                v.wait_ge(turned, NT * l + t + 1)
                if t >= RT:
                    v.wait_ge(low_done, NT * l + t - RT + 1)
                nc.vector.tensor_scalar(message[:, t % RT, :], proj_ps[t % (2 * KH)][:, 0:D], 0.0 if gin else floor[:, 0:1], FS,
                                        ALU.max, ALU.mult).then_inc(message_made, 1)

            def evacuate(l, a):
                v.wait_ge(slab_used, NSLAB * APASS * l + NSLAB * (a + 1) + USED0)
                for n in range(2):
                    for m in range(KH):
                        b = 2 * a + n
                        bank = sum_ps[KH * n + m][:, 0:AN]
                        if gin:
                            nc.vector.scalar_tensor_tensor(out=z_t[:, m, cols(b)], in0=h_t[:, m, cols(b)], scalar=own[:, 0:1],
                                                           in1=bank, op0=ALU.mult, op1=ALU.add).then_inc(evacuated, 1)
                        else:
                            nc.vector.tensor_tensor(z_t[:, m, cols(b)], bank, state["inv_degree"][:, cols(b)],
                                                    ALU.mult).then_inc(evacuated, 1)

            def block_stats(l, p, b):
                v.wait_ge(moved, KH * NBLK * PROJ * l + KH * (NBLK * p + b + 1) + MOVED0)
                for m in range(KH):
                    nc.vector.bn_stats(stats[:, m, b, :], z_t[:, m, b * AN:min((b + 1) * AN, N)]).then_inc(stat, 1)

            def gain_and_shift(l, p):
                base = 10 * l + 5 * p
                v.wait_ge(stat, 2 * KH * NBLK * l + KH * NBLK * (p + 1))
                v.sem_inc(v_passed, 1)
                for m in range(KH):
                    nc.vector.bn_aggr(mean_var[:, m, :], stats[:, m, :, :].rearrange("p b s -> p (b s)")).then_inc(aggr, 1)
                v.wait_ge(aggr, 2 * KH * l + KH * (p + 1))
                nc.vector.tensor_scalar(std[:, :], mean_var[:, :, 1], EPS, None, ALU.add).then_inc(step, 1)
                v.wait_ge(rooted, 2 * l + p + 1)
                nc.vector.reciprocal(std[:, :], std[:, :]).then_inc(step, 1)
                v.wait_ge(step, base + 2)
                nc.vector.tensor_tensor(gain[:, :], std[:, :], columns[:, 1 + 3 * p, :], ALU.mult).then_inc(step, 1)
                v.wait_ge(step, base + 3)
                nc.vector.tensor_tensor(shift[:, :], mean_var[:, :, 0], gain[:, :], ALU.mult).then_inc(step, 1)
                v.wait_ge(step, base + 4)
                nc.vector.tensor_tensor(shift[:, :], columns[:, 2 + 3 * p, :], shift[:, :], ALU.subtract).then_inc(step, 1)

            with v.Fori(0, LAYERS) as l:
                if gin:
                    nc.vector.tensor_copy(own[:, :], own_all[:, bass.ds(l, 1)]).then_inc(own_set, 1)
                else:
                    nc.vector.tensor_copy(floor[:, 0:1], floors[:, bass.ds(l, 1)]).then_inc(floor_set, 1)
                    v.wait_ge(floor_set, l + 1)
                make_message(l, 0)
                for t in range(NT):
                    if t + 1 < NT:
                        make_message(l, t + 1)
                    v.wait_ge(high_done, NT * l + t + 1)
                    nc.vector.tensor_tensor(low[:, t, :], message[:, t % RT, :], high[:, t, :], ALU.subtract).then_inc(low_done, 1)
                if gin:
                    v.wait_ge(own_set, l + 2)
                    v.wait_ge(floored, l + 2)
                evacuate(l, 0)
                if gin:
                    v.wait_ge(params_in, 32 * l + 32)
                for a in range(1, APASS):
                    evacuate(l, a)
                    if gin:
                        for b in range(2 * (a - 1), 2 * a):
                            block_stats(l, 0, b)
                if gin:
                    for b in range(NBLK - 2, NBLK):
                        block_stats(l, 0, b)
                    gain_and_shift(l, 0)
                    for b in range(NBLK):
                        block_stats(l, 1, b)
                    gain_and_shift(l, 1)
                    v.wait_ge(step, 10 * l + 10)
                    for b in range(NBLK):
                        nc.vector.tensor_scalar(h_t[:, 1, cols(b)], z_t[:, 1, cols(b)], gain[:, 1:2], shift[:, 1:2],
                                                ALU.mult, ALU.add).then_inc(h_done[1], 1)


PLAIN = ("L0_gnn_relation_emb", "L0_gnn_bq", "L0_gnn_bk", "L0_gnn_bv", "L0_gnn_bo", "L1_gnn_W_attn", "L1_gnn_a",
         "L2_gnn_eps")
TURNED = ("L1_gnn_W_lin",)




def gnn_kernel(nc, ins, out):
    with ExitStack() as ctx:
        def sb(name, shape, dt):
            return ctx.enter_context(nc.sbuf_tensor(name, shape, dt))
        scratch = {
            "adj": nc.dram_tensor("adj", [NP * AW, 1], F16, kind="Internal").ap(),
            "vk": nc.dram_tensor("vk", [NP, 2 * D], F32, kind="Internal").ap(),
            "q": nc.dram_tensor("q", [NP, D], F32, kind="Internal").ap(),
            "val": nc.dram_tensor("val", [NP, D + H], F32, kind="Internal").ap(),
            "alpha": nc.dram_tensor("alpha", [NP, H], F32, kind="Internal").ap(),
            "q_part": nc.dram_tensor("q_part", [PBUF, D], F32, kind="Internal").ap(),
            "alpha_part": nc.dram_tensor("alpha_part", [PBUF, H], F32, kind="Internal").ap(),
            "x1": nc.dram_tensor("x1", [NP, D], F32, kind="Internal").ap(),
            "out0": nc.dram_tensor("out0", [NP, D], F32, kind="Internal").ap(),
            "out1": nc.dram_tensor("out1", [NP, D], F32, kind="Internal").ap(),
        }
        keep = {
            "ident": sb("ident", [P, P], F32),
            "ones": sb("ones", [P, P], F32),
        }
        with ExitStack() as edge_ctx:
            def esb(name, shape, dt):
                return edge_ctx.enter_context(nc.sbuf_tensor(name, shape, dt))
            keep.update({
                "hsel": esb("hsel", [H, D], F32), "iota": esb("iota", [P, P], F32),
                "src": esb("src", [P, C], I32), "dst": esb("dst", [P, C], I32), "cell": esb("cell", [P, C], I32),
                "first": esb("first", [P, C], F32), "slot": esb("slot", [P, C], F32), "node": esb("node", [P, C], F32),
                "part_node": esb("part_node", [P, PT + 1], I32), "offset": esb("offset", [1, C], I32), "link": esb("link", [G * H, NG, LINK], BF16),
                "link_back": esb("link_back", [G * H, NG, P], BF16),
            })
            prepare_edges(nc, ins, keep, scratch)
            tables_layer0(nc, ins, keep, scratch)
            with ExitStack() as part_ctx:
                keep["sums"] = part_ctx.enter_context(nc.sbuf_tensor("sums0", [P, KH, PBUF], F32))
                keep["side"] = part_ctx.enter_context(nc.sbuf_tensor("side0", [SMALL, PBUF], F32))
                spread_to_parts(nc, keep, "parts0", scratch["q"], scratch["q_part"], D)
                attend_edges(nc, keep, scratch, 0, scratch["vk"], scratch["q_part"], 2 * D, D, float(DK) ** -0.5, (0, G // 2))
                merge_parts(nc, ins, keep, scratch, 0, "wo_t", scratch["out0"], float(DK) ** -0.5)
            with ExitStack() as x_ctx:
                keep["x"] = x_ctx.enter_context(nc.sbuf_tensor("x_1", [P, NT, D], F32))
                residual_norm(nc, ins, keep, scratch, 0, scratch["out0"], "L0_gnn_bo", ins["x"])
                tables_layer1(nc, ins, keep, scratch)
            with ExitStack() as part_ctx:
                keep["sums"] = part_ctx.enter_context(nc.sbuf_tensor("sums1", [P, KH, PBUF], F32))
                keep["side"] = part_ctx.enter_context(nc.sbuf_tensor("side1", [SMALL, PBUF], F32))
                spread_to_parts(nc, keep, "parts1", scratch["alpha"], scratch["alpha_part"], H)
                attend_edges(nc, keep, scratch, 1, scratch["val"], scratch["alpha_part"], D + H, H, 1.0, (C // 2, G // 2))
                merge_parts(nc, ins, keep, scratch, 1, None, scratch["out1"], 1.0)
        keep["x"] = sb("x", [P, NT, D], F32)
        residual_norm(nc, ins, keep, scratch, 1, scratch["out1"], None, scratch["x1"])
        state = {
            "h_t": sb("h_t", [P, KH, NP], F32), "z_t": sb("z_t", [P, KH, AW], F32),
            "high": sb("high", [P, NT, D], F16), "low": sb("low", [P, NT, D], F16),
            "slab": sb("slab", [P, NSLAB, SLAB, ACOLS], F16),
        }
        turn_x(nc, keep, state, "turn2")
        graph_layers(nc, ins, keep, scratch, state, "gin")
        add_turned(nc, keep, state, "add2")
        residual_norm(nc, ins, keep, scratch, 2, None, None)
        state["inv_degree"] = sb("inv_degree", [P, AW], F32)
        turn_x(nc, keep, state, "turn3")
        count_degrees(nc, state, scratch)
        graph_layers(nc, ins, keep, scratch, state, "sage")
        add_turned(nc, keep, state, "add3")
        residual_norm(nc, ins, keep, scratch, 3, None, None)
        store_x(nc, keep, out)


def kernel(**inputs):
    import numpy as _np
    import concourse.bacc as _bacc
    from concourse import mybir as _mybir
    from concourse.bass_utils import run_bass_kernel_spmd as _run

    def padded_t(a):
        return _np.pad(_np.asarray(a).T, ((0, 0), (0, NP - N)))

    x = _np.asarray(inputs["x"])
    text = _np.concatenate([_np.asarray(inputs["L0_gnn_user_text_embs"]), _np.asarray(inputs["L0_gnn_item_text_embs"])])
    src = _np.pad(_np.asarray(inputs["src"]), (0, C * P - E))
    dst = _np.pad(_np.asarray(inputs["dst"]), (0, C * P - E), constant_values=N)
    chunks = dst.reshape(C, P)
    arrays = {
        "x": _np.pad(x, ((0, NP - N), (0, 0))), "x_t": padded_t(x), "text_t": padded_t(text),
        "src_col": src.reshape(C, P).T, "dst_col": chunks.T,
        "dst_prev": _np.pad(chunks[:, :-1], ((0, 0), (1, 0)), constant_values=-1).T,
        "src_row": src.reshape(P, C), "dst_row": dst.reshape(P, C), "dst_chunk": chunks,
        "wq_t": _np.asarray(inputs["L0_gnn_Wq"]).T, "wk_t": _np.asarray(inputs["L0_gnn_Wk"]).T,
        "wv_t": _np.asarray(inputs["L0_gnn_Wv"]).T, "wo_t": _np.asarray(inputs["L0_gnn_Wo"]).T,
    }
    arrays["gin_w"] = _np.stack([_np.asarray(inputs["L2_gnn_W1"]), _np.asarray(inputs["L2_gnn_W2"])], axis=1)
    arrays["sage_w"] = _np.stack([_np.stack([_np.asarray(inputs[f"L3_gnn_W{l + 1}{side}"]).T for side in "lr"])
                                  for l in range(SAGE_LAYERS)])
    gin = _np.stack([_np.asarray(inputs[r]) for r in GIN_COLUMNS])
    arrays["gin_columns"] = gin.reshape(len(GIN_COLUMNS), GIN_LAYERS, KH, P).transpose(1, 3, 0, 2)
    sage = _np.stack([_np.asarray(inputs[r]) for r in SAGE_COLUMNS])
    arrays["sage_columns"] = sage.reshape(SAGE_LAYERS, 1, KH, P).transpose(0, 3, 1, 2)
    for name in PLAIN:
        arrays[name] = _np.asarray(inputs[name])
    for name in TURNED:
        arrays[name + "_t"] = _np.asarray(inputs[name]).T
    arrays = {"in_" + k: _np.ascontiguousarray(a) for k, a in arrays.items()}
    nc = _bacc.Bacc("TRN2", target_bir_lowering=False, num_devices=1)
    ins = {k[3:]: nc.dram_tensor(k, a.shape, _mybir.dt.from_np(a.dtype), kind="ExternalInput").ap() for k, a in arrays.items()}
    out = nc.dram_tensor("out_x", (N, D), _mybir.dt.float32, kind="ExternalOutput").ap()
    gnn_kernel(nc, ins, out)
    r = _run(nc, [arrays], core_ids=[0])
    return r.results[0]["out_x"]
```

```python
from contextlib import ExitStack

import concourse.bass as bass
from concourse import mybir

F32 = mybir.dt.float32
F16 = mybir.dt.float16
BF16 = mybir.dt.bfloat16
I32 = mybir.dt.int32
ALU = mybir.AluOpType
ACT = mybir.ActivationFunctionType
AX_X = mybir.AxisListType.X

P = 128
N = 3125
D = 256
E = 53125
KH = D // P
NT = -(-N // P)
NP = NT * P
H = 8
DK = D // H
RING = 4
C = 416
G = 8
NG = C // G
LINK = P + 1
PT = 28
PARTS = PT * P
PBUF = PARTS + P
BLK = 512
NB = PARTS // BLK
FAR = 1.0e30
SMALL = P
COL_MAX = 32
COL_NODE = 64
COL_SIZE = 96
EPS = 1e-5

APASS = 4
ACOLS = 782
AW = APASS * ACOLS
AN = ACOLS // 2
SLAB = 5
NSLAB = NT // SLAB
FS = 16.0


class Phase(ExitStack):

    def __init__(self, nc):
        super().__init__()
        self.nc, self.used = nc, []
        self.callback(self.clear)

    def clear(self):
        self.nc.clear_and_free_semaphores(self.used)
        self.nc.all_engine_barrier()


def sems(nc, ctx, *names):
    made = [nc.alloc_semaphore(name=n) for n in names]
    ctx.used += made
    return made


def prepare(nc, ins, keep, scratch):
    STEP = 2 * G
    STEPS = C // STEP
    TW = PT + 1
    TB = 3
    LH = NG // 2
    ZOUT = SLAB * (D + 1)
    with Phase(nc) as ctx:
        def sb(name, shape, dt):
            return ctx.enter_context(nc.sbuf_tensor("pr_" + name, shape, dt))
        x_t = sb("x_t", [P, KH, NP], F32)
        text_t = sb("text_t", [P, KH, NP], F32)
        w = sb("w", [P, 3, KH, D], F32)
        bias = sb("bias", [P, 3, D], F32)
        rel = sb("rel", [P, D], F32)
        out = sb("out", [P, TB, 3 * D], F32)
        dst = sb("dst", [P, C], I32)
        dst_prev = sb("dst_prev", [P, C], I32)
        src_row = sb("src_row", [P, C], I32)
        dst_row = sb("dst_row", [P, C], I32)
        dst_row_next = sb("dst_row_next", [P, C], I32)
        alike = sb("alike", [P, C], F32)
        alike_sum = sb("alike_sum", [P, 1], F32)
        order = sb("order", [P, C], F32)
        once = sb("once", [P, 2], F32)
        number = sb("number", [P, C], F32)
        row_base = sb("row_base", [P, C], F32)
        tri = sb("tri", [P, P], F32)
        zero16 = sb("zero16", [P, AW], F16)
        zero32 = sb("zero32", [P, ZOUT], F32)
        counts = sb("counts", [P, C + 1], F32)
        zrow = sb("zrow", [P, C], F32)
        ints = sb("ints", [P, 6, C], I32)
        tile_of = sb("tile_of", [P, C], F16)
        row_of = sb("row_of", [P, C], F16)
        digits = sb("digits", [P, C, 2], F16)
        iota16 = sb("iota16", [P, P], F16)
        is_row = sb("is_row", [P, 2, STEP, P], F16)
        is_tile = sb("is_tile", [P, 2, STEP, TW], F16)
        tile_digits = sb("tile_digits", [P, 2, STEP, 2, TW], F16)
        part_number = sb("part_number", [P, 2, TW], F32)
        link_in = sb("link_in", [G * H, LH, P], I32)
        table_ps = [ctx.enter_context(nc.psum_tensor(f"pr_table_ps{i}", [P, 2, BLK], F32)) for i in range(TB)]
        rank_ps = ctx.enter_context(nc.psum_tensor("pr_rank_ps", [P, BLK], F32))
        count_ps = ctx.enter_context(nc.psum_tensor("pr_count_ps", [P, BLK], F32))
        node_ps = count_ps
        (edges_in, zeroed, zero_set, const, ones_set, ramp, first, ranked, slot_sem, number_sem, int_sem, half_sem, counted,
         offset_sem, cells, rows_spotted, tiles_spotted, digits_spotted, placed, node_sem, same, link_done,
         loaded, bias_in, biased, summed, made, compared, alike_total, repeats_set) = sems(
            nc, ctx, *("pr_" + n for n in (
                "edges_in", "zeroed", "zero_set", "const", "ones_set", "ramp", "first", "ranked", "slot", "number", "int",
                "half", "counted", "offset", "cells", "rows_spotted", "tiles_spotted", "digits_spotted", "placed", "node",
                "same", "link_done", "loaded", "bias_in", "biased", "summed", "made", "compared", "alike_total", "repeats_set")))
        links_in = sems(nc, ctx, "pr_links_in0", "pr_links_in1")
        stored = sems(nc, ctx, *(f"pr_stored{i}" for i in range(TB)))
        block = ctx.enter_context(nc.Block("prepare"))

        def all_rows(ap):
            return bass.AP(tensor=ap.tensor, offset=ap.offset, ap=[[0, P]] + [list(a) for a in ap.ap])

        def store_tables(sp, t):
            sp.dma_start(scratch["vk"][t * P:(t + 1) * P, :], out[:, t % TB, 0:2 * D]).then_inc(stored[t % TB], 16)
            sp.dma_start(scratch["q"][t * P:(t + 1) * P, :], out[:, t % TB, 2 * D:3 * D]).then_inc(stored[t % TB], 16)

        @block.sync
        def _(sp):
            for to, of in ((dst, ins["dst_col"]), (dst_prev, ins["dst_prev"]), (keep["src"], ins["src_col"]),
                           (src_row, ins["src_row"]), (dst_row, ins["dst_row"]), (dst_row_next, ins["dst_row_next"])):
                sp.dma_start(to[:, :], of).then_inc(edges_in, 16)
            for i, name in enumerate(("wv_t", "wk_t", "wq_t")):
                sp.dma_start(w[:, i, :, :], ins[name].rearrange("(k p) o -> p k o", p=P)).then_inc(loaded, 16)
            sp.dma_start(x_t[:, :, :], ins["x_t"].rearrange("(k p) n -> p k n", p=P)).then_inc(loaded, 16)
            sp.dma_start(text_t[:, :, :], ins["text_t"].rearrange("(k p) n -> p k n", p=P)).then_inc(loaded, 16)
            for i, name in enumerate(("L0_gnn_bv", "L0_gnn_bk", "L0_gnn_bq")):
                sp.dma_start(bias[:, i, :], all_rows(ins[name])).then_inc(bias_in, 16)
            sp.dma_start(rel[:, :], all_rows(ins["L0_gnn_relation_emb"])).then_inc(bias_in, 16)

            def load_links(part):
                rows = ins["dst_chunk"].rearrange("(h g j) e -> h j g e", h=2, j=G)[part]
                for j in range(G):
                    wide = bass.AP(tensor=rows.tensor, offset=rows[j].offset, ap=[[0, H]] + [list(a) for a in rows[j].ap])
                    sp.dma_start(link_in[j * H:(j + 1) * H, :, :], wide).then_inc(links_in[part], 16)

            load_links(0)
            sp.wait_ge(zero_set, 2)
            adj = scratch["adj"].rearrange("(t p c) o -> t p (c o)", t=NT, p=P)
            for t in range(NT):
                if t >= TB:
                    sp.wait_ge(made, 2 * (t - TB + 1))
                sp.dma_start(adj[t], zero16[:, :]).then_inc(zeroed, 16)
                if t >= TB:
                    store_tables(sp, t - TB)
            for name, wide in (("out0", D), ("out1", D + 1)):
                rows = scratch[name].rearrange("(p t k) d -> t p (k d)", p=P, k=SLAB)
                for t in range(NSLAB):
                    sp.dma_start(rows[t], zero32[:, 0:SLAB * wide]).then_inc(zeroed, 16)
            for t in range(NT - TB, NT):
                sp.wait_ge(made, 2 * (t + 1))
                store_tables(sp, t)
            sp.wait_ge(same, 1)
            load_links(1)
            for i in range(TB):
                sp.wait_ge(stored[i], 32 * len(range(i, NT, TB)))
            sp.wait_ge(zeroed, 16 * (NT + 2 * NSLAB))

        @block.gpsimd
        def _(pool):
            nc.gpsimd.memset(tri[:, :], 1.0).then_inc(const, 1)
            nc.gpsimd.memset(keep["ident"][:, :], 0.0).then_inc(const, 1)
            nc.gpsimd.memset(keep["hsel"][:, :], 1.0).then_inc(const, 1)
            pool.wait_ge(const, 3)
            nc.gpsimd.affine_select(out=tri[:, :], in_=tri[:, :], compare_op=ALU.is_ge,
                                    fill=0.0, base=0, pattern=[[1, P]], channel_multiplier=-1).then_inc(const, 1)
            nc.gpsimd.affine_select(out=keep["ident"][:, :], in_=keep["ident"][:, :], compare_op=ALU.not_equal,
                                    fill=1.0, base=0, pattern=[[-1, P]], channel_multiplier=1).then_inc(const, 1)
            nc.gpsimd.affine_select(out=keep["hsel"][:, :], in_=keep["hsel"][:, :], compare_op=ALU.is_ge,
                                    fill=0.0, base=0, pattern=[[1, D]], channel_multiplier=-DK).then_inc(const, 1)
            pool.wait_ge(const, 6)
            nc.gpsimd.affine_select(out=keep["hsel"][:, :], in_=keep["hsel"][:, :], compare_op=ALU.is_ge,
                                    fill=0.0, base=DK - 1, pattern=[[-1, D]], channel_multiplier=DK).then_inc(const, 1)
            nc.gpsimd.iota(keep["iota"][:, :], [[1, P]], base=0, channel_multiplier=0,
                           allow_small_or_imprecise_dtypes=True).then_inc(ramp, 1)
            pool.wait_ge(ramp, 1)
            nc.gpsimd.tensor_copy(iota16[:, :], keep["iota"][:, :]).then_inc(ramp, 1)
            nc.gpsimd.iota(order[:, :], [[1, C]], base=0, channel_multiplier=C,
                           allow_small_or_imprecise_dtypes=True).then_inc(ramp, 1)
            nc.gpsimd.memset(zero16[:, :], 0.0).then_inc(zero_set, 1)
            nc.gpsimd.memset(zero32[:, :], 0.0).then_inc(zero_set, 1)
            pool.wait_ge(ramp, 3)
            pool.wait_ge(half_sem, 4)
            for u in range(STEPS):
                cols = slice(u * STEP, (u + 1) * STEP)
                if u >= 2:
                    pool.wait_ge(placed, u - 1)
                pool.wait_ge(tiles_spotted, u + 1)
                nc.gpsimd.tensor_tensor(tile_digits[:, u % 2, :, :, :],
                                        is_tile[:, u % 2, :, :].unsqueeze(2).to_broadcast([P, STEP, 2, TW]),
                                        digits[:, cols, :].unsqueeze(3).to_broadcast([P, STEP, 2, TW]), ALU.mult).then_inc(digits_spotted, 1)

        @block.vector
        def _(v):
            nc.vector.memset(keep["ones"][:, :], 1.0).then_inc(ones_set, 1)
            nc.vector.memset(zrow[:, :], 0.0).then_inc(ones_set, 1)
            nc.vector.memset(counts[:, 0:1], 0.0).then_inc(ones_set, 1)
            nc.vector.memset(keep["link"][:, :, 0:1], 0.0).then_inc(ones_set, 1)
            nc.vector.memset(keep["link"][:, :, P:P + 1], 0.0).then_inc(ones_set, 1)
            v.wait_ge(edges_in, 96)
            nc.vector.tensor_tensor(keep["first"][:, :], dst[:, :], dst_prev[:, :], ALU.not_equal).then_inc(first, 1)
            nc.vector.tensor_scalar(number[:, :], dst[:, :], 1.0, None, ALU.add).then_inc(number_sem, 1)
            nc.vector.tensor_scalar(row_base[:, :], src_row[:, :], float(AW), None, ALU.mult).then_inc(cells, 1)
            v.wait_ge(number_sem, 1)
            v.wait_ge(first, 1)
            nc.vector.tensor_tensor(keep["node"][:, :], number[:, :], keep["first"][:, :], ALU.mult).then_inc(number_sem, 1)
            v.wait_ge(number_sem, 2)
            nc.vector.tensor_copy(ints[:, 3, :], keep["node"][:, :]).then_inc(int_sem, 1)
            v.wait_ge(int_sem, 1)
            nc.vector.tensor_scalar(ints[:, 4, :], ints[:, 3, :], 6, None, ALU.arith_shift_right).then_inc(int_sem, 1)
            nc.vector.tensor_scalar(ints[:, 5, :], ints[:, 3, :], 63, None, ALU.bitwise_and).then_inc(int_sem, 1)
            v.wait_ge(int_sem, 3)
            nc.vector.tensor_copy(digits[:, :, 0], ints[:, 4, :]).then_inc(half_sem, 1)
            nc.vector.tensor_copy(digits[:, :, 1], ints[:, 5, :]).then_inc(half_sem, 1)
            v.wait_ge(ranked, 2)
            v.wait_ge(ones_set, 5)
            nc.vector.tensor_scalar(keep["slot"][:, :], rank_ps[:, 0:C], -1.0, None, ALU.add).then_inc(slot_sem, 1)
            nc.vector.tensor_tensor_scan(counts[:, 1:C + 1], zrow[:, :], count_ps[:, 0:C], 0.0, ALU.add, ALU.add).then_inc(counted, 1)
            v.wait_ge(counted, 1)
            v.wait_ge(slot_sem, 1)
            nc.vector.tensor_tensor(ints[:, 0, :], keep["slot"][:, :], counts[:, 0:C], ALU.add).then_inc(int_sem, 1)
            v.wait_ge(int_sem, 4)
            nc.vector.tensor_scalar(ints[:, 1, :], ints[:, 0, :], 7, None, ALU.arith_shift_right).then_inc(int_sem, 1)
            nc.vector.tensor_scalar(ints[:, 2, :], ints[:, 0, :], P - 1, None, ALU.bitwise_and).then_inc(int_sem, 1)
            v.wait_ge(int_sem, 6)
            nc.vector.tensor_copy(tile_of[:, :], ints[:, 1, :]).then_inc(half_sem, 1)
            nc.vector.tensor_copy(row_of[:, :], ints[:, 2, :]).then_inc(half_sem, 1)
            nc.vector.tensor_copy(keep["offset"][:, :], counts[0:1, 0:C]).then_inc(offset_sem, 1)
            v.wait_ge(bias_in, 64)
            nc.vector.tensor_tensor(bias[:, 1, :], bias[:, 1, :], rel[:, :], ALU.add).then_inc(biased, 1)
            v.wait_ge(half_sem, 4)
            v.wait_ge(ramp, 3)
            v.wait_ge(biased, 1)

            def spot(u):
                cols = slice(u * STEP, (u + 1) * STEP)
                if u >= 2:
                    v.wait_ge(digits_spotted, u - 1)
                nc.vector.tensor_tensor(is_tile[:, u % 2, :, :], iota16[:, 0:TW].unsqueeze(1).to_broadcast([P, STEP, TW]),
                                        tile_of[:, cols].unsqueeze(2).to_broadcast([P, STEP, TW]), ALU.is_equal).then_inc(tiles_spotted, 1)
                if u >= 2:
                    v.wait_ge(placed, u - 1)
                nc.vector.tensor_tensor(is_row[:, u % 2, :, :], iota16[:, :].unsqueeze(1).to_broadcast([P, STEP, P]),
                                        row_of[:, cols].unsqueeze(2).to_broadcast([P, STEP, P]),
                                        ALU.is_equal).then_inc(rows_spotted, 1)

            spot(0)
            for t in range(NT):
                spot(t + 1)
                v.wait_ge(summed, t + 1)
                if t >= TB:
                    v.wait_ge(stored[t % TB], 32 * (t // TB))
                nc.vector.tensor_tensor(out[:, t % TB, 0:2 * D], table_ps[t % TB][:, 0, :],
                                        bias[:, 0:2, :].rearrange("p a d -> p (a d)"), ALU.add).then_inc(made, 1)
                nc.vector.tensor_tensor(out[:, t % TB, 2 * D:3 * D], table_ps[t % TB][:, 1, 0:D], bias[:, 2, :], ALU.add).then_inc(made, 1)
            nc.vector.tensor_tensor(alike[:, :], dst_row[:, :], dst_row_next[:, :], ALU.is_equal).then_inc(compared, 1)
            v.wait_ge(compared, 1)
            nc.vector.tensor_reduce(alike_sum[:, :], alike[:, :], AX_X, ALU.add).then_inc(compared, 1)
            v.wait_ge(alike_total, 1)
            nc.vector.tensor_copy(keep["repeats"][:, :], rank_ps[:, 0:1]).then_inc(repeats_set, 1)
            nc.vector.tensor_scalar(once[:, 0:1], rank_ps[:, 0:1], 0.0, None, ALU.is_equal).then_inc(repeats_set, 1)
            nc.vector.tensor_scalar(once[:, 1:2], rank_ps[:, 0:1], 0.0, None, ALU.is_gt).then_inc(repeats_set, 1)
            v.wait_ge(cells, 1)
            nc.vector.tensor_tensor(row_base[:, :], row_base[:, :], dst_row[:, :], ALU.add).then_inc(cells, 1)
            v.wait_ge(cells, 2)
            v.wait_ge(repeats_set, 3)
            nc.vector.tensor_copy(keep["cell"][:, :], row_base[:, :]).then_inc(cells, 1)
            nc.vector.tensor_copy(keep["count_one"][:, :], once[:, 0:1]).then_inc(cells, 1)
            nc.vector.tensor_scalar(order[:, :], order[:, :], once[:, 1:2], None, ALU.mult).then_inc(cells, 1)
            v.wait_ge(cells, 5)
            nc.vector.scalar_tensor_tensor(out=keep["cell_once"][:, :], in0=row_base[:, :], scalar=once[:, 0:1],
                                           in1=order[:, :], op0=ALU.mult, op1=ALU.add).then_inc(cells, 1)
            for half in range(2):
                groups = slice(half * LH, (half + 1) * LH)
                v.wait_ge(links_in[half], 16 * G)
                nc.vector.tensor_tensor(keep["link"][:, groups, 1:P], link_in[:, :, 1:P], link_in[:, :, 0:P - 1], ALU.is_equal).then_inc(same, 1)
                v.wait_ge(same, half + 1)
                nc.vector.tensor_scalar(keep["link"][:, groups, 1:P], keep["link"][:, groups, 1:P], -1.0, FAR,
                                        ALU.add, ALU.mult).then_inc(link_done, 1)
                v.wait_ge(link_done, 2 * half + 1)
                nc.vector.tensor_copy(keep["link_back"][:, groups, :], keep["link"][:, groups, P:0:-1]).then_inc(link_done, 1)
            v.wait_ge(placed, STEPS)
            nc.vector.tensor_copy(part_number[:, :, :], node_ps[:, 0:2 * TW].rearrange("p (i t) -> p i t", i=2)).then_inc(node_sem, 1)
            v.wait_ge(node_sem, 1)
            nc.vector.scalar_tensor_tensor(out=part_number[:, 0, :], in0=part_number[:, 0, :], scalar=64.0,
                                           in1=part_number[:, 1, :], op0=ALU.mult, op1=ALU.add).then_inc(node_sem, 1)
            v.wait_ge(node_sem, 2)
            nc.vector.tensor_scalar(keep["part_node"][:, :], part_number[:, 0, :], -1.0, 0.0, ALU.add, ALU.max).then_inc(node_sem, 1)

        @block.tensor
        def _(pe):
            pe.wait_ge(const, 4)
            pe.wait_ge(ones_set, 1)
            pe.wait_ge(first, 1)
            nc.tensor.matmul(rank_ps[:, 0:C], tri[:, :], keep["first"][:, :], start=True, stop=True).then_inc(ranked, 1)
            nc.tensor.matmul(count_ps[:, 0:C], keep["ones"][:, :], keep["first"][:, :], start=True, stop=True).then_inc(ranked, 1)

            def place_nodes(u):
                pe.wait_ge(rows_spotted, u + 1)
                pe.wait_ge(digits_spotted, u + 1)
                for j in range(STEP):
                    mm = nc.tensor.matmul(node_ps[:, 0:2 * TW], is_row[:, u % 2, j, :],
                                          tile_digits[:, u % 2, j, :, :].rearrange("p i t -> p (i t)"),
                                          start=(u == 0 and j == 0), stop=(u == STEPS - 1 and j == STEP - 1))
                mm.then_inc(placed, 1)

            pe.wait_ge(loaded, 80)
            for t in range(NT):
                if t >= TB:
                    pe.wait_ge(made, 2 * (t - TB + 1))
                for i, of in enumerate((x_t, text_t, text_t)):
                    for k in range(KH):
                        mm = nc.tensor.matmul(table_ps[t % TB][:, i // 2, (i % 2) * D:(i % 2) * D + D],
                                              of[:, k, t * P:(t + 1) * P], w[:, i, k, :], start=(k == 0), stop=(k == KH - 1))
                mm.then_inc(summed, 1)
                place_nodes(t)
            place_nodes(NT)
            pe.wait_ge(compared, 2)
            nc.tensor.matmul(rank_ps[:, 0:1], keep["ones"][:, :], alike_sum[:, :], start=True, stop=True).then_inc(alike_total, 1)


def attend_edges(nc, keep, scratch, layer, by_src, by_node, by_part, ws, wd, scale, scatters):
    with Phase(nc) as ctx:
        def sb(name, shape, dt):
            return ctx.enter_context(nc.sbuf_tensor(f"e{layer}_" + name, shape, dt))
        from_src = sb("from_src", [P, RING, G, ws], F32)
        window = sb("window", [P, 2, G, wd], F32)
        src_ix = sb("src_ix", [P, RING, G], I32)
        cell_ix = sb("cell_ix", [P, RING, G], I32)
        one16 = sb("one16", [P, 1], F16)
        started = sb("started", [P, 1], F16)
        staged = keep["sums"][:, 0:KH, :].rearrange("p k n -> p (k n)")[:, 0:(PT + 1) * wd].rearrange("p (t d) -> p t d", d=wd)
        raw_score = sb("raw_score", [P, 2, G * H], F32)
        score = sb("score", [P, 2, G * H], F32)
        shifted = sb("shifted", [P, 2, G * H], F32)
        running = sb("running", [G * H, P], F32)
        peak = sb("peak", [G * H, 2, P], F32)
        small = sb("small", [P, 2, G, SMALL], F32)
        onehot = sb("onehot", [P, RING, G, P], F32)
        onehot_t = sb("onehot_t", [P, 2, G, P], F32)
        PAIRS = G // 2
        FIRST, SECOND = G // 2, 3 * G // 4

        def pst(name):
            return ctx.enter_context(nc.psum_tensor(f"e{layer}_" + name, [P, BLK], F32))
        turned = pst("turned")
        back = pst("back")
        part_ps = [pst(f"part_ps{i}") for i in range(2)]
        hot_ps = [pst(f"hot_ps{i}") for i in range(2)]
        spread_ps = [pst(f"spread_ps{i}") for i in range(2)]
        (ix_ready, cell_added, scored, t_turned, fwd, peaked, t_back, shift_done, prob, mask_done, weighted,
         zeroed, one_set, passed, pe_passed, hot, hot_turned, hot_copied, staged_in, staged_out) = sems(
            nc, ctx, *(f"e{layer}_" + n for n in (
                "ix_ready", "cell_added", "scored", "t_turned", "fwd", "peaked", "t_back", "shift_done",
                "prob", "mask_done", "weighted", "zeroed", "one_set", "passed", "pe_passed", "hot", "hot_turned",
                "hot_copied", "staged_in", "staged_out")))
        chunk_summed = sems(nc, ctx, *(f"e{layer}_chunk_summed{b}" for b in range(RING)))
        evacuated = sems(nc, ctx, *(f"e{layer}_evacuated{s}" for s in range(2)))
        src_in = sems(nc, ctx, *(f"e{layer}_src_in{b}" for b in range(RING)))
        win_in = sems(nc, ctx, *(f"e{layer}_win_in{b}" for b in range(2)))
        spread = sems(nc, ctx, *(f"e{layer}_spread{s}" for s in range(2)))
        used = sems(nc, ctx, *(f"e{layer}_used{s}" for s in range(2)))
        block = ctx.enter_context(nc.Block(f"edges{layer}"))

        LAST = NG // RING - 1

        def ticks(eng, tick):
            def at(it, b, first, last):
                before = (it, b - 1) if b else None if first else (it - 1, RING - 1)
                after = (it, b + 1) if b + 1 < RING else None if last else (it + 1, 0)
                tick(before, (it, b), after)

            for b in range(RING):
                at(0, b, True, False)
            with eng.Fori(1, LAST) as it:
                for b in range(RING):
                    at(it, b, False, False)
            for b in range(RING):
                at(LAST, b, False, True)

        @block.sync
        def _(sp):
            sp.wait_ge(staged_in, 16 * (PT + 1))
            sp.dma_start(by_part.rearrange("(t p) d -> p t d", p=P), staged).then_inc(staged_out, 16)
            sp.wait_ge(staged_out, 16)
            with sp.Fori(0, NG // RING) as it:
                for b in range(RING):
                    g = RING * it + b
                    sp.wait_ge(scored, g + 1)
                    for j in range(G):
                        at = sp.value_load(keep["offset"][0:1, bass.ds(g * G + j, 1)], min_val=0, max_val=PARTS)
                        sp.dma_start(window[:, b % 2, j, :], by_part[bass.ds(at, P), :]).then_inc(win_in[b % 2], 16)

        @block.gpsimd
        def _(pool):
            first_col, per_group = scatters
            for t in range(PT + 1):
                nc.gpsimd.indirect_dma_start(
                    staged[:, t, :], None, by_node,
                    bass.IndirectOffsetOnAxis(ap=keep["part_node"][:, t:t + 1], axis=0)).then_inc(staged_in, 16)
            pool.wait_ge(one_set, 1)
            nc.gpsimd.dma_start(started[:, :], one16[:, :]).then_inc(cell_added, 16)
            with pool.Fori(0, NG // RING) as it:
                for b in range(RING):
                    g = RING * it + b
                    pool.wait_ge(chunk_summed[b], G * it + 1)
                    nc.gpsimd.tensor_copy(src_ix[:, b, :], keep["src"][:, bass.ds(g * G, G)]).then_inc(ix_ready, 1)
                    nc.gpsimd.tensor_copy(cell_ix[:, b, 0:per_group],
                                          keep["cell_once"][:, bass.ds(g * per_group + first_col, per_group)]).then_inc(ix_ready, 1)
                    pool.wait_ge(ix_ready, 2 * (g + 1))
                    pool.sem_inc(passed, 1)
                    done = 0
                    for j in range(G):
                        nc.gpsimd.indirect_dma_start(
                            from_src[:, b, j, :], None, by_src,
                            bass.IndirectOffsetOnAxis(ap=src_ix[:, b, j:j + 1], axis=0)).then_inc(src_in[b], 16)
                        if (j + 1) * per_group // G > done:
                            pool.wait_ge(cell_added, 16 * per_group * g + 16 * (done + 1))
                            pool.sem_inc(passed, 1)
                            nc.gpsimd.indirect_dma_start(
                                scratch["adj"], bass.IndirectOffsetOnAxis(ap=cell_ix[:, b, done:done + 1], axis=0),
                                one16[:, 0:1], None, compute_op=ALU.add).then_inc(cell_added, 16)
                            done += 1
            pool.wait_ge(cell_added, 16 * (per_group * NG + 1))

        @block.vector
        def _(v):
            nc.vector.tensor_copy(one16[:, :], keep["count_one"][:, :]).then_inc(one_set, 1)
            nc.vector.memset(small[:, :, :, 0:COL_SIZE], 0.0).then_inc(zeroed, 1)
            nc.vector.memset(small[:, :, :, COL_SIZE:SMALL], 1.0).then_inc(zeroed, 1)
            nc.vector.memset(keep["sums"][:, KH, :], 0.0).then_inc(zeroed, 1)
            v.wait_ge(staged_out, 16)
            nc.vector.memset(keep["sums"][:, 0:KH, :], 0.0).then_inc(zeroed, 1)
            v.wait_ge(zeroed, 4)

            def spot_slots(it, b):
                v.wait_ge(chunk_summed[b], G * it + 1)
                nc.vector.tensor_tensor(onehot[:, b, :, :], keep["iota"][:, :].unsqueeze(1).to_broadcast([P, G, P]),
                                        keep["slot"][:, bass.ds((RING * it + b) * G, G)].unsqueeze(2).to_broadcast([P, G, P]),
                                        ALU.is_equal).then_inc(hot, 1)

            def tick(before, group, after):
                it, b = group
                g, r = RING * it + b, b % 2
                pair = RING // 2 * it + b // 2
                cols = bass.ds(g * G, G)
                v.wait_ge(chunk_summed[(b - 2) % RING], G * it + (G if b >= 2 else 0) + 1)
                v.wait_ge(src_in[b], 16 * G * it + 16 * G)
                if layer == 0:
                    for i in range(PAIRS):
                        v.wait_ge(spread[i % 2], PAIRS // 2 * g + i // 2 + 1)
                        k_rows = from_src[:, b, 2 * i:2 * i + 2, D:2 * D]
                        nc.vector.tensor_tensor(k_rows, k_rows, spread_ps[i % 2][:, :].rearrange("p (j d) -> p j d", j=2),
                                                ALU.mult).then_inc(used[i % 2], 1)
                    for i in range(2):
                        v.wait_ge(used[i], PAIRS // 2 * (g + 1) + 1)
                    nc.vector.tensor_reduce(score[:, r, :].rearrange("p (j h) -> p j h", h=H),
                                            from_src[:, b, :, D:2 * D].rearrange("p j (h d) -> p j h d", h=H),
                                            AX_X, ALU.add).then_inc(scored, 1)
                else:
                    v.wait_ge(spread[r], pair + 1)
                    nc.vector.tensor_tensor(raw_score[:, r, :].rearrange("p (j h) -> p j h", h=H), from_src[:, b, :, D:D + H],
                                            spread_ps[r][:, 0:G * H].rearrange("p (j h) -> p j h", h=H), ALU.add).then_inc(used[r], 1)
                    v.wait_ge(used[r], pair + 2)
                    nc.vector.scalar_tensor_tensor(out=score[:, r, :], in0=raw_score[:, r, :], scalar=0.2,
                                                   in1=raw_score[:, r, :], op0=ALU.mult, op1=ALU.max).then_inc(scored, 1)
                v.wait_ge(t_turned, g + 1)
                nc.vector.tensor_tensor_scan(running[:, :], keep["link"][:, g, 0:P], turned[0:G * H, 0:P],
                                             -FAR, ALU.add, ALU.max).then_inc(fwd, 1)
                v.wait_ge(fwd, g + 1)
                nc.vector.tensor_tensor_scan(peak[:, r, ::-1], keep["link_back"][:, g, :], running[:, ::-1],
                                             -FAR, ALU.add, ALU.max).then_inc(peaked, 1)
                if after:
                    spot_slots(*after)
                v.wait_ge(t_back, g + 1)
                nc.vector.tensor_tensor(shifted[:, r, :], score[:, r, :], back[:, 0:G * H], ALU.subtract).then_inc(shift_done, 1)
                nc.vector.tensor_tensor(small[:, r, :, COL_MAX:COL_MAX + H],
                                        back[:, 0:G * H].rearrange("p (j h) -> p j h", h=H),
                                        keep["first"][:, cols].unsqueeze(2).to_broadcast([P, G, H]), ALU.mult).then_inc(mask_done, 1)
                nc.vector.tensor_copy(small[:, r, :, COL_NODE:COL_NODE + H],
                                      keep["node"][:, cols].unsqueeze(2).to_broadcast([P, G, H])).then_inc(mask_done, 1)
                v.wait_ge(prob, g + 1)
                nc.vector.tensor_tensor(
                    from_src[:, b, :, 0:D].rearrange("p j (h d) -> p j h d", h=H),
                    from_src[:, b, :, 0:D].rearrange("p j (h d) -> p j h d", h=H),
                    small[:, r, :, 0:H].unsqueeze(3).to_broadcast([P, G, H, DK]), ALU.mult).then_inc(weighted, 1)

            spot_slots(0, 0)
            ticks(v, tick)

        @block.tensor
        def _(pe):
            for b in range(RING):
                pe.sem_inc(chunk_summed[b], 1)
            for s in range(2):
                pe.sem_inc(used[s], 1)
                pe.sem_inc(scored, 1)

            def turn_slots(it, b):
                g = RING * it + b
                pe.wait_ge(hot, g + 1)
                for q in range(2):
                    pe.wait_ge(hot_copied, 2 * g + q + 1)
                    pe.sem_inc(pe_passed, 1)
                    for j in range(4 * q, 4 * q + 4):
                        mm = nc.tensor.transpose(hot_ps[q][:, j % 4 * P:(j % 4 + 1) * P], onehot[:, b, j, :], keep["ident"][:, :])
                    mm.then_inc(hot_turned, 1)

            def spread_windows(it, b):
                g, r = RING * it + b, b % 2
                pair = RING // 2 * it + b // 2
                pe.wait_ge(win_in[r], 16 * G * pair + 16 * G)
                for j in range(G):
                    if j % 4 == 0:
                        pe.wait_ge(hot_copied, 2 * g + j // 4 + 3)
                    if layer == 0:
                        s = j // 2 % 2
                        if j % 2 == 0:
                            pe.wait_ge(used[s], PAIRS // 2 * g + j // 4 + 1)
                        to = spread_ps[s][:, j % 2 * D:(j % 2 + 1) * D]
                    else:
                        s = r
                        if j == 0:
                            pe.wait_ge(used[s], pair + 1)
                        to = spread_ps[s][:, j * H:(j + 1) * H]
                    mm = nc.tensor.matmul(to, onehot_t[:, r, j, :], window[:, r, j, :], start=True, stop=True)
                    if (layer == 0 and j % 2) or j == G - 1:
                        mm.then_inc(spread[s], 1)

            def turn_scores(it, b):
                g, r = RING * it + b, b % 2
                pe.wait_ge(scored, g + 3)
                pe.sem_inc(pe_passed, 1)
                nc.tensor.transpose(turned[0:G * H, 0:P], score[:, r, :], keep["ident"][:, :]).then_inc(t_turned, 1)

            def turn_peaks(it, b):
                g, r = RING * it + b, b % 2
                pe.wait_ge(peaked, g + 1)
                pe.sem_inc(pe_passed, 1)
                nc.tensor.transpose(back[:, 0:G * H], peak[:, r, :], keep["ident"][0:G * H, 0:G * H]).then_inc(t_back, 1)

            def sum_parts(it, b, chunks):
                g, r = RING * it + b, b % 2
                if chunks[0] == 0:
                    pe.wait_ge(weighted, g + 1)
                    pe.wait_ge(mask_done, 2 * g + 2)
                for j in chunks:
                    s = j % 2
                    pe.wait_ge(evacuated[s], G // 2 * g + j // 2 + 1)
                    for k in range(KH):
                        nc.tensor.matmul(part_ps[s][:, k * P:(k + 1) * P], from_src[:, b, j, k * P:(k + 1) * P],
                                         onehot[:, b, j, :], start=True, stop=True)
                    nc.tensor.matmul(part_ps[s][0:SMALL, KH * P:KH * P + P], small[:, r, j, :], onehot[:, b, j, :],
                                     start=True, stop=True).then_inc(chunk_summed[b], 1)

            def tick(before, group, after):
                spread_windows(*group)
                if before:
                    sum_parts(*before, range(0, FIRST))
                turn_scores(*group)
                if before:
                    sum_parts(*before, range(FIRST, SECOND))
                turn_peaks(*group)
                if before:
                    sum_parts(*before, range(SECOND, G))
                if after:
                    turn_slots(*after)
                if layer == 1:
                    for _ in range(2):
                        nc.tensor.matmul(turned[:, :], keep["ident"][:, :], onehot[:, group[1], 0:4, :].rearrange("p j e -> p (j e)"),
                                         start=True, stop=True)

            turn_slots(0, 0)
            ticks(pe, tick)
            sum_parts(LAST, RING - 1, range(G))

        @block.scalar
        def _(act):
            act.wait_ge(zeroed, 4)
            for s in range(2):
                act.sem_inc(evacuated[s], 1)
                act.sem_inc(hot_copied, 1)

            def copy_turned(it, b):
                g, r = RING * it + b, b % 2
                for q in range(2):
                    act.wait_ge(hot_turned, 2 * g + q + 1)
                    nc.scalar.activation(onehot_t[:, r, 4 * q:4 * q + 4, :], hot_ps[q][:, :].rearrange("p (j e) -> p j e", j=4),
                                         ACT.Copy).then_inc(hot_copied, 1)

            def weigh(it, b):
                g, r = RING * it + b, b % 2
                act.wait_ge(shift_done, g + 1)
                nc.scalar.activation(small[:, r, :, 0:H], shifted[:, r, :].rearrange("p (j h) -> p j h", h=H),
                                     ACT.Exp, scale=scale).then_inc(prob, 1)

            def copy_sums(it, b, chunks):
                g = RING * it + b
                starts = {j: act.value_load(keep["offset"][0:1, bass.ds(g * G + j, 1)], min_val=0, max_val=PARTS) for j in chunks}
                for j in chunks:
                    s = j % 2
                    act.wait_ge(chunk_summed[b], G * it + j + 2)
                    act.wait_ge(evacuated[1 - s], G // 2 * g + (j + 1) // 2 + 1)
                    nc.scalar.activation(keep["sums"][:, :, bass.ds(starts[j], P)],
                                         part_ps[s][:, 0:(KH + 1) * P].rearrange("p (k e) -> p k e", k=KH + 1),
                                         ACT.Copy).then_inc(evacuated[s], 1)

            def tick(before, group, after):
                if before:
                    copy_sums(*before, range(0, SECOND))
                weigh(*group)
                if before:
                    copy_sums(*before, range(SECOND, G))
                if after:
                    copy_turned(*after)

            copy_turned(0, 0)
            ticks(act, tick)
            copy_sums(LAST, RING - 1, range(G))


def add_repeated(nc, keep, scratch):
    STEP = 8
    PAST = float(1 << 25)
    with Phase(nc) as ctx:
        def sb(name, shape, dt):
            return ctx.enter_context(nc.sbuf_tensor("ar_" + name, shape, dt))
        cells = sb("cells", [P, C], F32)
        before = sb("before", [P, P], F32)
        diagonal = sb("diagonal", [P, P], F32)
        same = sb("same", [P, P], F32)
        earlier = sb("earlier", [P, P], F32)
        number = sb("number", [P, 1], F32)
        number_before = sb("number_before", [P, 1], F32)
        moved_by = sb("moved_by", [P, 1], F32)
        amount = sb("amount", [P, 1], F16)
        index = sb("index", [P, 1], I32)
        started = sb("started", [P, 1], I32)
        row_ps = ctx.enter_context(nc.psum_tensor("ar_row_ps", [P, P], F32))
        const, cells_set, step, row_made, added, passed = sems(
            nc, ctx, "ar_const", "ar_cells_set", "ar_step", "ar_row_made", "ar_added", "ar_passed")
        block = ctx.enter_context(nc.Block("repeated"))

        @block.gpsimd
        def _(pool):
            repeats = pool.value_load(keep["repeats"][0:1, 0:1], min_val=0, max_val=C * P)
            with pool.If(repeats > 0):
                nc.gpsimd.memset(before[:, :], 1.0).then_inc(const, 1)
                pool.wait_ge(const, 1)
                nc.gpsimd.affine_select(out=before[:, :], in_=before[:, :], compare_op=ALU.is_gt,
                                        fill=0.0, base=0, pattern=[[-1, P]], channel_multiplier=1).then_inc(const, 1)
                nc.gpsimd.dma_start(started[:, :], keep["repeats"][:, :]).then_inc(added, 16)
                with pool.Fori(0, C) as t:
                    pool.wait_ge(step, STEP * t + STEP)
                    pool.sem_inc(passed, 1)
                    nc.gpsimd.indirect_dma_start(
                        scratch["adj"], bass.IndirectOffsetOnAxis(ap=index[:, 0:1], axis=0), amount[:, 0:1], None,
                        bounds_check=NP * AW - 1, oob_is_err=False, compute_op=ALU.add).then_inc(added, 16)
                pool.wait_ge(added, 16 * (C + 1))

        @block.tensor
        def _(pe):
            repeats = pe.value_load(keep["repeats"][0:1, 0:1], min_val=0, max_val=C * P)
            with pe.If(repeats > 0):
                with pe.Fori(0, C) as t:
                    pe.wait_ge(step, STEP * t + 1)
                    nc.tensor.matmul(row_ps[:, :], keep["ones"][:, :], diagonal[:, :], start=True, stop=True).then_inc(row_made, 1)

        @block.vector
        def _(v):
            repeats = v.value_load(keep["repeats"][0:1, 0:1], min_val=0, max_val=C * P)
            with v.If(repeats > 0):
                nc.vector.tensor_copy(cells[:, :], keep["cell"][:, :]).then_inc(cells_set, 1)
                v.wait_ge(cells_set, 1)
                v.wait_ge(const, 2)
                with v.Fori(0, C) as t:
                    v.wait_ge(added, 16 * t + 16)
                    column = cells[:, bass.ds(t, 1)]
                    nc.vector.tensor_tensor(diagonal[:, :], keep["ident"][:, :], column.to_broadcast([P, P]), ALU.mult).then_inc(step, 1)
                    v.wait_ge(row_made, t + 1)
                    nc.vector.tensor_tensor(same[:, :], row_ps[:, :], column.to_broadcast([P, P]), ALU.is_equal).then_inc(step, 1)
                    v.wait_ge(step, STEP * t + 2)
                    nc.vector.tensor_reduce(number[:, :], same[:, :], AX_X, ALU.add).then_inc(step, 1)
                    nc.vector.tensor_tensor(earlier[:, :], same[:, :], before[:, :], ALU.mult).then_inc(step, 1)
                    v.wait_ge(step, STEP * t + 4)
                    nc.vector.tensor_reduce(number_before[:, :], earlier[:, :], AX_X, ALU.add).then_inc(step, 1)
                    v.wait_ge(step, STEP * t + 5)
                    nc.vector.tensor_scalar(moved_by[:, :], number_before[:, :], 0.0, PAST, ALU.is_gt, ALU.mult).then_inc(step, 1)
                    v.wait_ge(step, STEP * t + 6)
                    nc.vector.tensor_tensor(index[:, :], moved_by[:, :], column, ALU.add).then_inc(step, 1)
                    nc.vector.tensor_copy(amount[:, :], number[:, :]).then_inc(step, 1)




def merge_parts(nc, ins, keep, layer, weight, out_rows, scale):
    WIDE = D if weight is not None else D + 1
    TILES = BLK // P
    with Phase(nc) as ctx:
        def sb(name, shape, dt):
            return ctx.enter_context(nc.sbuf_tensor(f"m{layer}_" + name, shape, dt))
        w_out = sb("w_out", [P, KH, D], F32)
        joined = sb("joined", [P, PARTS], BF16)
        joined_rows = sb("joined_rows", [H, PARTS + 1], F32)
        peak = sb("peak", [H, PARTS], F32)
        link = sb("link", [H, PARTS + 1], F32)
        work = sb("work", [H, PARTS], F32)
        top = sb("top", [H, PARTS], F32)
        blocked = sb("blocked", [H * NB, BLK], F32)
        rows = sb("rows", [P, 4, WIDE], F32)
        size = sb("size", [1, PARTS], F32)
        degree = sb("degree", [1, PARTS], F32)
        last = sb("last", [P, 2, PT], F32)
        index = sb("index", [P, PT], I32)

        def pst(name):
            return ctx.enter_context(nc.psum_tensor(f"m{layer}_" + name, [P, BLK], F32))
        wide_ps = [pst(f"wide_ps{i}") for i in range(4)]
        row_ps = [pst(f"row_ps{i}") for i in range(2)]
        number_ps = pst("number_ps")
        next_ps = pst("next_ps")
        sums, side = keep["sums"], keep["sums"][:, KH, :]
        nodes = side[COL_NODE:COL_NODE + H, :]
        (w_in, peak_set, ends_set, rows_joined, linked, joined_wide, joined_set, running, top_set, below, expd, weight_sum, summed_up,
         total_blocked, clipped, inverted, inverse_in, wide, scaled, size_set, degree_set, added, wide_inverse, divided, index_turned, index_set,
         projected, out_copied) = sems(
            nc, ctx, *(f"m{layer}_" + n for n in (
                "w_in", "peak_set", "ends_set", "rows_joined", "linked", "joined_wide", "joined_set", "running", "top_set",
                "below", "expd", "weight_sum", "summed_up", "total_blocked", "clipped", "inverted", "inverse_in", "wide",
                "scaled", "size_set", "degree_set", "added", "wide_inverse", "divided", "index_turned", "index_set", "projected", "out_copied")))
        stored = sems(nc, ctx, *(f"m{layer}_stored{i}" for i in range(4)))
        block = ctx.enter_context(nc.Block(f"merge{layer}"))

        def cols(b):
            return slice(b * BLK, (b + 1) * BLK)

        @block.sync
        def _(sp):
            if weight is not None:
                sp.dma_start(w_out[:, :, :], ins[weight].rearrange("(k p) o -> p k o", p=P)).then_inc(w_in, 16)
            sp.wait_ge(summed_up, 1)
            for h in range(H):
                sp.dma_start(blocked[h * NB:(h + 1) * NB, :], top[h:h + 1, :]).then_inc(total_blocked, 16)
            sp.wait_ge(inverted, 1)
            for h in range(H):
                sp.dma_start(work[h:h + 1, :], blocked[h * NB:(h + 1) * NB, :]).then_inc(inverse_in, 16)

        @block.scalar
        def _(act):
            nc.scalar.activation(peak[:, :], side[COL_MAX:COL_MAX + H, 0:PARTS], ACT.Copy).then_inc(peak_set, 1)
            if weight is None:
                nc.scalar.activation(size[:, :], side[COL_SIZE:COL_SIZE + 1, 0:PARTS], ACT.Copy).then_inc(size_set, 1)
            act.wait_ge(below, 1)
            nc.scalar.activation(peak[:, :], work[:, :], ACT.Exp, scale=scale).then_inc(expd, 1)
            for b in range(NB):
                act.wait_ge(joined_wide, b + 1)
                nc.scalar.activation(joined[:, cols(b)], wide_ps[b % 4][:, :], ACT.Copy).then_inc(joined_set, 1)
            for t in range(PT):
                act.wait_ge(projected, t + 1)
                if t >= 4:
                    act.wait_ge(stored[t % 4], 16 * (t // 4))
                nc.scalar.activation(rows[:, t % 4, :], row_ps[t % 2][:, 0:WIDE], ACT.Copy).then_inc(out_copied, 1)

        @block.tensor
        def _(pe):
            pe.wait_ge(rows_joined, 1)
            for b in range(NB):
                if b >= 4:
                    pe.wait_ge(joined_set, b - 3)
                nc.tensor.matmul(wide_ps[b % 4][:, :], keep["ones"][0:1, :], joined_rows[0:1, cols(b)],
                                 start=True, stop=True).then_inc(joined_wide, 1)
            for t in range(PT):
                mm = nc.tensor.matmul(number_ps[:, t:t + 1], nodes[0:1, t * P:(t + 1) * P], keep["ones"][COL_NODE:COL_NODE + 1, 0:1],
                                      start=True, stop=True)
            mm.then_inc(index_turned, 1)
            for t in range(PT):
                mm = nc.tensor.matmul(next_ps[:, t:t + 1], joined_rows[0:1, t * P + 1:(t + 1) * P + 1],
                                      keep["ones"][0:1, 0:1], start=True, stop=True)
            mm.then_inc(index_turned, 1)
            pe.wait_ge(expd, 1)
            pe.wait_ge(joined_set, NB)
            for n in range(KH * NB):
                if n >= 4:
                    pe.wait_ge(scaled, n - 3)
                nc.tensor.matmul(wide_ps[n % 4][:, :], keep["hsel"][:, n % KH * P:(n % KH + 1) * P], peak[:, cols(n // KH)],
                                 start=True, stop=True).then_inc(wide, 1)
            pe.wait_ge(scaled, KH * NB)
            pe.wait_ge(inverse_in, 16 * H)

            def spread_inverse(b):
                for n in range(KH * b, KH * (b + 1)):
                    if n >= 4:
                        pe.wait_ge(divided, n - 3)
                    nc.tensor.matmul(wide_ps[n % 4][:, :], keep["hsel"][:, n % KH * P:(n % KH + 1) * P], work[:, cols(b)],
                                     start=True, stop=True).then_inc(wide_inverse, 1)

            if weight is None:
                pe.wait_ge(degree_set, 1)
            spread_inverse(0)
            spread_inverse(1)
            if weight is not None:
                pe.wait_ge(w_in, 16)
            for t in range(PT):
                if t % TILES == 0:
                    pe.wait_ge(divided, KH * (t // TILES + 1))
                if t >= 2:
                    pe.wait_ge(out_copied, t - 1)
                for k in range(KH):
                    if weight is None:
                        nc.tensor.transpose(row_ps[t % 2][:, k * P:(k + 1) * P], sums[:, k, t * P:(t + 1) * P],
                                                 keep["ident"][:, :])
                    else:
                        mm = nc.tensor.matmul(row_ps[t % 2][:, 0:D], sums[:, k, t * P:(t + 1) * P], w_out[:, k, :],
                                              start=(k == 0), stop=(k == KH - 1))
                if weight is None:
                    mm = nc.tensor.matmul(row_ps[t % 2][:, D:WIDE], degree[:, t * P:(t + 1) * P], keep["ones"][0:1, 0:1],
                                          start=True, stop=True)
                mm.then_inc(projected, 1)
                if t % TILES == TILES - 1 and t // TILES + 2 < NB:
                    spread_inverse(t // TILES + 2)

        @block.vector
        def _(v):
            nc.vector.memset(joined_rows[:, 0:1], 0.0).then_inc(ends_set, 1)
            nc.vector.memset(joined_rows[:, PARTS:PARTS + 1], 0.0).then_inc(ends_set, 1)
            nc.vector.tensor_tensor(joined_rows[:, 1:PARTS], nodes[:, 1:PARTS], nodes[:, 0:PARTS - 1], ALU.is_equal).then_inc(rows_joined, 1)
            v.wait_ge(rows_joined, 1)
            v.wait_ge(ends_set, 2)
            nc.vector.tensor_scalar(link[:, :], joined_rows[:, :], -1.0, FAR, ALU.add, ALU.mult).then_inc(linked, 1)
            v.wait_ge(linked, 1)
            v.wait_ge(peak_set, 1)
            nc.vector.tensor_tensor_scan(work[:, :], link[:, 0:PARTS], peak[:, :], -FAR, ALU.add, ALU.max).then_inc(running, 1)
            v.wait_ge(running, 1)
            nc.vector.tensor_tensor_scan(top[:, ::-1], link[:, PARTS:0:-1], work[:, ::-1], -FAR, ALU.add, ALU.max).then_inc(top_set, 1)
            v.wait_ge(top_set, 1)
            nc.vector.tensor_tensor(work[:, :], peak[:, :], top[:, :], ALU.subtract).then_inc(below, 1)
            v.wait_ge(index_turned, 2)
            nc.vector.tensor_copy(last[:, 0, :], number_ps[:, 0:PT]).then_inc(index_set, 1)
            nc.vector.tensor_copy(last[:, 1, :], next_ps[:, 0:PT]).then_inc(index_set, 1)
            v.wait_ge(index_set, 2)
            nc.vector.scalar_tensor_tensor(out=last[:, 1, :], in0=last[:, 0, :], scalar=0.0, in1=last[:, 1, :],
                                           op0=ALU.is_equal, op1=ALU.add).then_inc(index_set, 1)
            v.wait_ge(index_set, 3)
            nc.vector.scalar_tensor_tensor(out=last[:, 0, :], in0=last[:, 1, :], scalar=8192.0, in1=last[:, 0, :],
                                           op0=ALU.mult, op1=ALU.add).then_inc(index_set, 1)
            v.wait_ge(index_set, 4)
            nc.vector.tensor_scalar(index[:, :], last[:, 0, :], -1.0, None, ALU.add).then_inc(index_set, 1)
            v.wait_ge(expd, 1)
            nc.vector.tensor_tensor(work[:, :], side[0:H, 0:PARTS], peak[:, :], ALU.mult).then_inc(weight_sum, 1)
            v.wait_ge(weight_sum, 1)
            nc.vector.tensor_tensor_scan(top[:, :], joined_rows[:, 0:PARTS], work[:, :], 0.0, ALU.mult, ALU.add).then_inc(summed_up, 1)
            if weight is None:
                v.wait_ge(size_set, 1)
                nc.vector.tensor_tensor_scan(degree[:, :], joined_rows[0:1, 0:PARTS], size[:, :], 0.0, ALU.mult, ALU.add).then_inc(degree_set, 1)
            for n in range(KH * NB):
                part = sums[:, n % KH, cols(n // KH)]
                v.wait_ge(wide, n + 1)
                nc.vector.tensor_tensor(part, part, wide_ps[n % 4][:, :], ALU.mult).then_inc(scaled, 1)
            v.wait_ge(total_blocked, 16 * H)
            nc.vector.tensor_scalar(blocked[:, :], blocked[:, :], 1e-30, None, ALU.max).then_inc(clipped, 1)
            v.wait_ge(clipped, 1)
            nc.vector.reciprocal(blocked[:, :], blocked[:, :]).then_inc(inverted, 1)
            v.wait_ge(scaled, KH * NB)
            v.wait_ge(joined_set, NB)
            for k in range(KH):
                nc.vector.tensor_tensor_scan(sums[:, k, 0:PARTS], joined[:, :], sums[:, k, 0:PARTS], 0.0, ALU.mult, ALU.add).then_inc(added, 1)
            v.wait_ge(added, KH)
            for n in range(KH * NB):
                part = sums[:, n % KH, cols(n // KH)]
                v.wait_ge(wide_inverse, n + 1)
                nc.vector.tensor_tensor(part, part, wide_ps[n % 4][:, :], ALU.mult).then_inc(divided, 1)

        @block.gpsimd
        def _(pool):
            pool.wait_ge(index_set, 5)
            for t in range(PT):
                pool.wait_ge(out_copied, t + 1)
                nc.gpsimd.indirect_dma_start(
                    out_rows, bass.IndirectOffsetOnAxis(ap=index[:, t:t + 1], axis=0), rows[:, t % 4, :], None,
                    bounds_check=N - 1, oob_is_err=False).then_inc(stored[t % 4], 16)
            for i in range(4):
                pool.wait_ge(stored[i], 16 * (PT // 4))


def residual_norm(nc, ins, keep, scratch, layer, add=None, added_t=None, bias=None, x_from=None, turned_to=None, rows_to=None):
    wide = D if add is None else add.shape[1]
    with Phase(nc) as ctx:
        def sb(name, shape, dt):
            return ctx.enter_context(nc.sbuf_tensor(f"n{layer}_" + name, shape, dt))

        def pst(name):
            return ctx.enter_context(nc.psum_tensor(f"n{layer}_" + name, [P, BLK], F32))
        more = sb("more", [P, NT, wide], F32) if add is not None else None
        bias_all = sb("bias_all", [P, D], F32)
        stats = sb("stats", [P, NT, 6], F32)
        mean_var = sb("mean_var", [P, NT, 2], F32)
        std = sb("std", [P, NT], F32)
        shift = sb("shift", [P, NT], F32)
        inverse = sb("inverse", [P, NT], F32)
        inverse_rows = sb("inverse_rows", [NT, P], F32)
        in_ps = [pst(f"in_ps{i}") for i in range(3)]
        out_ps = [pst(f"out_ps{i}") for i in range(3)]
        inverse_ps = ctx.enter_context(nc.psum_tensor(f"n{layer}_inverse_ps", [NT, P], F32))
        x = keep["x"]
        (bias_in, in_turned, summed, biased, stat, aggr, variance, rooted, inv, shifted, normed, out_turned, out_copied,
         clipped, inverted, inverse_turned, rows_copied, inverse_stored, rows_stored) = sems(
            nc, ctx, *(f"n{layer}_" + n for n in (
                "bias_in", "in_turned", "summed", "biased", "stat", "aggr", "variance", "rooted", "inv", "shifted", "normed",
                "out_turned", "out_copied", "clipped", "inverted", "inverse_turned", "rows_copied", "inverse_stored",
                "rows_stored")))
        loaded = sems(nc, ctx, *(f"n{layer}_loaded{s}" for s in range(NSLAB)))
        loads = (add is not None) + (x_from is not None)
        block = ctx.enter_context(nc.Block(f"norm{layer}"))

        def tiles(s):
            return range(s * SLAB, (s + 1) * SLAB)

        def by_slab(of):
            return of.rearrange("(s t p) d -> s p t d", s=NSLAB, p=P)

        @block.sync
        def _(sp):
            for s in range(NSLAB):
                if x_from is not None:
                    sp.dma_start(x[:, s * SLAB:(s + 1) * SLAB, :], by_slab(x_from)[s]).then_inc(loaded[s], 16)
                if add is not None:
                    sp.dma_start(more[:, s * SLAB:(s + 1) * SLAB, :], by_slab(add)[s]).then_inc(loaded[s], 16)
                if s == 0 and bias is not None:
                    of = ins[bias]
                    sp.dma_start(bias_all[:, :], bass.AP(tensor=of.tensor, offset=of.offset,
                                                         ap=[[0, P]] + [list(a) for a in of.ap])).then_inc(bias_in, 16)
            if rows_to is not None:
                stores = 0
                for s in range(NSLAB):
                    sp.wait_ge(normed, SLAB * (s + 1))
                    last = min((s + 1) * SLAB, rows_to.shape[0] // P)
                    sp.dma_start(rows_to[s * SLAB * P:last * P, :].rearrange("(t p) d -> p t d", p=P),
                                 x[:, s * SLAB:last, :]).then_inc(rows_stored, 16)
                    stores += 1
                    if last < (s + 1) * SLAB:
                        sp.dma_start(rows_to[last * P:, :], x[0:rows_to.shape[0] - last * P, last, :]).then_inc(rows_stored, 16)
                        stores += 1
                sp.wait_ge(rows_stored, 16 * stores)
            if wide > D:
                sp.wait_ge(rows_copied, 1)
                sp.dma_start(scratch["inv_degree"].rearrange("(t p) o -> t (p o)", p=P), inverse_rows[:, :]).then_inc(inverse_stored, 16)
                sp.wait_ge(inverse_stored, 16)

        @block.vector
        def _(v):
            def take_stats(s):
                slab = slice(s * SLAB, (s + 1) * SLAB)
                if loads:
                    v.wait_ge(loaded[s], 16 * loads)
                if add is not None:
                    nc.vector.tensor_tensor(x[:, slab, :], x[:, slab, :], more[:, slab, 0:D], ALU.add).then_inc(summed, 1)
                    v.wait_ge(summed, s + 1)
                if added_t is not None:
                    for t in tiles(s):
                        v.wait_ge(in_turned, t + 1)
                        nc.vector.tensor_tensor(x[:, t, :], x[:, t, :], in_ps[t % 3][:, 0:D], ALU.add).then_inc(summed, 1)
                    v.wait_ge(summed, SLAB * (s + 1))
                if bias is not None:
                    if s == 0:
                        v.wait_ge(bias_in, 16)
                    nc.vector.tensor_tensor(x[:, slab, :], x[:, slab, :], bias_all[:, :].unsqueeze(1).to_broadcast([P, SLAB, D]),
                                            ALU.add).then_inc(biased, 1)
                    v.wait_ge(biased, s + 1)
                for t in tiles(s):
                    nc.vector.bn_stats(stats[:, t, :], x[:, t, :]).then_inc(stat, 1)
                v.wait_ge(stat, SLAB * (s + 1))
                for t in tiles(s):
                    nc.vector.bn_aggr(mean_var[:, t, :], stats[:, t, :]).then_inc(aggr, 1)
                v.wait_ge(aggr, SLAB * (s + 1))
                nc.vector.tensor_scalar(std[:, slab], mean_var[:, slab, 1], EPS, None, ALU.add).then_inc(variance, 1)

            def make_shift(s):
                slab = slice(s * SLAB, (s + 1) * SLAB)
                v.wait_ge(rooted, s + 1)
                nc.vector.reciprocal(std[:, slab], std[:, slab]).then_inc(inv, 1)
                v.wait_ge(inv, s + 1)
                nc.vector.scalar_tensor_tensor(out=shift[:, slab], in0=mean_var[:, slab, 0], scalar=-1.0, in1=std[:, slab],
                                               op0=ALU.mult, op1=ALU.mult).then_inc(shifted, 1)

            take_stats(0)
            for s in range(1, NSLAB):
                take_stats(s)
                make_shift(s - 1)
            make_shift(NSLAB - 1)
            if wide > D:
                nc.vector.tensor_scalar(inverse[:, :], more[:, :, D], 1.0, FS, ALU.max, ALU.mult).then_inc(clipped, 1)
                v.wait_ge(clipped, 1)
                nc.vector.reciprocal(inverse[:, :], inverse[:, :]).then_inc(inverted, 1)

        @block.scalar
        def _(act):
            def root(s):
                slab = slice(s * SLAB, (s + 1) * SLAB)
                act.wait_ge(variance, s + 1)
                nc.scalar.activation(std[:, slab], std[:, slab], ACT.Sqrt).then_inc(rooted, 1)

            def normalise(s):
                act.wait_ge(shifted, s + 1)
                for t in tiles(s):
                    nc.scalar.activation(x[:, t, :], x[:, t, :], ACT.Identity, bias=shift[:, t:t + 1],
                                         scale=std[:, t:t + 1]).then_inc(normed, 1)

            def copy_turned(s):
                for t in tiles(s):
                    act.wait_ge(out_turned, t + 1)
                    nc.scalar.activation(turned_to[:, :, t * P:(t + 1) * P], out_ps[t % 3][:, 0:D].rearrange("p (k n) -> p k n", k=KH),
                                         ACT.Copy).then_inc(out_copied, 1)

            root(0)
            for s in range(NSLAB):
                if s + 1 < NSLAB:
                    root(s + 1)
                normalise(s)
                if turned_to is not None:
                    copy_turned(s)
            if wide > D:
                act.wait_ge(inverse_turned, 1)
                nc.scalar.activation(inverse_rows[:, :], inverse_ps[:, :], ACT.Copy).then_inc(rows_copied, 1)

        @block.tensor
        def _(pe):
            def turn_in(s):
                for t in tiles(s):
                    if t >= 3:
                        pe.wait_ge(summed, t - 2)
                    for k in range(KH):
                        mm = nc.tensor.transpose(in_ps[t % 3][:, k * P:(k + 1) * P], added_t[:, k, t * P:(t + 1) * P], keep["ident"][:, :])
                    mm.then_inc(in_turned, 1)

            def turn_out(s):
                for t in tiles(s):
                    pe.wait_ge(normed, t + 1)
                    if t >= 3:
                        pe.wait_ge(out_copied, t - 2)
                    for k in range(KH):
                        mm = nc.tensor.transpose(out_ps[t % 3][:, k * P:(k + 1) * P], x[:, t, k * P:(k + 1) * P], keep["ident"][:, :])
                    mm.then_inc(out_turned, 1)

            if added_t is not None:
                turn_in(0)
            for s in range(NSLAB):
                if added_t is not None and s + 1 < NSLAB:
                    turn_in(s + 1)
                if turned_to is not None:
                    turn_out(s)
            if wide > D:
                pe.wait_ge(inverted, 1)
                nc.tensor.transpose(inverse_ps[:, :], inverse[:, :], keep["ident"][:, :]).then_inc(inverse_turned, 1)




def tables_layer1(nc, ins, scratch, x_t):
    HEADS4, DH = 4, D // 4
    WIDE = D + 2 * H
    with Phase(nc) as ctx:
        def sb(name, shape, dt):
            return ctx.enter_context(nc.sbuf_tensor("t1_" + name, shape, dt))
        w_attn = sb("w_attn", [P, KH, D], F32)
        a_cols = sb("a_cols", [P, KH, 2 * H], F32)
        w_all = sb("w_all", [P, KH, WIDE], F32)
        out = sb("out", [P, 4, WIDE], F32)
        ps = [ctx.enter_context(nc.psum_tensor(f"t1_ps{i}", [P, BLK], F32)) for i in range(4)]
        fold_ps = ctx.enter_context(nc.psum_tensor("t1_fold_ps", [P, KH, 2 * H], F32))
        cleared, w_in, a_in, folded, fold_copied, summed, made = sems(
            nc, ctx, *("t1_" + n for n in ("cleared", "w_in", "a_in", "folded", "fold_copied", "summed", "made")))
        stored = sems(nc, ctx, *(f"t1_stored{i}" for i in range(4)))
        block = ctx.enter_context(nc.Block("tables1"))

        @block.sync
        def _(sp):
            sp.dma_start(w_attn[:, :, :], ins["L1_gnn_W_attn"].rearrange("(k p) i -> p k i", p=P)).then_inc(w_in, 16)
            sp.dma_start(w_all[:, :, 0:D], ins["L1_gnn_W_lin_t"].rearrange("(k p) o -> p k o", p=P)).then_inc(w_in, 16)
            sp.wait_ge(cleared, 1)
            a = ins["L1_gnn_a"]
            for h in range(HEADS4):
                rows = slice(h * DH % P, h * DH % P + DH)
                for side in range(2):
                    for twin in range(2):
                        col = side * H + 2 * h + twin
                        sp.dma_start(a_cols[rows, h * DH // P, col:col + 1],
                                     a[h, side * DH:(side + 1) * DH].rearrange("(d o) -> d o", o=1)).then_inc(a_in, 16)
            for t in range(NT):
                sp.wait_ge(made, t + 1)
                sp.dma_start(scratch["val"][t * P:(t + 1) * P, :], out[:, t % 4, 0:D + H]).then_inc(stored[t % 4], 16)
                sp.dma_start(scratch["alpha"][t * P:(t + 1) * P, :], out[:, t % 4, D + H:WIDE]).then_inc(stored[t % 4], 16)
            for i in range(4):
                sp.wait_ge(stored[i], 32 * len(range(i, NT, 4)))

        @block.tensor
        def _(pe):
            pe.wait_ge(w_in, 32)
            pe.wait_ge(a_in, 256)
            for k_in in range(KH):
                for k in range(KH):
                    mm = nc.tensor.matmul(fold_ps[:, k_in, :], w_attn[:, k, k_in * P:(k_in + 1) * P], a_cols[:, k, :],
                                          start=(k == 0), stop=(k == KH - 1))
            mm.then_inc(folded, 1)
            pe.wait_ge(fold_copied, 1)
            for t in range(NT):
                if t >= 4:
                    pe.wait_ge(made, t - 3)
                for k in range(KH):
                    mm = nc.tensor.matmul(ps[t % 4][:, 0:WIDE], x_t[:, k, t * P:(t + 1) * P], w_all[:, k, :],
                                          start=(k == 0), stop=(k == KH - 1))
                mm.then_inc(summed, 1)

        @block.vector
        def _(v):
            nc.vector.memset(a_cols[:, :, :], 0.0).then_inc(cleared, 1)
            v.wait_ge(folded, 1)
            nc.vector.tensor_copy(w_all[:, :, D:WIDE], fold_ps[:, :, :]).then_inc(fold_copied, 1)

        @block.scalar
        def _(act):
            for t in range(NT):
                act.wait_ge(summed, t + 1)
                if t >= 4:
                    act.wait_ge(stored[t % 4], 32 * (t // 4))
                nc.scalar.activation(out[:, t % 4, :], ps[t % 4][:, 0:WIDE], ACT.Copy).then_inc(made, 1)


GIN_LAYERS = 5
SAGE_LAYERS = 3
GIN_COLUMNS = ("L2_gnn_b1", "L2_gnn_g1", "L2_gnn_bt1", "L2_gnn_b2", "L2_gnn_bn_g", "L2_gnn_bn_b")
SAGE_COLUMNS = ("L3_gnn_b1l", "L3_gnn_b2l", "L3_gnn_b3l")


def load_degrees(nc, state, scratch):
    with Phase(nc) as ctx:
        loaded, = sems(nc, ctx, "ld_loaded")
        block = ctx.enter_context(nc.Block("degrees"))

        @block.sync
        def _(sp):
            of = scratch["inv_degree"]
            sp.dma_start(state["inv_degree"][:, :], bass.AP(tensor=of.tensor, offset=of.offset, ap=[[0, P], [1, AW]])).then_inc(loaded, 16)
            sp.wait_ge(loaded, 16)


def slabs_of(scratch):
    return scratch["adj"].rearrange("(s k p a c) o -> s a p k (c o)", s=NSLAB, k=SLAB, p=P, a=APASS)


def graph_layers(nc, ins, keep, scratch, state, kind):
    gin = kind == "gin"
    LAYERS = GIN_LAYERS if gin else SAGE_LAYERS
    COLS = len(GIN_COLUMNS if gin else SAGE_COLUMNS[:1])
    NBLK = 2 * APASS
    PROJ = 2 if gin else 1
    LAG = 3
    RT = 3
    with Phase(nc) as ctx:
        def sb(n, shape, dt):
            return ctx.enter_context(nc.sbuf_tensor(f"{kind}_{n}", shape, dt))

        def pst(n):
            return ctx.enter_context(nc.psum_tensor(f"{kind}_{n}", [P, BLK], F32))
        w = sb("w", [P, 2, KH, D], F32)
        columns = sb("columns", [P, COLS, KH], F32)
        floors = sb("floors", [P, LAYERS], F32)
        floor = sb("floor", [P, 2], F32)
        message = sb("message", [P, RT, D], F32)
        stats = sb("stats", [P, KH, NBLK, 6], F32)
        mean_var = sb("mean_var", [P, KH, 2], F32)
        std = sb("std", [P, KH], F32)
        gain = sb("gain", [P, KH], F32)
        shift = sb("shift", [P, KH], F32)
        own_all = sb("own_all", [P, LAYERS], F32)
        own = sb("own", [P, 1], F32)
        sum_ps = [pst(f"sum_ps{i}") for i in range(2 * KH)]
        proj_ps = [pst(f"proj_ps{i}") for i in range(2 * KH)]
        h_t, z_t, high, low, slab = (state[n] for n in ("h_t", "z_t", "high", "low", "slab"))
        (ready, own_in, own_set, floor_set, pool_floor_set, params_in, turned, message_made, high_done, low_done, floored,
         slab_used, evacuated, summed, moved, normed, stat, aggr, step, rooted, passed,
         v_passed, pool_passed) = sems(
            nc, ctx, *(f"{kind}_" + n for n in (
                "ready", "own_in", "own_set", "floor_set", "pool_floor_set", "params_in", "turned", "message_made",
                "high_done", "low_done", "floored", "slab_used", "evacuated", "summed", "moved", "normed", "stat", "aggr",
                "step", "rooted", "passed", "v_passed", "pool_passed")))
        slab_in = sems(nc, ctx, *(f"{kind}_slab_in{s}" for s in range(NSLAB)))
        h_done = sems(nc, ctx, *(f"{kind}_h_done{m}" for m in range(KH)))
        block = ctx.enter_context(nc.Block(f"{kind}_layers"))
        adj = slabs_of(scratch)

        USED0, EVAC0, H0 = NSLAB, 1, NBLK
        MOVED0 = 2 * KH + KH * NBLK

        def cols(b):
            return slice(b * AN, (b + 1) * AN)

        def wait_h(eng, l, b):
            if gin:
                for m in range(KH):
                    eng.wait_ge(h_done[m], NBLK * l + b + 1)
            else:
                eng.wait_ge(moved, KH * NBLK * l + 2 * KH + KH * (b + 1))

        @block.sync
        def _(sp):
            if gin:
                eps = ins["L2_gnn_eps"]
                sp.dma_start(own_all[:, :], bass.AP(tensor=eps.tensor, offset=eps.offset,
                                                    ap=[[0, P]] + [list(a) for a in eps.ap])).then_inc(own_in, 16)
            with sp.Fori(0, LAYERS) as l:
                for a in range(APASS):
                    for s in range(NSLAB):
                        sp.wait_ge(slab_used, NSLAB * APASS * l + NSLAB * a + s + 1)
                        sp.dma_start(slab[:, s, :, :], adj[s, a]).then_inc(slab_in[s], 16)
                    if a == 0:
                        wait_h(sp, l, NBLK - 1)
                        sp.dma_start(w[:, :, :, :], ins[kind + "_w"][bass.ds(l, 1)].rearrange("l i (k p) o -> p (l i) k o", p=P)).then_inc(params_in, 16)
                        sp.dma_start(columns[:, :, :], ins[kind + "_columns"][bass.ds(l, 1)].rearrange("l p c k -> p (l c) k")).then_inc(params_in, 16)

        @block.tensor
        def _(pe):
            pe.sem_inc(slab_used, USED0)
            pe.sem_inc(evacuated, EVAC0)
            pe.sem_inc(moved, MOVED0)
            for m in range(KH):
                pe.sem_inc(h_done[m], H0)

            def turn(l, t):
                wait_h(pe, l, min(NBLK - 1, ((t + 1) * P - 1) // AN) if gin else NBLK - 1)
                if t >= 2 * KH:
                    pe.wait_ge(message_made, NT * l + t - 2 * KH + 1)
                pe.sem_inc(passed, 1)
                for k in range(KH):
                    mm = nc.tensor.transpose(proj_ps[t % (2 * KH)][:, k * P:(k + 1) * P], h_t[:, k, t * P:(t + 1) * P],
                                             keep["ident"][:, :])
                mm.then_inc(turned, 1)

            def sum_tile(l, a, t):
                s, k = t // SLAB, t % SLAB
                if t == 0:
                    pe.wait_ge(evacuated, 2 * KH * APASS * l + 2 * KH * a + EVAC0)
                if k == 0:
                    pe.wait_ge(slab_in[s], 16 * APASS * l + 16 * (a + 1))
                for m in range(KH):
                    for i, part in enumerate((high, low)):
                        for n in range(2):
                            mm = nc.tensor.matmul(sum_ps[KH * n + m][:, 0:AN], part[:, t, m * P:(m + 1) * P],
                                                  slab[:, s, k, n * AN:(n + 1) * AN],
                                                  start=(t == 0 and i == 0), stop=(t == NT - 1 and i == 1))
                if k == SLAB - 1:
                    mm.then_inc(slab_used, 1)

            def project(l, p, b, terms):
                pe.wait_ge(moved, KH * NBLK * PROJ * l + KH * (NBLK * p + b - 1) + MOVED0)
                for m in range(KH):
                    for i, (src, weight) in enumerate(terms):
                        for k in range(KH):
                            mm = nc.tensor.matmul(proj_ps[KH * (b % 2) + m][:, 0:AN], weight[:, k, m * P:(m + 1) * P],
                                                  src[:, k, cols(b)], start=(i == 0 and k == 0),
                                                  stop=(i == len(terms) - 1 and k == KH - 1))
                mm.then_inc(summed, 1)

            with pe.Fori(0, LAYERS) as l:
                for t in range(NT + LAG):
                    if t < NT:
                        turn(l, t)
                    if t >= LAG:
                        pe.wait_ge(low_done, NT * l + t - LAG + 1)
                        sum_tile(l, 0, t - LAG)
                for a in range(1, APASS + 1):
                    if a < APASS:
                        for t in range(NT):
                            sum_tile(l, a, t)
                    if a == 1:
                        pe.wait_ge(params_in, 32 * l + 32)
                        if not gin:
                            pe.wait_ge(floored, NBLK * (l + 1) + 1)
                    for b in range(2 * (a - 1), 2 * a):
                        pe.wait_ge(evacuated, 2 * KH * APASS * l + KH * (b + 1) + EVAC0)
                        project(l, 0, b, [(z_t, w[:, 0])] if gin else [(z_t, w[:, 0]), (h_t, w[:, 1])])
                if gin:
                    for b in range(NBLK):
                        pe.wait_ge(normed, KH * NBLK * l + KH * (b + 1))
                        project(l, 1, b, [(z_t, w[:, 1])])

        @block.gpsimd
        def _(pool):
            nc.gpsimd.memset(floors[:, 0:1], -FAR).then_inc(ready, 1)
            nc.gpsimd.memset(floors[:, 1:LAYERS], 0.0).then_inc(ready, 1)
            pool.wait_ge(ready, 2)
            pool.sem_inc(floored, 1)
            with pool.Fori(0, LAYERS) as l:
                pool.wait_ge(floored, NBLK * l + 1)
                nc.gpsimd.tensor_copy(floor[:, 1:2], floors[:, bass.ds(l, 1)]).then_inc(pool_floor_set, 1)
                pool.wait_ge(pool_floor_set, l + 1)
                for b in range(NBLK):
                    pool.wait_ge(turned, NT * l + -(-(b + 1) * AN // P))
                    pool.sem_inc(pool_passed, 1)
                    nc.gpsimd.tensor_scalar(h_t[:, :, cols(b)], h_t[:, :, cols(b)], floor[:, 1:2], None, ALU.max).then_inc(floored, 1)

        @block.scalar
        def _(act):
            def move(l, p, b):
                act.wait_ge(summed, NBLK * PROJ * l + NBLK * p + b + 1)
                to = z_t if gin else h_t
                for m in range(KH):
                    nc.scalar.activation(to[:, m, cols(b)], proj_ps[KH * (b % 2) + m][:, 0:AN], ACT.Identity,
                                         bias=columns[:, 3 * p, m:m + 1], scale=1.0 / FS if gin and p == 0 else 1.0).then_inc(moved, 1)

            def root(l, p):
                act.wait_ge(step, 10 * l + 5 * p + 1)
                nc.scalar.activation(std[:, :], std[:, :], ACT.Sqrt).then_inc(rooted, 1)
                act.wait_ge(step, 10 * l + 5 * p + 5)

            def norm_relu(b):
                for m in range(KH):
                    nc.scalar.activation(z_t[:, m, cols(b)], z_t[:, m, cols(b)], ACT.Relu,
                                         bias=shift[:, m:m + 1], scale=gain[:, m:m + 1]).then_inc(normed, 1)

            with act.Fori(0, LAYERS) as l:
                for t in range(NT):
                    act.wait_ge(message_made, NT * l + t + 1)
                    nc.scalar.activation(high[:, t, :], message[:, t % RT, :], ACT.Copy).then_inc(high_done, 1)
                act.wait_ge(params_in, 32 * l + 32)
                for b in range(NBLK):
                    move(l, 0, b)
                if gin:
                    root(l, 0)
                    norm_relu(0)
                    norm_relu(1)
                    for b in range(NBLK):
                        move(l, 1, b)
                        if b + 2 < NBLK:
                            norm_relu(b + 2)
                    root(l, 1)
                    for b in range(NBLK):
                        nc.scalar.activation(h_t[:, 0, cols(b)], z_t[:, 0, cols(b)], ACT.Identity,
                                             bias=shift[:, 0:1], scale=gain[:, 0:1]).then_inc(h_done[0], 1)

        @block.vector
        def _(v):
            v.wait_ge(ready, 2)
            if gin:
                v.wait_ge(own_in, 16)
                nc.vector.tensor_scalar(own_all[:, :], own_all[:, :], 1.0, FS, ALU.add, ALU.mult).then_inc(own_set, 1)
                v.wait_ge(own_set, 1)

            def make_message(l, t):
                v.wait_ge(turned, NT * l + t + 1)
                if t >= RT:
                    v.wait_ge(low_done, NT * l + t - RT + 1)
                nc.vector.tensor_scalar(message[:, t % RT, :], proj_ps[t % (2 * KH)][:, 0:D], 0.0 if gin else floor[:, 0:1], FS,
                                        ALU.max, ALU.mult).then_inc(message_made, 1)

            def evacuate(l, a):
                v.wait_ge(slab_used, NSLAB * APASS * l + NSLAB * (a + 1) + USED0)
                for n in range(2):
                    for m in range(KH):
                        b = 2 * a + n
                        bank = sum_ps[KH * n + m][:, 0:AN]
                        if gin:
                            nc.vector.scalar_tensor_tensor(out=z_t[:, m, cols(b)], in0=h_t[:, m, cols(b)], scalar=own[:, 0:1],
                                                           in1=bank, op0=ALU.mult, op1=ALU.add).then_inc(evacuated, 1)
                        else:
                            nc.vector.tensor_tensor(z_t[:, m, cols(b)], bank, state["inv_degree"][:, cols(b)],
                                                    ALU.mult).then_inc(evacuated, 1)

            def block_stats(l, p, b):
                v.wait_ge(moved, KH * NBLK * PROJ * l + KH * (NBLK * p + b + 1) + MOVED0)
                for m in range(KH):
                    nc.vector.bn_stats(stats[:, m, b, :], z_t[:, m, b * AN:min((b + 1) * AN, N)]).then_inc(stat, 1)

            def gain_and_shift(l, p):
                base = 10 * l + 5 * p
                v.wait_ge(stat, 2 * KH * NBLK * l + KH * NBLK * (p + 1))
                v.sem_inc(v_passed, 1)
                for m in range(KH):
                    nc.vector.bn_aggr(mean_var[:, m, :], stats[:, m, :, :].rearrange("p b s -> p (b s)")).then_inc(aggr, 1)
                v.wait_ge(aggr, 2 * KH * l + KH * (p + 1))
                nc.vector.tensor_scalar(std[:, :], mean_var[:, :, 1], EPS, None, ALU.add).then_inc(step, 1)
                v.wait_ge(rooted, 2 * l + p + 1)
                nc.vector.reciprocal(std[:, :], std[:, :]).then_inc(step, 1)
                v.wait_ge(step, base + 2)
                nc.vector.tensor_tensor(gain[:, :], std[:, :], columns[:, 1 + 3 * p, :], ALU.mult).then_inc(step, 1)
                v.wait_ge(step, base + 3)
                nc.vector.tensor_tensor(shift[:, :], mean_var[:, :, 0], gain[:, :], ALU.mult).then_inc(step, 1)
                v.wait_ge(step, base + 4)
                nc.vector.tensor_tensor(shift[:, :], columns[:, 2 + 3 * p, :], shift[:, :], ALU.subtract).then_inc(step, 1)

            with v.Fori(0, LAYERS) as l:
                if gin:
                    nc.vector.tensor_copy(own[:, :], own_all[:, bass.ds(l, 1)]).then_inc(own_set, 1)
                else:
                    nc.vector.tensor_copy(floor[:, 0:1], floors[:, bass.ds(l, 1)]).then_inc(floor_set, 1)
                    v.wait_ge(floor_set, l + 1)
                make_message(l, 0)
                for t in range(NT):
                    if t + 1 < NT:
                        make_message(l, t + 1)
                    v.wait_ge(high_done, NT * l + t + 1)
                    nc.vector.tensor_tensor(low[:, t, :], message[:, t % RT, :], high[:, t, :], ALU.subtract).then_inc(low_done, 1)
                if gin:
                    v.wait_ge(own_set, l + 2)
                    v.wait_ge(floored, NBLK * (l + 1) + 1)
                evacuate(l, 0)
                if gin:
                    v.wait_ge(params_in, 32 * l + 32)
                for a in range(1, APASS):
                    evacuate(l, a)
                    if gin:
                        for b in range(2 * (a - 1), 2 * a):
                            block_stats(l, 0, b)
                if gin:
                    for b in range(NBLK - 2, NBLK):
                        block_stats(l, 0, b)
                    gain_and_shift(l, 0)
                    for b in range(NBLK):
                        block_stats(l, 1, b)
                    gain_and_shift(l, 1)
                    v.wait_ge(step, 10 * l + 10)
                    for b in range(NBLK):
                        nc.vector.tensor_scalar(h_t[:, 1, cols(b)], z_t[:, 1, cols(b)], gain[:, 1:2], shift[:, 1:2],
                                                ALU.mult, ALU.add).then_inc(h_done[1], 1)


PLAIN = ("L0_gnn_relation_emb", "L0_gnn_bq", "L0_gnn_bk", "L0_gnn_bv", "L0_gnn_bo", "L1_gnn_W_attn", "L1_gnn_a",
         "L2_gnn_eps")
TURNED = ("L1_gnn_W_lin",)




def gnn_kernel(nc, ins, out):
    with ExitStack() as ctx:
        def sb(name, shape, dt):
            return ctx.enter_context(nc.sbuf_tensor(name, shape, dt))
        scratch = {
            "adj": nc.dram_tensor("adj", [NP * AW, 1], F16, kind="Internal").ap(),
            "vk": nc.dram_tensor("vk", [NP, 2 * D], F32, kind="Internal").ap(),
            "q": nc.dram_tensor("q", [NP, D], F32, kind="Internal").ap(),
            "val": nc.dram_tensor("val", [NP, D + H], F32, kind="Internal").ap(),
            "alpha": nc.dram_tensor("alpha", [NP, H], F32, kind="Internal").ap(),
            "q_part": nc.dram_tensor("q_part", [PBUF, D], F32, kind="Internal").ap(),
            "alpha_part": nc.dram_tensor("alpha_part", [PBUF, H], F32, kind="Internal").ap(),
            "x1": nc.dram_tensor("x1", [NP, D], F32, kind="Internal").ap(),
            "out0": nc.dram_tensor("out0", [NP, D], F32, kind="Internal").ap(),
            "inv_degree": nc.dram_tensor("inv_degree", [NP, 1], F32, kind="Internal").ap(),
            "out1": nc.dram_tensor("out1", [NP, D + 1], F32, kind="Internal").ap(),
        }
        keep = {
            "ident": sb("ident", [P, P], F32),
            "ones": sb("ones", [P, P], F32),
        }
        with ExitStack() as edge_ctx:
            def esb(name, shape, dt):
                return edge_ctx.enter_context(nc.sbuf_tensor(name, shape, dt))
            keep.update({
                "hsel": esb("hsel", [H, D], F32), "iota": esb("iota", [P, P], F32),
                "src": esb("src", [P, C], I32), "cell": esb("cell", [P, C], I32), "cell_once": esb("cell_once", [P, C], I32),
                "repeats": esb("repeats", [P, 1], I32), "count_one": esb("count_one", [P, 1], F16),
                "first": esb("first", [P, C], F32), "slot": esb("slot", [P, C], F32), "node": esb("node", [P, C], F32),
                "part_node": esb("part_node", [P, PT + 1], I32), "offset": esb("offset", [1, C], I32), "link": esb("link", [G * H, NG, LINK], BF16),
                "link_back": esb("link_back", [G * H, NG, P], BF16),
            })
            prepare(nc, ins, keep, scratch)
            with ExitStack() as part_ctx:
                keep["sums"] = part_ctx.enter_context(nc.sbuf_tensor("sums0", [P, KH + 1, PBUF], F32))
                attend_edges(nc, keep, scratch, 0, scratch["vk"], scratch["q"], scratch["q_part"], 2 * D, D, float(DK) ** -0.5, (0, G // 2))
                merge_parts(nc, ins, keep, 0, "wo_t", scratch["out0"], float(DK) ** -0.5)
            with ExitStack() as x_ctx:
                keep["x"] = x_ctx.enter_context(nc.sbuf_tensor("x_1", [P, NT, D], F32))
                x_t = x_ctx.enter_context(nc.sbuf_tensor("x_t_1", [P, KH, NP], F32))
                residual_norm(nc, ins, keep, scratch, 0, add=scratch["out0"], bias="L0_gnn_bo", x_from=ins["x"],
                              turned_to=x_t, rows_to=scratch["x1"])
                tables_layer1(nc, ins, scratch, x_t)
            with ExitStack() as part_ctx:
                keep["sums"] = part_ctx.enter_context(nc.sbuf_tensor("sums1", [P, KH + 1, PBUF], F32))
                attend_edges(nc, keep, scratch, 1, scratch["val"], scratch["alpha"], scratch["alpha_part"], D + H, H, 1.0, (C // 2, G // 2))
                add_repeated(nc, keep, scratch)
                merge_parts(nc, ins, keep, 1, None, scratch["out1"], 1.0)
        keep["x"] = sb("x", [P, NT, D], F32)
        h_t = sb("h_t", [P, KH, NP], F32)
        residual_norm(nc, ins, keep, scratch, 1, add=scratch["out1"], x_from=scratch["x1"], turned_to=h_t)
        state = {
            "h_t": h_t, "z_t": sb("z_t", [P, KH, AW], F32),
            "high": sb("high", [P, NT, D], F16), "low": sb("low", [P, NT, D], F16),
            "slab": sb("slab", [P, NSLAB, SLAB, ACOLS], F16),
        }
        graph_layers(nc, ins, keep, scratch, state, "gin")
        residual_norm(nc, ins, keep, scratch, 2, added_t=h_t, turned_to=h_t)
        state["inv_degree"] = sb("inv_degree_all", [P, AW], F32)
        load_degrees(nc, state, scratch)
        graph_layers(nc, ins, keep, scratch, state, "sage")
        residual_norm(nc, ins, keep, scratch, 3, added_t=h_t, rows_to=out)


def kernel(**inputs):
    import numpy as _np
    import concourse.bacc as _bacc
    from concourse import mybir as _mybir
    from concourse.bass_utils import run_bass_kernel_spmd as _run

    def padded_t(a):
        return _np.pad(_np.asarray(a).T, ((0, 0), (0, NP - N)))

    x = _np.asarray(inputs["x"])
    text = _np.concatenate([_np.asarray(inputs["L0_gnn_user_text_embs"]), _np.asarray(inputs["L0_gnn_item_text_embs"])])
    src = _np.pad(_np.asarray(inputs["src"]), (0, C * P - E))
    dst = _np.pad(_np.asarray(inputs["dst"]), (0, C * P - E), constant_values=N)
    chunks = dst.reshape(C, P)
    arrays = {
        "x": _np.pad(x, ((0, NP - N), (0, 0))), "x_t": padded_t(x), "text_t": padded_t(text),
        "src_col": src.reshape(C, P).T, "dst_col": chunks.T,
        "dst_prev": _np.pad(chunks[:, :-1], ((0, 0), (1, 0)), constant_values=-1).T,
        "src_row": src.reshape(P, C), "dst_row": dst.reshape(P, C),
        "dst_row_next": _np.pad(dst.reshape(P, C)[1:], ((0, 1), (0, 0)), constant_values=-1), "dst_chunk": chunks,
        "wq_t": _np.asarray(inputs["L0_gnn_Wq"]).T, "wk_t": _np.asarray(inputs["L0_gnn_Wk"]).T,
        "wv_t": _np.asarray(inputs["L0_gnn_Wv"]).T, "wo_t": _np.asarray(inputs["L0_gnn_Wo"]).T,
    }
    arrays["gin_w"] = _np.stack([_np.asarray(inputs["L2_gnn_W1"]), _np.asarray(inputs["L2_gnn_W2"])], axis=1)
    arrays["sage_w"] = _np.stack([_np.stack([_np.asarray(inputs[f"L3_gnn_W{l + 1}{side}"]).T for side in "lr"])
                                  for l in range(SAGE_LAYERS)])
    gin = _np.stack([_np.asarray(inputs[r]) for r in GIN_COLUMNS])
    arrays["gin_columns"] = gin.reshape(len(GIN_COLUMNS), GIN_LAYERS, KH, P).transpose(1, 3, 0, 2)
    sage = _np.stack([_np.asarray(inputs[r]) for r in SAGE_COLUMNS])
    arrays["sage_columns"] = sage.reshape(SAGE_LAYERS, 1, KH, P).transpose(0, 3, 1, 2)
    for name in PLAIN:
        arrays[name] = _np.asarray(inputs[name])
    for name in TURNED:
        arrays[name + "_t"] = _np.asarray(inputs[name]).T
    arrays = {"in_" + k: _np.ascontiguousarray(a) for k, a in arrays.items()}
    nc = _bacc.Bacc("TRN2", target_bir_lowering=False, num_devices=1)
    ins = {k[3:]: nc.dram_tensor(k, a.shape, _mybir.dt.from_np(a.dtype), kind="ExternalInput").ap() for k, a in arrays.items()}
    out = nc.dram_tensor("out_x", (N, D), _mybir.dt.float32, kind="ExternalOutput").ap()
    gnn_kernel(nc, ins, out)
    r = _run(nc, [arrays], core_ids=[0])
    return r.results[0]["out_x"]
```
